# Optimizing a Trainium2 kernel written in Bass

```python
import numpy as np
import jax
import jax.numpy as jnp

def _softmax(x, axis=-1):
    return jax.nn.softmax(x, axis=axis)

def _gelu(x):
    return jax.nn.gelu(x, approximate=True)

def _silu(x):
    return jax.nn.silu(x)

def _sigmoid(x):
    return jax.nn.sigmoid(x)

def _layernorm(x, axis=-1, eps=1e-05):
    m = jnp.mean(x, axis=axis, keepdims=True)
    v = jnp.var(x, axis=axis, keepdims=True)
    return (x - m) / jnp.sqrt(v + eps)

def _scatter_add(tgt, idx, src, axis=0):
    return tgt.at[idx].add(src)

def _segment_sum(src, seg, n):
    return jax.ops.segment_sum(src, seg, n)
kernel_name = 'mk_sandwich_d1_jaxref_r8_cba5d4'

def setup_inputs(seed: int=0):
    np.random.seed(seed)
    _w = jnp.asarray

    def _L0_attn_setup():
        import jax, jax.numpy as jnp
        import numpy as np
        from math import sqrt
        N_HEAD = 16

        def _reference_tuple_inner(x, Wq_w, Wdkv_w, Wuk_w, Wuv_w, Wo_w):
            B, T, C = x.shape
            nh = N_HEAD
            hs = C // nh
            nl = Wdkv_w.shape[0]
            k_eff = (Wq_w.T @ Wuk_w).reshape(nh, hs, nl)
            v_eff = jnp.transpose((Wuv_w.T @ Wo_w.T).reshape(nl, nh, hs), (1, 0, 2))
            c_kv = x @ Wdkv_w.T
            q = (x @ Wq_w.T).reshape(B, T, nh, hs).transpose(0, 2, 1, 3)
            q_lat = jnp.einsum('bhts,hsl->bhtl', q, k_eff)
            attn = jnp.einsum('bhtl,bkl->bhtk', q_lat, c_kv) / sqrt(hs)
            causal = jnp.tril(jnp.ones((T, T), dtype=bool))
            attn = jnp.where(causal[None, None], attn, -jnp.inf)
            attn = jax.nn.softmax(attn, axis=-1)
            y_lat = jnp.einsum('bhtk,bkl->bhtl', attn, c_kv)
            y = jnp.einsum('bhtl,hld->bhtd', y_lat, v_eff)
            y = y.transpose(0, 2, 1, 3).reshape(B, T, C)
            return (y, c_kv)
        key = jax.random.key(seed)
        ks = jax.random.split(key, 6)
        B, T, C, NL = (2, 256, 256, 64)
        s = 0.02
        return {'x': jax.random.normal(ks[0], (B, T, C), jnp.float32), 'Wq_w': jax.random.normal(ks[1], (C, C), jnp.float32) * s, 'Wdkv_w': jax.random.normal(ks[2], (NL, C), jnp.float32) * s, 'Wuk_w': jax.random.normal(ks[3], (C, NL), jnp.float32) * s, 'Wuv_w': jax.random.normal(ks[4], (C, NL), jnp.float32) * s, 'Wo_w': jax.random.normal(ks[5], (C, C), jnp.float32) * s}
    _L0_attn_in = _L0_attn_setup()

    def _L0_ffn_setup():
        import jax, jax.numpy as jnp
        import numpy as np
        B, S, D, I, E, K = (4, 128, 256, 128, 8, 2)
        key = jax.random.key(seed)
        ks = jax.random.split(key, 7)

        def w(k, shape, fan_in):
            return jax.random.normal(k, shape, dtype=jnp.float32) * fan_in ** (-0.5)
        return {'hidden_states': jax.random.normal(ks[0], (B, S, D), dtype=jnp.float32), 'router_w': w(ks[1], (D, E), D), 'gate_up_w': w(ks[2], (E, D, 2 * I), D), 'down_w': w(ks[3], (E, I, D), I), 'shared_gate_w': w(ks[4], (D, I), D), 'shared_up_w': w(ks[5], (D, I), D), 'shared_down_w': w(ks[6], (I, D), I)}
    _L0_ffn_in = _L0_ffn_setup()
    _d = {'L0_attn_x': _L0_attn_in['x'], 'L0_attn_Wq_w': _L0_attn_in['Wq_w'], 'L0_attn_Wdkv_w': _L0_attn_in['Wdkv_w'], 'L0_attn_Wuk_w': _L0_attn_in['Wuk_w'], 'L0_attn_Wuv_w': _L0_attn_in['Wuv_w'], 'L0_attn_Wo_w': _L0_attn_in['Wo_w'], 'L0_ffn_router_w': _L0_ffn_in['router_w'], 'L0_ffn_gate_up_w': _L0_ffn_in['gate_up_w'], 'L0_ffn_down_w': _L0_ffn_in['down_w'], 'L0_ffn_shared_gate_w': _L0_ffn_in['shared_gate_w'], 'L0_ffn_shared_up_w': _L0_ffn_in['shared_up_w'], 'L0_ffn_shared_down_w': _L0_ffn_in['shared_down_w']}
    _x0 = _d['L0_attn_x']
    _d['L0_attn_x'] = jax.random.normal(jax.random.fold_in(jax.random.key(seed), 1), (16, 256, 256), dtype=_x0.dtype)
    del _x0
    return _d

def reference(L0_attn_x, L0_attn_Wq_w, L0_attn_Wdkv_w, L0_attn_Wuk_w, L0_attn_Wuv_w, L0_attn_Wo_w, L0_ffn_router_w, L0_ffn_gate_up_w, L0_ffn_down_w, L0_ffn_shared_gate_w, L0_ffn_shared_up_w, L0_ffn_shared_down_w):

    def _L0_attn_ref(x, Wq_w, Wdkv_w, Wuk_w, Wuv_w, Wo_w):
        import jax, jax.numpy as jnp
        import numpy as np
        from math import sqrt
        N_HEAD = 16

        def _reference_tuple_inner(x, Wq_w, Wdkv_w, Wuk_w, Wuv_w, Wo_w):
            B, T, C = x.shape
            nh = N_HEAD
            hs = C // nh
            nl = Wdkv_w.shape[0]
            k_eff = (Wq_w.T @ Wuk_w).reshape(nh, hs, nl)
            v_eff = jnp.transpose((Wuv_w.T @ Wo_w.T).reshape(nl, nh, hs), (1, 0, 2))
            c_kv = x @ Wdkv_w.T
            q = (x @ Wq_w.T).reshape(B, T, nh, hs).transpose(0, 2, 1, 3)
            q_lat = jnp.einsum('bhts,hsl->bhtl', q, k_eff)
            attn = jnp.einsum('bhtl,bkl->bhtk', q_lat, c_kv) / sqrt(hs)
            causal = jnp.tril(jnp.ones((T, T), dtype=bool))
            attn = jnp.where(causal[None, None], attn, -jnp.inf)
            attn = jax.nn.softmax(attn, axis=-1)
            y_lat = jnp.einsum('bhtk,bkl->bhtl', attn, c_kv)
            y = jnp.einsum('bhtl,hld->bhtd', y_lat, v_eff)
            y = y.transpose(0, 2, 1, 3).reshape(B, T, C)
            return (y, c_kv)
        return _reference_tuple_inner(x, Wq_w, Wdkv_w, Wuk_w, Wuv_w, Wo_w)[0]

    def _L0_ffn_ref(hidden_states, router_w, gate_up_w, down_w, shared_gate_w, shared_up_w, shared_down_w):
        import jax, jax.numpy as jnp
        import numpy as np
        B, S, D, I, E, K = (4, 128, 256, 128, 8, 2)
        Bb, Ss, Dd = hidden_states.shape
        x = hidden_states.reshape(-1, Dd)
        T = x.shape[0]
        shared = jax.nn.silu(x @ shared_gate_w) * (x @ shared_up_w) @ shared_down_w
        logits = x @ router_w
        top_val, top_idx = jax.lax.top_k(logits, K)
        probs = jnp.zeros_like(logits).at[jnp.arange(T)[:, None], top_idx].set(jax.nn.sigmoid(top_val))
        xin = probs.T[:, :, None] * x[None]
        gu = jnp.einsum('etd,edf->etf', xin, gate_up_w)
        gate, up = jnp.split(gu, 2, axis=-1)
        h = jax.nn.silu(gate) * up
        expert_out = jnp.einsum('eti,eid->etd', h, down_w)
        combined = shared + expert_out.sum(axis=0)
        return combined.reshape(Bb, Ss, Dd)
    x = L0_attn_x
    x = x + _layernorm(_L0_attn_ref(_layernorm(x, axis=-1), L0_attn_Wq_w, L0_attn_Wdkv_w, L0_attn_Wuk_w, L0_attn_Wuv_w, L0_attn_Wo_w), axis=-1)
    x = x + _layernorm(_L0_ffn_ref(_layernorm(x, axis=-1), L0_ffn_router_w, L0_ffn_gate_up_w, L0_ffn_down_w, L0_ffn_shared_gate_w, L0_ffn_shared_up_w, L0_ffn_shared_down_w), axis=-1)
    return x

_drawn_inputs = setup_inputs


def setup_inputs(seed=0):
    import zlib

    import numpy as np

    out = dict(_drawn_inputs(seed))
    spreads = {}
    factors = {'L0_attn_Wq_w': 2.977, 'L0_attn_Wuk_w': 2.742}
    for name, (base, spread) in spreads.items():
        noise = np.random.default_rng([zlib.crc32(name.encode()), seed]).standard_normal(out[name].shape)
        drawn = base * np.exp(spread * noise) if base else spread * noise
        out[name] = jnp.asarray(drawn.astype(out[name].dtype))
    for name, factor in factors.items():
        out[name] = (out[name] * factor).astype(out[name].dtype)
    return out
```

```python
import concourse.bass as bass
from concourse import mybir
from contextlib import ExitStack


def sandwich_block_kernel(
    nc: bass.Bass,
    x: bass.AP,
    w_q: bass.AP,
    w_dkv: bass.AP,
    w_uk: bass.AP,
    w_uv: bass.AP,
    w_o: bass.AP,
    router_w: bass.AP,
    gate_up_w: bass.AP,
    down_w: bass.AP,
    shared_gate_w: bass.AP,
    shared_up_w: bass.AP,
    shared_down_w: bass.AP,
    out: bass.AP,
):
    fp32 = mybir.dt.float32
    f32r = mybir.dt.float32r
    bf16 = mybir.dt.bfloat16
    ALU = mybir.AluOpType
    ACT = mybir.ActivationFunctionType
    AX = mybir.AxisListType

    P = 128
    BATCH, T, C = x.shape
    NL = w_dkv.shape[0]
    HEADS = 16
    HS = C // HEADS
    TT = T // P
    CT = C // P
    HM = HEADS // CT
    EXPERTS, _, GU = gate_up_w.shape
    I = GU // 2
    TILES = BATCH * TT
    EPS = 1e-5
    MASK = -1e30
    SCALE = float(HS) ** -0.5
    SHARED = EXPERTS
    NE = EXPERTS + 1

    Q_PARTS = [0, 0, 1, 1, 0, 2]
    K_PARTS = [0, 1, 0, 1, 2, 0]
    SROWS = HS * len(Q_PARTS)
    MROWS = 3
    UNIT = 2 * T + 2 * P
    UNITS = HEADS // 2
    GROUPS = HEADS // 4
    FILLS = 3 * GROUPS

    x_tok = x.rearrange("b (t p) c -> b p t c", p=P)
    x1_dram = nc.dram_tensor("x1_scratch", (BATCH, T, C), fp32, kind="Internal").ap()
    xn2_dram = nc.dram_tensor("xn2_scratch", (BATCH, T, C), fp32, kind="Internal").ap()
    x1_tok = x1_dram.rearrange("b (t p) c -> b p t c", p=P)
    xn2_tok = xn2_dram.rearrange("b (t p) c -> b p t c", p=P)
    x1_tile = x1_dram.rearrange("b (t p) c -> (b t) p c", p=P)
    xn2_tile = xn2_dram.rearrange("b (t p) c -> (b t) p c", p=P)
    out_tile = out.rearrange("b (t p) c -> (b t) p c", p=P)

    ctx = ExitStack()
    with ctx:
        def sb(name, shape, dt=fp32):
            return ctx.enter_context(nc.sbuf_tensor(name, shape, dt))

        def ps(name, shape):
            return ctx.enter_context(nc.psum_tensor(name, shape, fp32))

        def sem(name):
            return ctx.enter_context(nc.semaphore(name))

        ident = sb("ident", [P, P])
        identb = sb("identb", [P, P], bf16)
        maskq = sb("maskq", [P, P], bf16)
        maskk = sb("maskk", [P, P], bf16)
        neg_half = sb("neg_half", [P, TT])
        wq_hi, wq_lo, wk_hi, wk_lo, wv_hi, wv_lo = (
            sb(n, [P, CT, C], f32r) for n in ("wq_hi", "wq_lo", "wk_hi", "wk_lo", "wv_hi", "wv_lo"))
        r_hi = sb("r_hi", [P, CT, EXPERTS], f32r)
        r_lo = sb("r_lo", [P, CT, EXPERTS], f32r)
        gu_hi = sb("gu_hi", [P, NE, CT, GU], f32r)
        gu_lo = sb("gu_lo", [P, NE, CT, GU], f32r)
        dn_hi = sb("dn_hi", [P, NE, C], f32r)
        dn_lo = sb("dn_lo", [P, NE, C], f32r)
        logits = sb("logits", [P, TILES, EXPERTS])
        top8 = sb("top8", [P, TILES, 8])
        probs = sb("probs", [P, TILES, EXPERTS])

        ctx1 = ExitStack()

        def sb1(name, shape, dt=fp32):
            return ctx1.enter_context(nc.sbuf_tensor(name, shape, dt))

        xa = sb1("xa", [P, 3, TT, C])
        xr = sb1("xr", [P, TT, C])
        xn = sb1("xn", [P, TT, C])
        st1 = sb1("st1", [P, TT, 6])
        mv1 = sb1("mv1", [P, TT, 2])
        rs1 = sb1("rs1", [P, TT])
        xt_hi = sb1("xt_hi", [P, CT, T], f32r)
        xt_lo = sb1("xt_lo", [P, CT, T], f32r)
        q_part = sb1("q_part", [P, 3, CT, T], bf16)
        k_part = sb1("k_part", [P, 3, CT, T], bf16)
        q_rest = sb1("q_rest", [P, CT, T])
        k_rest = sb1("k_rest", [P, CT, T])
        q_stack = sb1("q_stack", [P, 3, HEADS, T], bf16)
        k_stack = sb1("k_stack", [P, 3, HEADS, T], bf16)
        v_sb = sb1("v_sb", [P, 3, TT, HEADS, 32])
        rowmax = sb1("rowmax", [P, TT, HEADS])
        m_part = sb1("m_part", [HEADS, 3, T], bf16)
        m_rest = sb1("m_rest", [HEADS, 2, T])
        prob_t = sb1("prob_t", [P, 4, UNIT])
        yt_sb = sb1("yt_sb", [P, 3, GROUPS, T])
        inv = sb1("inv", [P, TT, HEADS])
        y_sb = sb1("y_sb", [P, TT, C])
        sty = sb1("sty", [P, TT, 6])
        mvy = sb1("mvy", [P, TT, 2])
        rsy = sb1("rsy", [P, TT])
        x1_sb = sb1("x1_sb", [P, TT, C])
        st2 = sb1("st2", [P, TT, 6])
        mv2 = sb1("mv2", [P, TT, 2])
        rs2 = sb1("rs2", [P, TT])
        xn2_sb = sb1("xn2_sb", [P, TT, C])

        consts_ready = sem("consts_ready")
        w_loaded = sem("w_loaded")
        prep_pe = sem("prep_pe")
        prep_copied = sem("prep_copied")
        gu_loaded = [sem(f"gu_loaded{n}") for n in range(3)]
        gu_split = sem("gu_split")
        prep_chain = sem("prep_chain")
        x_loaded = [sem(f"x_loaded{n}") for n in range(3)]
        xr_loaded = sem("xr_loaded")
        bn1_done = sem("bn1_done")
        stats1 = sem("stats1")
        veps1 = sem("veps1")
        rstd1 = sem("rstd1")
        xn_ready = sem("xn_ready")
        xt_done = sem("xt_done")
        xt_hi_ready = sem("xt_hi_ready")
        xt_lo_ready = sem("xt_lo_ready")
        qk_done = sem("qk_done")
        qk_p0 = sem("qk_p0")
        qk_rest = sem("qk_rest")
        qk_p1 = sem("qk_p1")
        qk_p2 = sem("qk_p2")
        v_done = sem("v_done")
        v_ready = sem("v_ready")
        q_stacked = sem("q_stacked")
        k_stacked = sem("k_stacked")
        m_stacked = sem("m_stacked")
        s_done = sem("s_done")
        s_max = sem("s_max")
        mt_done = sem("mt_done")
        m_chain = sem("m_chain")
        m_ready = sem("m_ready")
        st_done = sem("st_done")
        p_ready = sem("p_ready")
        pv_done = sem("pv_done")
        yt_ready = sem("yt_ready")
        ytr_done = sem("ytr_done")
        inv_ready = sem("inv_ready")
        y_ready = sem("y_ready")
        bny_done = sem("bny_done")
        statsy = sem("statsy")
        vepsy = sem("vepsy")
        rstdy = sem("rstdy")
        lny = sem("lny")
        x1_ready = sem("x1_ready")
        bn2_done = sem("bn2_done")
        stats2 = sem("stats2")
        veps2 = sem("veps2")
        rstd2 = sem("rstd2")
        x1_stored = sem("x1_stored")
        xn2_stored = sem("xn2_stored")
        xn2_ready = sem("xn2_ready")

        QD = 16 * len(Q_PARTS) * CT
        MD = 16 * MROWS

        with ExitStack() as c0:
            def sb0(name, shape, dt=fp32):
                return c0.enter_context(nc.sbuf_tensor(name, shape, dt))

            wq_raw = sb0("wq_raw", [P, CT, C])
            wo_raw = sb0("wo_raw", [P, CT, C])
            wuk_raw = sb0("wuk_raw", [P, CT, NL])
            wuv_raw = sb0("wuv_raw", [P, CT, NL])
            wdkv_raw = sb0("wdkv_raw", [NL, C])
            wo_t = sb0("wo_t", [P, CT, C])
            keff_t = sb0("keff_t", [NL, C])
            veff = sb0("veff", [NL, C])
            full = sb0("full", [P, 3, CT, C])
            r_raw = sb0("r_raw", [P, CT, EXPERTS])
            gu_raw = prob_t[:, :, :].rearrange("p a b -> p (a b)")[:, 0:3 * CT * GU].rearrange(
                "p (e c n) -> p e c n", e=3, c=CT)
            dn_raw = yt_sb[:, :, :, :].rearrange("p a b c -> p (a b c)")[:, 0:NE * C].rearrange(
                "p (e c) -> p e c", e=NE)
            pt = [c0.enter_context(nc.psum_tensor(f"pt{n}", [P, 512], fp32)) for n in range(6)]
            block = c0.enter_context(nc.Block())

            @block.sync
            def _(sp):
                for dst, src in ((wq_raw, w_q), (wo_raw, w_o), (wuk_raw, w_uk), (wuv_raw, w_uv),
                                 (r_raw, router_w)):
                    sp.dma_start(dst[:], src.rearrange("(t p) n -> p t n", p=P)).then_inc(w_loaded, 16)
                sp.dma_start(wdkv_raw[:], w_dkv).then_inc(w_loaded, 16)
                sp.dma_start(dn_raw[:, 0:EXPERTS, :], down_w.rearrange("e i c -> i e c")).then_inc(w_loaded, 16)
                sp.dma_start(dn_raw[:, SHARED, :], shared_down_w).then_inc(w_loaded, 16)
                for e in range(NE):
                    if e >= 3:
                        sp.wait_ge(gu_split, e - 2)
                    if e < EXPERTS:
                        sp.dma_start(gu_raw[:, e % 3], gate_up_w[e].rearrange("(t p) n -> p t n", p=P)).then_inc(gu_loaded[e % 3], 32)
                    else:
                        sp.dma_start(gu_raw[:, e % 3, :, 0:I], shared_gate_w.rearrange("(t p) n -> p t n", p=P)).then_inc(gu_loaded[e % 3], 16)
                        sp.dma_start(gu_raw[:, e % 3, :, I:GU], shared_up_w.rearrange("(t p) n -> p t n", p=P)).then_inc(gu_loaded[e % 3], 16)

            @block.gpsimd
            def _(pool):
                nc.gpsimd.memset(ident[:], 0.0).then_inc(consts_ready, 1)
                nc.gpsimd.memset(maskq[:], 0.0).then_inc(consts_ready, 1)
                nc.gpsimd.memset(maskk[:], 0.0).then_inc(consts_ready, 1)
                nc.gpsimd.memset(neg_half[:], -0.5).then_inc(consts_ready, 1)
                nc.gpsimd.memset(v_sb[:], 0.0).then_inc(consts_ready, 1)
                pool.wait_ge(consts_ready, 6)
                nc.gpsimd.memset(v_sb[:, :, :, :, HS:HS + 1], 1.0).then_inc(consts_ready, 1)
                nc.gpsimd.affine_select(out=ident[:], in_=ident[:], compare_op=ALU.not_equal, fill=1.0, base=0,
                                        pattern=[[-1, P]], channel_multiplier=1).then_inc(consts_ready, 1)
                nc.gpsimd.affine_select(out=maskq[:], in_=maskq[:], compare_op=ALU.is_ge, fill=MASK, base=0,
                                        pattern=[[-1, P]], channel_multiplier=1).then_inc(consts_ready, 1)
                nc.gpsimd.affine_select(out=maskk[:], in_=maskk[:], compare_op=ALU.is_ge, fill=MASK, base=0,
                                        pattern=[[1, P]], channel_multiplier=-1).then_inc(consts_ready, 1)
                pool.wait_ge(consts_ready, 10)
                nc.gpsimd.tensor_copy(identb[:], ident[:]).then_inc(consts_ready, 1)
                pool.wait_ge(w_loaded, 16 * 8)
                nc.gpsimd.tensor_scalar(dn_raw[:], dn_raw[:], 0.5, None, ALU.mult).then_inc(consts_ready, 1)

            @block.tensor
            def _(pe):
                pe.wait_ge(consts_ready, 12)
                for n, raw in enumerate((wq_raw, wo_raw)):
                    for ct in range(CT):
                        for rt in range(CT):
                            last = nc.tensor.transpose(pt[n][:, ct * C + rt * P:ct * C + (rt + 1) * P],
                                                       raw[:, rt, ct * P:(ct + 1) * P], ident[:])
                last.then_inc(prep_pe, 1)
                for ct in range(CT):
                    last = nc.tensor.matmul(pt[2][0:NL, 0:C], wuk_raw[:, ct, :], wq_raw[:, ct, :],
                                            start=(ct == 0), stop=(ct == CT - 1))
                last.then_inc(prep_pe, 1)
                pe.wait_ge(prep_copied, 1)
                for ct in range(CT):
                    last = nc.tensor.matmul(pt[3][0:NL, 0:C], wuv_raw[:, ct, :], wo_t[:, ct, :],
                                            start=(ct == 0), stop=(ct == CT - 1))
                last.then_inc(prep_pe, 1)
                pe.wait_ge(prep_copied, 3)
                for n, eff in ((4, keff_t), (5, veff)):
                    for ct in range(CT):
                        last = nc.tensor.matmul(pt[n][:, ct * C:(ct + 1) * C], wdkv_raw[:, ct * P:(ct + 1) * P],
                                                eff[:], start=True, stop=True)
                last.then_inc(prep_pe, 1)

            @block.scalar
            def _(act):
                act.wait_ge(prep_pe, 1)
                nc.scalar.copy(wo_t[:], pt[1][:].rearrange("p (t n) -> p t n", t=CT)).then_inc(prep_copied, 1)
                act.wait_ge(prep_pe, 2)
                nc.scalar.copy(keff_t[:], pt[2][0:NL, 0:C]).then_inc(prep_copied, 1)
                act.wait_ge(prep_pe, 3)
                nc.scalar.copy(veff[:], pt[3][0:NL, 0:C]).then_inc(prep_copied, 1)
                for e in range(NE):
                    act.wait_ge(gu_loaded[e % 3], 32 * (e // 3 + 1))
                    nc.scalar.copy(gu_hi[:, e], gu_raw[:, e % 3]).then_inc(prep_copied, 1)

            @block.vector
            def _(dve):
                steps = [0]

                def step(ins):
                    steps[0] += 1
                    ins.then_inc(prep_chain, 1)
                    dve.wait_ge(prep_chain, steps[0])

                nc.vector.memset(k_stack[SROWS:P], -1.0).then_inc(consts_ready, 1)
                dve.wait_ge(prep_pe, 1)
                for ct in range(CT):
                    step(nc.vector.tensor_copy(
                        full[:, 0, ct, :].rearrange("p (m d h) -> p m h d", m=CT, h=HM),
                        pt[0][:, ct * C:(ct + 1) * C].rearrange("p (m h d) -> p m h d", m=CT, h=HM)))
                dve.wait_ge(prep_pe, 4)
                for ct in range(CT):
                    step(nc.vector.tensor_copy(
                        full[:, 1, ct, :].rearrange("p (m d h) -> p m h d", m=CT, h=HM),
                        pt[4][:, ct * C:(ct + 1) * C].rearrange("p (m h d) -> p m h d", m=CT, h=HM)))
                step(nc.vector.tensor_copy(full[:, 2], pt[5][:].rearrange("p (t n) -> p t n", t=CT)))
                for n, (hi, lo) in enumerate(((wq_hi, wq_lo), (wk_hi, wk_lo), (wv_hi, wv_lo))):
                    step(nc.vector.tensor_copy(hi[:], full[:, n]))
                    step(nc.vector.tensor_tensor(lo[:], full[:, n], hi[:].bitcast(fp32), ALU.subtract))
                dve.wait_ge(consts_ready, 12)
                step(nc.vector.tensor_copy(r_hi[:], r_raw[:]))
                step(nc.vector.tensor_tensor(r_lo[:], r_raw[:], r_hi[:].bitcast(fp32), ALU.subtract))
                step(nc.vector.tensor_copy(dn_hi[:], dn_raw[:]))
                step(nc.vector.tensor_tensor(dn_lo[:], dn_raw[:], dn_hi[:].bitcast(fp32), ALU.subtract))
                for e in range(NE):
                    dve.wait_ge(prep_copied, 3 + e + 1)
                    nc.vector.tensor_tensor(gu_lo[:, e], gu_raw[:, e % 3], gu_hi[:, e].bitcast(fp32),
                                            ALU.subtract).then_inc(gu_split, 1)
                dve.wait_ge(gu_split, NE)
                dve.wait_ge(consts_ready, 12)

        st_ps = [ctx1.enter_context(nc.psum_tensor(f"st_ps{n}", [P, 1024], fp32)) for n in range(2)]
        s_ps = [ctx1.enter_context(nc.psum_tensor(f"s_ps{n}", [P, 512], fp32)) for n in range(2)]
        pv_ps = ctx1.enter_context(nc.psum_tensor("pv_ps", [P, 512], fp32))
        w_ps = ctx1.enter_context(nc.psum_tensor("w_ps", [P, 512], fp32))
        w_half = w_ps[:, :].rearrange("p (t n) -> p t n", t=2)

        FIRST, LAST = 1, BATCH - 4
        BODY = 3

        turns = [0]

        def turn_of(b, k):
            return turns[0]

        def steps_of(eng, step):
            for b in range(-3, FIRST):
                step(b, b)
            with eng.Fori(0, (LAST - FIRST + 1) // BODY) as turn:
                turns[0] = turn
                for n in range(BODY):
                    step(turn * BODY + (FIRST + n), FIRST + n)
            for b in range(LAST + 1, BATCH + 1):
                step(b, b)

        def has(b, lag):
            return 0 <= b + lag < BATCH

        def wait(eng, semaphore, value):
            if not isinstance(value, int) or value > 0:
                eng.wait_ge(semaphore, value)

        passed = sem("passed")

        def wait_apart(eng, semaphore, value):
            wait(eng, semaphore, value)
            if not isinstance(value, int):
                eng.sem_inc(passed, 1)

        with ctx1, ExitStack() as c2:
            block = c2.enter_context(nc.Block())

            @block.sync
            def _(sp):
                def step(b, k):
                    loop = not isinstance(b, int)

                    def on(lag):
                        return loop or has(b, lag)

                    if on(3):
                        wait_apart(sp, xn_ready, b + 1)
                        sp.dma_start(xa[:, k % 3], x_tok[b + 3]).then_inc(x_loaded[k % 3], 16)
                    if on(-1):
                        wait_apart(sp, x1_ready, b)
                        sp.dma_start(xr[:], x_tok[b - 1]).then_inc(xr_loaded, 16)
                    for n, (stack, part, parts, stacked) in enumerate((
                            (q_stack, q_part, Q_PARTS, q_stacked), (k_stack, k_part, K_PARTS, k_stacked))):
                        if not on(2):
                            continue
                        wait_apart(sp, st_done, b * UNITS)
                        for r, which in enumerate(parts):
                            wait_apart(sp, (qk_p0, qk_p1, qk_p2)[which], (b + 2) * 2 + n + 1)
                            for m in range(CT):
                                sp.dma_start(stack[r * HS:(r + 1) * HS, (k + 2) % 3, m * HM:(m + 1) * HM, :],
                                             part[:, which, m, :]).then_inc(stacked, 16)
                    if on(1):
                        wait_apart(sp, m_ready, b + 2)
                        for r in range(MROWS):
                            sp.dma_start(q_stack[SROWS + r:SROWS + r + 1, (k + 1) % 3, :, :],
                                         m_part[:, r, :]).then_inc(m_stacked, 16)
                    if on(-1):
                        wait_apart(sp, x1_ready, b + 1)
                        sp.dma_start(x1_tok[b - 1], x1_sb[:]).then_inc(x1_stored, 16)
                        wait_apart(sp, xn2_ready, b)
                        sp.dma_start(xn2_tok[b - 1], xn2_sb[:]).then_inc(xn2_stored, 16)

                steps_of(sp, step)
                sp.wait_ge(x1_stored, 16 * (BATCH + 1))
                sp.wait_ge(xn2_stored, 16 * (BATCH + 1))

            @block.tensor
            def _(pe):
                def s_fill(b, k, f):
                    g, part = divmod(f, 3)
                    wait(pe, s_max, (b + 1) * FILLS + f - 1)
                    qs, ks = q_stack[0:SROWS, (k + 1) % 3], k_stack[0:SROWS, (k + 1) % 3]
                    bank = s_ps[f % 2]
                    for j in range(2 if part < 2 else 4):
                        h = 4 * g + (2 * part + j if part < 2 else j)
                        qt, width = (1, T) if part < 2 else (0, P)
                        o = bank[:, j * width:(j + 1) * width]
                        nc.tensor.matmul(o, qs[:, h, qt * P:(qt + 1) * P], ks[:, h, 0:width], start=True, stop=False)
                        last = nc.tensor.matmul(o[:, width - P:width], identb[:], maskq[:], start=False, stop=True)
                    last.then_inc(s_done, 1)

                def st_unit(b, k, u):
                    wait(pe, p_ready, b * UNITS + u - 1)
                    qs, ks = q_stack[0:SROWS + MROWS, k % 3], k_stack[0:SROWS + MROWS, k % 3]
                    bank = st_ps[u % 2]
                    for kt in range(TT):
                        for j in range(2):
                            h = 2 * u + j
                            width = T - kt * P
                            o = bank[:, kt * 2 * T + j * width:kt * 2 * T + (j + 1) * width]
                            nc.tensor.matmul(o, ks[:, h, kt * P:(kt + 1) * P], qs[:, h, kt * P:T], start=True, stop=False)
                            last = nc.tensor.matmul(o[:, 0:P], identb[:], maskk[:], start=False, stop=True)
                    last.then_inc(st_done, 1)

                def pv_group(b, k, g):
                    wait(pe, p_ready, b * UNITS + 2 * g + 2)
                    wait(pe, yt_ready, b * GROUPS + g)
                    for kt in range(TT):
                        for j in range(4):
                            width = T - kt * P
                            pos = kt * 2 * T + (j % 2) * width
                            last = nc.tensor.matmul(
                                pv_ps[32 * j:32 * (j + 1), kt * P:T], v_sb[:, k % 3, kt, 4 * g + j, :],
                                prob_t[:, (2 * g + j // 2) % 4, pos:pos + width],
                                start=(kt == 0), stop=(kt == TT - 1), tile_position=(0, 32 * j))
                    last.then_inc(pv_done, 1)

                def project(dst, pairs, lhs_of, rhs_of):
                    for n, (a, c) in enumerate(pairs):
                        last = nc.tensor.matmul(dst, lhs_of(a, c), rhs_of(a, c), start=(n == 0), stop=(n == len(pairs) - 1))
                    return last

                PAIRS = [((px, pw), c) for px, pw in ((0, 0), (0, 1), (1, 0)) for c in range(CT)]
                xt = (xt_hi, xt_lo)

                def step(b, k):
                    loop = not isinstance(b, int)

                    def on(lag):
                        return loop or has(b, lag)

                    for u in range(UNITS):
                        if on(0):
                            if u == 0:
                                wait(pe, m_stacked, (b + 1) * MD)
                            st_unit(b, k, u)
                        if on(1) and u < 6:
                            if u == 0:
                                wait(pe, q_stacked, (b + 2) * QD)
                                wait(pe, k_stacked, (b + 2) * QD)
                            s_fill(b, k, 2 * u)
                            s_fill(b, k, 2 * u + 1)
                        if on(-1) and u == 0:
                            pv_group(b - 1, k - 1, GROUPS - 1)
                        if on(0) and u in (2, 4, 6):
                            pv_group(b, k, u // 2 - 1)
                        if on(2) and u == 1:
                            wait(pe, xn_ready, b + 3)
                            wait(pe, v_ready, b + 2)
                            for c in range(CT):
                                for t in range(TT):
                                    last = nc.tensor.transpose(w_half[:, c, t * P:(t + 1) * P],
                                                               xn[:, t, c * P:(c + 1) * P], ident[:])
                            last.then_inc(xt_done, 1)
                        if on(-1) and u in (2, 3):
                            t = u - 2
                            if t == 0:
                                wait(pe, yt_ready, b * GROUPS)
                                wait(pe, xt_lo_ready, b + 3 if on(2) else BATCH)
                                if not on(2):
                                    wait(pe, v_ready, BATCH)
                                    wait(pe, m_ready, min(b + 1, BATCH))
                                    wait(pe, y_ready, (b - 1) * TT)
                            else:
                                wait(pe, y_ready, (b - 1) * TT + 1)
                            for g in range(GROUPS):
                                last = nc.tensor.transpose(w_ps[:, g * P:(g + 1) * P],
                                                           yt_sb[:, (k - 1) % 3, g, t * P:(t + 1) * P], ident[:])
                            last.then_inc(ytr_done, 1)
                        if on(2) and u in (4, 5):
                            n = u - 4
                            w = ((wq_hi, wq_lo), (wk_hi, wk_lo))[n]
                            if n == 0:
                                wait(pe, xt_lo_ready, b + 3)
                                wait(pe, y_ready, b * TT)
                            else:
                                wait(pe, qk_rest, (b + 2) * 2 + 1)
                            for m in range(CT):
                                last = project(w_half[:, m, :], PAIRS,
                                               lambda a, c: w[a[1]][:, c, m * P:(m + 1) * P], lambda a, c: xt[a[0]][:, c, :])
                            last.then_inc(qk_done, 1)
                        if on(1) and u == 6:
                            wait(pe, s_max, (b + 2) * FILLS)
                            wait(pe, qk_rest, (b + 3) * 2 if on(2) else 2 * BATCH)
                            if not on(2):
                                wait(pe, y_ready, b * TT)
                            for t in range(TT):
                                last = nc.tensor.transpose(w_ps[0:HEADS, t * P:(t + 1) * P], rowmax[:, t, :], ident[:])
                            last.then_inc(mt_done, 1)
                        if on(2) and u == 7:
                            wait(pe, m_ready, b + 2)
                            if not on(1):
                                wait(pe, qk_rest, (b + 3) * 2)
                            for t in range(TT):
                                last = project(w_half[:, t, :], PAIRS,
                                               lambda a, c: xt[a[0]][:, c, t * P:(t + 1) * P],
                                               lambda a, c: (wv_hi, wv_lo)[a[1]][:, c, :])
                            last.then_inc(v_done, 1)

                steps_of(pe, step)

            @block.scalar
            def _(act):
                def step(b, k):
                    loop = not isinstance(b, int)

                    def on(lag):
                        return loop or has(b, lag)

                    def copy_group(bb, kk, g):
                        wait(act, pv_done, bb * GROUPS + g + 1)
                        nc.scalar.copy(yt_sb[:, kk % 3, g, :], pv_ps[:, 0:T]).then_inc(yt_ready, 1)

                    for u in range(UNITS):
                        if on(0):
                            wait(act, st_done, b * UNITS + u + 1)
                            wait(act, pv_done, b * GROUPS + u // 2 - 1)
                            nc.scalar.activation(prob_t[:, u % 4, :], st_ps[u % 2][:, 0:UNIT], ACT.Exp,
                                                 scale=SCALE).then_inc(p_ready, 1)
                        if on(-1) and u == 0:
                            copy_group(b - 1, k - 1, GROUPS - 1)
                        if on(0) and u in (2, 4, 6):
                            copy_group(b, k, u // 2 - 1)
                        if on(2) and u == 1:
                            wait(act, xt_done, b + 3)
                            nc.scalar.copy(xt_hi[:], w_half).then_inc(xt_hi_ready, 1)
                        if on(2) and u in (4, 5):
                            n = u - 4
                            wait(act, qk_done, (b + 2) * 2 + n + 1)
                            wait(act, (q_stacked, k_stacked)[n], (b + 2) * QD)
                            nc.scalar.copy((q_part, k_part)[n][:, 0], w_half).then_inc(qk_p0, 1)
                        if on(2) and u == 7:
                            wait(act, v_done, b + 3)
                            wait(act, pv_done, b * GROUPS)
                            for t in range(TT):
                                last = nc.scalar.copy(v_sb[:, (k + 2) % 3, t, :, 0:HS],
                                                      w_half[:, t, :].rearrange("p (h d) -> p h d", h=HEADS))
                            last.then_inc(v_ready, 1)

                steps_of(act, step)

            @block.vector
            def _(dve):
                def step(b, k):
                    loop = not isinstance(b, int)

                    def on(lag):
                        return loop or has(b, lag)

                    def stats(src, st, mv, count, bn_done, done):
                        for t in range(TT):
                            nc.vector.bn_stats(st[:, t, :], src[:, t, :]).then_inc(bn_done, 1)
                        for t in range(TT):
                            wait_apart(dve, bn_done, count * TT + t + 1)
                            nc.vector.bn_aggr(mv[:, t, :], st[:, t, :]).then_inc(done, 1)

                    for u in range(UNITS):
                        if on(1) and u < 6:
                            for f in (2 * u, 2 * u + 1):
                                g, part = divmod(f, 3)
                                wait(dve, s_done, (b + 1) * FILLS + f + 1)
                                if f == 0:
                                    wait(dve, mt_done, b + 1)
                                n, width = (2, T) if part < 2 else (4, P)
                                h = 4 * g + 2 * part if part < 2 else 4 * g
                                nc.vector.tensor_reduce(rowmax[:, 1 if part < 2 else 0, h:h + n],
                                                        s_ps[f % 2][:, :].rearrange("p (h k) -> p h k", h=n),
                                                        AX.X, ALU.max).then_inc(s_max, 1)
                        if on(2) and u == 1:
                            wait(dve, xt_hi_ready, b + 3)
                            nc.vector.tensor_tensor(xt_lo[:], w_half, xt_hi[:].bitcast(fp32), ALU.subtract).then_inc(xt_lo_ready, 1)
                        if on(-1) and u in (2, 3):
                            t = u - 2
                            wait(dve, ytr_done, (b - 1) * TT + t + 1)
                            heads = w_ps[:, :].rearrange("p (h d) -> p h d", d=32)
                            nc.vector.reciprocal(inv[:, t, :], heads[:, :, HS]).then_inc(inv_ready, 1)
                            wait(dve, inv_ready, (b - 1) * TT + t + 1)
                            if t == 0:
                                wait(dve, x1_ready, b)
                            nc.vector.tensor_tensor(y_sb[:, t, :].rearrange("p (h d) -> p h d", d=HS), heads[:, :, 0:HS],
                                                    inv[:, t, :].unsqueeze(2).to_broadcast([P, HEADS, HS]),
                                                    ALU.mult).then_inc(y_ready, 1)
                            if t == 1:
                                wait(dve, y_ready, b * TT)
                                stats(y_sb, sty, mvy, b - 1, bny_done, statsy)
                        if on(2) and u in (4, 5):
                            n = u - 4
                            wait(dve, qk_p0, (b + 2) * 2 + n + 1)
                            wait(dve, qk_p2, (b + 1) * 2 + n + 1)
                            nc.vector.tensor_tensor((q_rest, k_rest)[n][:], w_half, (q_part, k_part)[n][:, 0],
                                                    ALU.subtract).then_inc(qk_rest, 1)
                        if on(1) and u == 6:
                            wait(dve, mt_done, b + 2)
                            wait(dve, m_stacked, (b + 1) * MD)
                            base = (b + 1) * 3
                            nc.vector.tensor_copy(m_part[:, 0, :], w_ps[0:HEADS, 0:T]).then_inc(m_chain, 1)
                            wait(dve, m_chain, base + 1)
                            nc.vector.tensor_tensor(m_rest[:, 0, :], w_ps[0:HEADS, 0:T], m_part[:, 0, :],
                                                    ALU.subtract).then_inc(m_chain, 1)
                            wait(dve, m_chain, base + 2)
                            nc.vector.tensor_copy(m_part[:, 1, :], m_rest[:, 0, :]).then_inc(m_chain, 1)
                            wait(dve, m_chain, base + 3)
                            nc.vector.tensor_tensor(m_part[:, 2, :], m_rest[:, 0, :], m_part[:, 1, :],
                                                    ALU.subtract).then_inc(m_ready, 1)
                        if on(-1) and u == 7:
                            wait(dve, x1_ready, b + 1)
                            stats(x1_sb, st2, mv2, b - 1, bn2_done, stats2)
                        if on(3) and u == 7:
                            wait(dve, x_loaded[k % 3], ((b + 3) // 3 + 1) * 16 if isinstance(b, int) else (turn_of(b, k) + (k + 3) // 3 + 1) * 16)
                            wait(dve, xn_ready, b + 3)
                            stats(xa[:, k % 3], st1, mv1, b + 3, bn1_done, stats1)

                steps_of(dve, step)

            @block.gpsimd
            def _(pool):
                def rstd(mv, rs, count, veps, done):
                    nc.gpsimd.tensor_scalar(rs[:], mv[:, :, 1], EPS, None, ALU.add).then_inc(veps, 1)
                    wait_apart(pool, veps, count + 1)
                    nc.gpsimd.tensor_tensor(rs[:], rs[:], neg_half[:], ALU.pow).then_inc(done, 1)
                    wait_apart(pool, done, count + 1)

                def normalise(dst, src, mv, rs):
                    for t in range(TT):
                        last = nc.gpsimd.tensor_scalar(dst[:, t, :], src[:, t, :], mv[:, t, 0:1], rs[:, t:t + 1],
                                                       ALU.subtract, ALU.mult)
                    return last

                pool.sem_inc(x1_ready, 1)
                pool.sem_inc(x1_stored, 16)
                pool.sem_inc(xn2_stored, 16)

                def step(b, k):
                    loop = not isinstance(b, int)

                    def on(lag):
                        return loop or has(b, lag)

                    if on(-1):
                        wait_apart(pool, statsy, b * TT)
                        rstd(mvy, rsy, b - 1, vepsy, rstdy)
                        normalise(y_sb, y_sb, mvy, rsy).then_inc(lny, 1)
                        wait_apart(pool, lny, b)
                        wait_apart(pool, xr_loaded, 16 * b)
                        wait_apart(pool, x1_stored, 16 * b)
                        nc.gpsimd.tensor_tensor(x1_sb[:], y_sb[:], xr[:], ALU.add).then_inc(x1_ready, 1)
                    if on(2):
                        for n, (part, rest, stacked) in enumerate(((q_part, q_rest, q_stacked), (k_part, k_rest, k_stacked))):
                            wait_apart(pool, qk_rest, (b + 2) * 2 + n + 1)
                            wait_apart(pool, stacked, (b + 2) * QD)
                            nc.gpsimd.tensor_copy(part[:, 1], rest[:]).then_inc(qk_p1, 1)
                            wait_apart(pool, qk_p1, (b + 2) * 2 + n + 1)
                            nc.gpsimd.tensor_tensor(part[:, 2], rest[:], part[:, 1], ALU.subtract).then_inc(qk_p2, 1)
                    if on(-1):
                        wait_apart(pool, stats2, b * TT)
                        rstd(mv2, rs2, b - 1, veps2, rstd2)
                        wait_apart(pool, xn2_stored, 16 * b)
                        normalise(xn2_sb, x1_sb, mv2, rs2).then_inc(xn2_ready, 1)
                    if on(3):
                        wait_apart(pool, stats1, (b + 4) * TT)
                        wait_apart(pool, xt_done, b + 3)
                        rstd(mv1, rs1, b + 3, veps1, rstd1)
                        normalise(xn, xa[:, k % 3], mv1, rs1).then_inc(xn_ready, 1)

                steps_of(pool, step)

        with ExitStack() as c3:
            def sb3(name, shape, dt=fp32):
                return c3.enter_context(nc.sbuf_tensor(name, shape, dt))

            rx = sb3("rx", [P, 2, C])
            rxt_hi = sb3("rxt_hi", [P, 2, CT, P], f32r)
            rxt_lo = sb3("rxt_lo", [P, 2, CT, P], f32r)
            top_at = sb3("top_at", [P, TILES, 8], mybir.dt.uint32)
            at_f = sb3("at_f", [P, TILES, 2])
            columns = sb3("columns", [P, EXPERTS])
            gate = sb3("gate", [P, TILES, 2])
            hot = sb3("hot", [P, 2, TILES, EXPERTS])
            rt_ps = [c3.enter_context(nc.psum_tensor(f"rt_ps{n}", [P, 512], fp32)) for n in range(2)]
            rl_ps = [c3.enter_context(nc.psum_tensor(f"rl_ps{n}", [P, 512], fp32)) for n in range(2)]
            rx_loaded0, rx_loaded1, rt_done, rhi, rlo, rl_done, rl_copied, r_chain, r_exp, cols_ready = (
                sem(n) for n in ("rx_loaded0", "rx_loaded1", "rt_done", "rhi", "rlo", "rl_done", "rl_copied", "r_chain", "r_exp", "cols_ready"))
            rx_loaded = (rx_loaded0, rx_loaded1)
            block = c3.enter_context(nc.Block())

            @block.sync
            def _(sp):
                for t in range(2):
                    sp.dma_start(rx[:, t], xn2_tile[t]).then_inc(rx_loaded[t], 16)
                with sp.Fori(0, TILES // 2 - 1) as turn:
                    for n in range(2):
                        wait_apart(sp, rt_done, turn * 2 + (n + 1))
                        sp.dma_start(rx[:, n], xn2_tile[turn * 2 + (n + 2)]).then_inc(rx_loaded[n], 16)

            @block.tensor
            def _(pe):
                for t in range(TILES):
                    pe.wait_ge(rx_loaded[t % 2], 16 * (t // 2 + 1))
                    if t >= 2:
                        pe.wait_ge(rlo, t - 1)
                    for c in range(CT):
                        last = nc.tensor.transpose(rt_ps[t % 2][:, c * P:(c + 1) * P], rx[:, t % 2, c * P:(c + 1) * P], ident[:])
                    last.then_inc(rt_done, 1)
                    pe.wait_ge(rlo, t + 1)
                    if t >= 2:
                        pe.wait_ge(rl_copied, t - 1)
                    n = 0
                    for a, w in ((rxt_hi, r_hi), (rxt_hi, r_lo), (rxt_lo, r_hi)):
                        for c in range(CT):
                            last = nc.tensor.matmul(rl_ps[t % 2][:, 0:EXPERTS], a[:, t % 2, c, :], w[:, c, :],
                                                    start=(n == 0), stop=(n == 5))
                            n += 1
                    last.then_inc(rl_done, 1)

            @block.scalar
            def _(act):
                for t in range(TILES):
                    act.wait_ge(rt_done, t + 1)
                    if t >= 2:
                        act.wait_ge(rl_done, t - 1)
                    nc.scalar.copy(rxt_hi[:, t % 2], rt_ps[t % 2][:, 0:C].rearrange("p (c n) -> p c n", c=CT)).then_inc(rhi, 1)
                act.wait_ge(rl_copied, TILES * 3)
                nc.scalar.activation(gate[:], top8[:, :, 0:2], ACT.Exp, scale=-1.0).then_inc(r_exp, 1)

            @block.gpsimd
            def _(pool):
                nc.gpsimd.iota(columns[:], pattern=[[1, EXPERTS]], base=0, channel_multiplier=0,
                               allow_small_or_imprecise_dtypes=True).then_inc(cols_ready, 1)

            @block.vector
            def _(dve):
                for t in range(TILES):
                    dve.wait_ge(rhi, t + 1)
                    nc.vector.tensor_tensor(rxt_lo[:, t % 2], rt_ps[t % 2][:, 0:C].rearrange("p (c n) -> p c n", c=CT),
                                            rxt_hi[:, t % 2].bitcast(fp32), ALU.subtract).then_inc(rlo, 1)
                    dve.wait_ge(rl_done, t + 1)
                    nc.vector.tensor_copy(logits[:, t, :], rl_ps[t % 2][:, 0:EXPERTS]).then_inc(rl_copied, 1)
                dve.wait_ge(rl_copied, TILES)
                for t in range(TILES):
                    nc.vector.max(top8[:, t, :], logits[:, t, :]).then_inc(rl_copied, 1)
                dve.wait_ge(rl_copied, TILES * 2)
                for t in range(TILES):
                    nc.vector.max_index(top_at[:, t, :], top8[:, t, :], logits[:, t, :]).then_inc(rl_copied, 1)
                steps = [0]

                def step(ins):
                    steps[0] += 1
                    ins.then_inc(r_chain, 1)
                    dve.wait_ge(r_chain, steps[0])

                dve.wait_ge(rl_copied, TILES * 3)
                dve.wait_ge(r_exp, 1)
                dve.wait_ge(cols_ready, 1)
                step(nc.vector.tensor_copy(at_f[:], top_at[:, :, 0:2]))
                step(nc.vector.tensor_scalar(gate[:], gate[:], 1.0, None, ALU.add))
                step(nc.vector.reciprocal(gate[:], gate[:]))
                for k in range(2):
                    step(nc.vector.tensor_tensor(hot[:, k], columns[:].unsqueeze(1).to_broadcast([P, TILES, EXPERTS]),
                                                 at_f[:, :, k:k + 1].to_broadcast([P, TILES, EXPERTS]), ALU.is_equal))
                    step(nc.vector.tensor_tensor(hot[:, k], hot[:, k], gate[:, :, k:k + 1].to_broadcast([P, TILES, EXPERTS]), ALU.mult))
                step(nc.vector.tensor_tensor(probs[:], hot[:, 0], hot[:, 1], ALU.add))

        with ExitStack() as c4:
            def sb4(name, shape, dt=fp32):
                return c4.enter_context(nc.sbuf_tensor(name, shape, dt))

            ex = sb4("ex", [P, 2, C])
            ex1 = sb4("ex1", [P, 2, C])
            xin = sb4("xin", [P, 2, C])
            et_hi = sb4("et_hi", [P, 2, CT, P], f32r)
            et_lo = sb4("et_lo", [P, 2, CT, P], f32r)
            th = sb4("th", [P, 2, I])
            ga = sb4("ga", [P, 2, I])
            hh = sb4("hh", [P, 2, I])
            ht_hi = sb4("ht_hi", [P, 2, P], f32r)
            ht_lo = sb4("ht_lo", [P, 2, P], f32r)
            ones = sb4("ones", [P, 1])
            f_sb = sb4("f_sb", [P, 2, C])
            stf = sb4("stf", [P, 2, 6])
            mvf = sb4("mvf", [P, 2, 2])
            rsf = sb4("rsf", [P, 2])
            o_sb = sb4("o_sb", [P, 2, C])
            et_ps, gu_ps, ht_ps, f_ps = (
                [c4.enter_context(nc.psum_tensor(f"{nm}{n}", [P, 512], fp32)) for n in range(2)]
                for nm in ("et_ps", "gu_ps", "ht_ps", "f_ps"))
            (e_loaded0, e_loaded1, e1_loaded0, e1_loaded1, xin_ready, et_done, et_hi_ready, et_lo_ready, gu_done, th_ready, ga_ready, h_ready,
             ht_done, ht_hi_ready, ht_lo_ready, dn_done, f_ready, bnf_done, statsf, vepsf, rstdf, lnf, o_ready, o_stored) = (
                sem(n) for n in ("e_loaded0", "e_loaded1", "e1_loaded0", "e1_loaded1", "xin_ready", "et_done", "et_hi_ready", "et_lo_ready", "gu_done",
                                 "th_ready", "ga_ready", "h_ready", "ht_done", "ht_hi_ready", "ht_lo_ready", "dn_done", "f_ready",
                                 "bnf_done", "statsf", "vepsf", "rstdf", "lnf", "o_ready", "o_stored"))
            e_loaded, e1_loaded = (e_loaded0, e_loaded1), (e1_loaded0, e1_loaded1)
            block = c4.enter_context(nc.Block())

            @block.sync
            def _(sp):
                for t in range(TILES):
                    if t >= 2:
                        sp.wait_ge(xin_ready, NE * (t - 1))
                        sp.wait_ge(o_ready, t - 1)
                    sp.dma_start(ex[:, t % 2], xn2_tile[t]).then_inc(e_loaded[t % 2], 16)
                    sp.dma_start(ex1[:, t % 2], x1_tile[t]).then_inc(e1_loaded[t % 2], 16)
                    if t >= 2:
                        sp.dma_start(out_tile[t - 2], o_sb[:, t % 2]).then_inc(o_stored, 16)
                        sp.wait_ge(o_stored, 16 * (t - 1))
                for t in range(TILES, TILES + 2):
                    sp.wait_ge(o_ready, t - 1)
                    sp.wait_ge(o_stored, 16 * (t - 2))
                    sp.dma_start(out_tile[t - 2], o_sb[:, t % 2]).then_inc(o_stored, 16)
                sp.wait_ge(o_stored, 16 * TILES)

            @block.gpsimd
            def _(pool):
                nc.gpsimd.memset(ones[:], 1.0).then_inc(vepsf, 1)
                pool.wait_ge(vepsf, 1)

                def tail(t):
                    pool.wait_ge(statsf, t + 1)
                    nc.gpsimd.tensor_scalar(rsf[:, t % 2:t % 2 + 1], mvf[:, t % 2, 1:2], EPS, None, ALU.add).then_inc(vepsf, 1)
                    pool.wait_ge(vepsf, t + 2)
                    nc.gpsimd.tensor_tensor(rsf[:, t % 2:t % 2 + 1], rsf[:, t % 2:t % 2 + 1], neg_half[:, 0:1], ALU.pow).then_inc(rstdf, 1)
                    pool.wait_ge(rstdf, t + 1)
                    nc.gpsimd.tensor_scalar(f_sb[:, t % 2], f_sb[:, t % 2], mvf[:, t % 2, 0:1], rsf[:, t % 2:t % 2 + 1],
                                            ALU.subtract, ALU.mult).then_inc(lnf, 1)
                    pool.wait_ge(lnf, t + 1)
                    if t >= 2:
                        pool.wait_ge(o_stored, 16 * (t - 1))
                    pool.wait_ge(e1_loaded[t % 2], 16 * (t // 2 + 1))
                    nc.gpsimd.tensor_tensor(o_sb[:, t % 2], f_sb[:, t % 2], ex1[:, t % 2], ALU.add).then_inc(o_ready, 1)

                for t in range(TILES):
                    pool.wait_ge(e_loaded[t % 2], 16 * (t // 2 + 1))
                    for e in range(NE):
                        n = NE * t + e
                        if n >= 2:
                            pool.wait_ge(et_done, n - 1)
                        scale = probs[:, t, e:e + 1] if e < EXPERTS else ones[:]
                        nc.gpsimd.tensor_scalar(xin[:, n % 2], ex[:, t % 2], scale, None, ALU.mult).then_inc(xin_ready, 1)
                    if t >= 1:
                        tail(t - 1)
                tail(TILES - 1)

            N = TILES * NE

            @block.tensor
            def _(pe):
                for m in range(-2, N + 1):
                    n = m + 2
                    if n < N:
                        pe.wait_ge(xin_ready, n + 1)
                        if n >= 2:
                            pe.wait_ge(et_lo_ready, n - 1)
                        for c in range(CT):
                            last = nc.tensor.transpose(et_ps[n % 2][:, c * P:(c + 1) * P], xin[:, n % 2, c * P:(c + 1) * P], ident[:])
                        last.then_inc(et_done, 1)
                    n = m + 1
                    if 0 <= n < N:
                        pe.wait_ge(et_lo_ready, n + 1)
                        if n >= 2:
                            pe.wait_ge(h_ready, n - 1)
                        j = 0
                        for a, w in ((et_hi, gu_hi), (et_hi, gu_lo), (et_lo, gu_hi)):
                            for c in range(CT):
                                last = nc.tensor.matmul(gu_ps[n % 2][:, 0:GU], a[:, n % 2, c, :], w[:, n % NE, c, :], start=(j == 0), stop=(j == 5))
                                j += 1
                        last.then_inc(gu_done, 1)
                    n = m
                    if 0 <= n < N:
                        pe.wait_ge(h_ready, n + 1)
                        if n >= 2:
                            pe.wait_ge(ht_lo_ready, n - 1)
                        nc.tensor.transpose(ht_ps[n % 2][:, 0:P], hh[:, n % 2, :], ident[:]).then_inc(ht_done, 1)
                    n = m - 1
                    if 0 <= n:
                        pe.wait_ge(ht_lo_ready, n + 1)
                        t, e = divmod(n, NE)
                        if e == 0 and t >= 2:
                            pe.wait_ge(f_ready, t - 1)
                        for j, (a, w) in enumerate(((ht_hi, dn_hi), (ht_hi, dn_lo), (ht_lo, dn_hi))):
                            last = nc.tensor.matmul(f_ps[t % 2][:, 0:C], a[:, n % 2, :], w[:, e, :], start=(e == 0 and j == 0), stop=(e == NE - 1 and j == 2))
                        last.then_inc(dn_done, 1)

            @block.scalar
            def _(act):
                for m in range(-2, N + 1):
                    n = m + 2
                    if n < N:
                        act.wait_ge(et_done, n + 1)
                        if n >= 2:
                            act.wait_ge(gu_done, n - 1)
                        nc.scalar.copy(et_hi[:, n % 2], et_ps[n % 2][:, 0:C].rearrange("p (c n) -> p c n", c=CT)).then_inc(et_hi_ready, 1)
                    n = m + 1
                    if 0 <= n < N:
                        act.wait_ge(gu_done, n + 1)
                        if n >= 2:
                            act.wait_ge(ga_ready, n - 1)
                        nc.scalar.activation(th[:, n % 2], gu_ps[n % 2][:, 0:I], ACT.Tanh, scale=0.5).then_inc(th_ready, 1)
                    n = m
                    if 0 <= n < N:
                        act.wait_ge(ht_done, n + 1)
                        if n >= 2:
                            act.wait_ge(dn_done, n - 1)
                        nc.scalar.copy(ht_hi[:, n % 2], ht_ps[n % 2][:, 0:P]).then_inc(ht_hi_ready, 1)
                    n = m - 1
                    if n >= 0 and n % NE == NE - 1:
                        t = n // NE
                        act.wait_ge(dn_done, n + 1)
                        if t >= 2:
                            act.wait_ge(lnf, t - 1)
                            act.wait_ge(o_ready, t - 1)
                        nc.scalar.copy(f_sb[:, t % 2], f_ps[t % 2][:, 0:C]).then_inc(f_ready, 1)

            @block.vector
            def _(dve):
                for m in range(-2, N + 1):
                    n = m + 2
                    if n < N:
                        dve.wait_ge(et_hi_ready, n + 1)
                        nc.vector.tensor_tensor(et_lo[:, n % 2], et_ps[n % 2][:, 0:C].rearrange("p (c n) -> p c n", c=CT),
                                                et_hi[:, n % 2].bitcast(fp32), ALU.subtract).then_inc(et_lo_ready, 1)
                    n = m + 1
                    if 0 <= n < N:
                        dve.wait_ge(th_ready, n + 1)
                        nc.vector.scalar_tensor_tensor(out=ga[:, n % 2], in0=th[:, n % 2], scalar=1.0, in1=gu_ps[n % 2][:, 0:I],
                                                       op0=ALU.add, op1=ALU.mult).then_inc(ga_ready, 1)
                        dve.wait_ge(ga_ready, n + 1)
                        if n >= 2:
                            dve.wait_ge(ht_done, n - 1)
                        nc.vector.tensor_tensor(hh[:, n % 2], ga[:, n % 2], gu_ps[n % 2][:, I:GU], ALU.mult).then_inc(h_ready, 1)
                    n = m
                    if 0 <= n < N:
                        dve.wait_ge(ht_hi_ready, n + 1)
                        nc.vector.tensor_tensor(ht_lo[:, n % 2], ht_ps[n % 2][:, 0:P], ht_hi[:, n % 2].bitcast(fp32),
                                                ALU.subtract).then_inc(ht_lo_ready, 1)
                    n = m - 1
                    if n >= 0 and n % NE == NE - 1:
                        t = n // NE
                        dve.wait_ge(f_ready, t + 1)
                        nc.vector.bn_stats(stf[:, t % 2], f_sb[:, t % 2]).then_inc(bnf_done, 1)
                        dve.wait_ge(bnf_done, t + 1)
                        nc.vector.bn_aggr(mvf[:, t % 2], stf[:, t % 2]).then_inc(statsf, 1)


_INS = ["L0_attn_x", "L0_attn_Wq_w", "L0_attn_Wdkv_w", "L0_attn_Wuk_w", "L0_attn_Wuv_w", "L0_attn_Wo_w",
        "L0_ffn_router_w", "L0_ffn_gate_up_w", "L0_ffn_down_w", "L0_ffn_shared_gate_w", "L0_ffn_shared_up_w",
        "L0_ffn_shared_down_w"]


def kernel(**inputs):
    import numpy as _np
    import concourse.bacc as _bacc
    from concourse import mybir as _mybir
    from concourse.bass_utils import run_bass_kernel_spmd as _run

    nc = _bacc.Bacc("TRN2", target_bir_lowering=False, num_devices=1)
    arrays, args = {}, []
    for name in _INS:
        a = _np.ascontiguousarray(inputs[name])
        arrays[f"in_{name}_dram"] = a
        args.append(nc.dram_tensor(f"in_{name}_dram", a.shape, _mybir.dt.from_np(a.dtype), kind="ExternalInput").ap())
    shape = inputs["L0_attn_x"].shape
    args.append(nc.dram_tensor("out_dram", shape, _mybir.dt.float32, kind="ExternalOutput").ap())
    sandwich_block_kernel(nc, *args)
    r = _run(nc, [arrays], core_ids=[0])
    return r.results[0]["out_dram"]
```

```python
import concourse.bass as bass
from concourse import mybir
from contextlib import ExitStack


def sandwich_block_kernel(
    nc: bass.Bass,
    x: bass.AP,
    w_q: bass.AP,
    w_dkv: bass.AP,
    w_uk: bass.AP,
    w_uv: bass.AP,
    w_o: bass.AP,
    router_w: bass.AP,
    gate_up_w: bass.AP,
    down_w: bass.AP,
    shared_gate_w: bass.AP,
    shared_up_w: bass.AP,
    shared_down_w: bass.AP,
    out: bass.AP,
):
    fp32 = mybir.dt.float32
    f32r = mybir.dt.float32r
    bf16 = mybir.dt.bfloat16
    ALU = mybir.AluOpType
    ACT = mybir.ActivationFunctionType
    AX = mybir.AxisListType
    f16 = mybir.dt.float16
    u32 = mybir.dt.uint32
    i32 = mybir.dt.int32

    P = 128
    BATCH, T, C = x.shape
    NL = w_dkv.shape[0]
    HEADS = 16
    HS = C // HEADS
    TT = T // P
    CT = C // P
    HM = HEADS // CT
    EXPERTS, _, GU = gate_up_w.shape
    I = GU // 2
    TILES = BATCH * TT
    EPS = 1e-5
    MASK = -1e30
    SCALE = float(HS) ** -0.5
    SHARED = EXPERTS
    NE = EXPERTS + 1
    GW = GU + EXPERTS
    TOKENS = BATCH * T
    LOG_P = P.bit_length() - 1
    BLOCKS = 2 * TOKENS // P + EXPERTS

    Q_PARTS = [0, 0, 1, 1, 0, 2]
    K_PARTS = [0, 1, 0, 1, 2, 0]
    SROWS = HS * len(Q_PARTS)
    MROWS = 3
    UNIT = 2 * T + 2 * P
    UNITS = HEADS // 2
    GROUPS = HEADS // 4
    FILLS = 3 * GROUPS

    x_tok = x.rearrange("b (t p) c -> b p t c", p=P)
    x1_dram = nc.dram_tensor("x1_scratch", (BATCH, T, C), fp32, kind="Internal").ap()
    xn2_dram = nc.dram_tensor("xn2_scratch", (BATCH, T, C), fp32, kind="Internal").ap()
    x1_tok = x1_dram.rearrange("b (t p) c -> b p t c", p=P)
    xn2_tok = xn2_dram.rearrange("b (t p) c -> b p t c", p=P)
    x1_tile = x1_dram.rearrange("b (t p) c -> (b t) p c", p=P)
    xn2_tile = xn2_dram.rearrange("b (t p) c -> (b t) p c", p=P)
    xn2_rows = xn2_dram.rearrange("b t c -> (b t) c")
    o_rows = nc.dram_tensor("o_scratch", (BLOCKS * P, C), fp32, kind="Internal").ap()
    o_dram = o_rows.rearrange("(n p) c -> n p c", p=P)
    out_tile = out.rearrange("b (t p) c -> (b t) p c", p=P)

    ctx = ExitStack()
    with ctx:
        def sb(name, shape, dt=fp32):
            return ctx.enter_context(nc.sbuf_tensor(name, shape, dt))

        def ps(name, shape):
            return ctx.enter_context(nc.psum_tensor(name, shape, fp32))

        def sem(name):
            return ctx.enter_context(nc.semaphore(name))

        ident = sb("ident", [P, P])
        identb = sb("identb", [P, P], bf16)
        maskq = sb("maskq", [P, P], bf16)
        maskk = sb("maskk", [P, P], bf16)
        neg_half = sb("neg_half", [P, TT])
        gu_hi = sb("gu_hi", [P, NE, CT, GW], f32r)
        gu_lo = sb("gu_lo", [P, NE, CT, GW], f32r)
        dn_hi = sb("dn_hi", [P, NE, C], f32r)
        dn_lo = sb("dn_lo", [P, NE, C], f32r)

        ctx1 = ExitStack()

        def sb1(name, shape, dt=fp32):
            return ctx1.enter_context(nc.sbuf_tensor(name, shape, dt))

        wq_hi, wq_lo, wk_hi, wk_lo, wv_hi, wv_lo = (
            sb1(n, [P, CT, C], f32r) for n in ("wq_hi", "wq_lo", "wk_hi", "wk_lo", "wv_hi", "wv_lo"))
        xa = sb1("xa", [P, 3, TT, C])
        xr = sb1("xr", [P, TT, C])
        xn = sb1("xn", [P, TT, C])
        st1 = sb1("st1", [P, TT, 6])
        mv1 = sb1("mv1", [P, TT, 2])
        rs1 = sb1("rs1", [P, TT])
        xt_hi = sb1("xt_hi", [P, CT, T], f32r)
        xt_lo = sb1("xt_lo", [P, CT, T], f32r)
        q_part = sb1("q_part", [P, 3, CT, T], bf16)
        k_part = sb1("k_part", [P, 3, CT, T], bf16)
        q_rest = sb1("q_rest", [P, CT, T])
        k_rest = sb1("k_rest", [P, CT, T])
        q_stack = sb1("q_stack", [P, 3, HEADS, T], bf16)
        k_stack = sb1("k_stack", [P, 3, HEADS, T], bf16)
        v_sb = sb1("v_sb", [P, 3, TT, HEADS, 32])
        rowmax = sb1("rowmax", [P, TT, HEADS])
        m_part = sb1("m_part", [HEADS, 3, T], bf16)
        m_rest = sb1("m_rest", [HEADS, 2, T])
        prob_t = sb1("prob_t", [P, 4, UNIT])
        yt_sb = sb1("yt_sb", [P, 3, GROUPS, T])
        inv = sb1("inv", [P, TT, HEADS])
        y_sb = sb1("y_sb", [P, TT, C])
        sty = sb1("sty", [P, TT, 6])
        mvy = sb1("mvy", [P, TT, 2])
        rsy = sb1("rsy", [P, TT])
        x1_sb = sb1("x1_sb", [P, TT, C])
        st2 = sb1("st2", [P, TT, 6])
        mv2 = sb1("mv2", [P, TT, 2])
        rs2 = sb1("rs2", [P, TT])
        xn2_sb = sb1("xn2_sb", [P, TT, C])

        consts_ready = sem("consts_ready")
        w_loaded = sem("w_loaded")
        prep_pe = sem("prep_pe")
        prep_copied = sem("prep_copied")
        gu_loaded = [sem(f"gu_loaded{n}") for n in range(3)]
        gu_split = sem("gu_split")
        prep_chain = sem("prep_chain")
        x_loaded = [sem(f"x_loaded{n}") for n in range(3)]
        xr_loaded = sem("xr_loaded")
        bn1_done = sem("bn1_done")
        stats1 = sem("stats1")
        veps1 = sem("veps1")
        rstd1 = sem("rstd1")
        xn_ready = sem("xn_ready")
        xt_done = sem("xt_done")
        xt_hi_ready = sem("xt_hi_ready")
        xt_lo_ready = sem("xt_lo_ready")
        qk_done = sem("qk_done")
        qk_p0 = sem("qk_p0")
        qk_rest = sem("qk_rest")
        qk_p1 = sem("qk_p1")
        qk_p2 = sem("qk_p2")
        v_done = sem("v_done")
        v_ready = sem("v_ready")
        q_stacked = sem("q_stacked")
        k_stacked = sem("k_stacked")
        m_stacked = sem("m_stacked")
        s_done = sem("s_done")
        s_max = sem("s_max")
        mt_done = sem("mt_done")
        m_chain = sem("m_chain")
        m_ready = sem("m_ready")
        st_done = sem("st_done")
        p_ready = sem("p_ready")
        pv_done = sem("pv_done")
        yt_ready = sem("yt_ready")
        ytr_done = sem("ytr_done")
        inv_ready = sem("inv_ready")
        y_ready = sem("y_ready")
        bny_done = sem("bny_done")
        statsy = sem("statsy")
        vepsy = sem("vepsy")
        rstdy = sem("rstdy")
        lny = sem("lny")
        x1_ready = sem("x1_ready")
        bn2_done = sem("bn2_done")
        stats2 = sem("stats2")
        veps2 = sem("veps2")
        rstd2 = sem("rstd2")
        x1_stored = sem("x1_stored")
        xn2_stored = sem("xn2_stored")
        xn2_ready = sem("xn2_ready")

        QD = 16 * len(Q_PARTS)
        MD = 16 * MROWS

        with ExitStack() as c0:
            def sb0(name, shape, dt=fp32):
                return c0.enter_context(nc.sbuf_tensor(name, shape, dt))

            wq_raw = sb0("wq_raw", [P, CT, C])
            wo_raw = sb0("wo_raw", [P, CT, C])
            wuk_raw = sb0("wuk_raw", [P, CT, NL])
            wuv_raw = sb0("wuv_raw", [P, CT, NL])
            wdkv_raw = sb0("wdkv_raw", [NL, C])
            wo_t = sb0("wo_t", [P, CT, C])
            keff_t = sb0("keff_t", [NL, C])
            veff = sb0("veff", [NL, C])
            full = sb0("full", [P, 3, CT, C])
            r_raw = sb0("r_raw", [P, CT, EXPERTS])
            gu_raw = prob_t[:, :, :].rearrange("p a b -> p (a b)")[:, 0:3 * CT * GU].rearrange(
                "p (e c n) -> p e c n", e=3, c=CT)
            dn_raw = yt_sb[:, :, :, :].rearrange("p a b c -> p (a b c)")[:, 0:NE * C].rearrange(
                "p (e c) -> p e c", e=NE)
            pt = [c0.enter_context(nc.psum_tensor(f"pt{n}", [P, 512], fp32)) for n in range(6)]
            block = c0.enter_context(nc.Block())

            @block.sync
            def _(sp):
                for dst, src in ((wq_raw, w_q), (wo_raw, w_o), (wuk_raw, w_uk), (wuv_raw, w_uv),
                                 (r_raw, router_w)):
                    sp.dma_start(dst[:], src.rearrange("(t p) n -> p t n", p=P)).then_inc(w_loaded, 16)
                sp.dma_start(wdkv_raw[:], w_dkv).then_inc(w_loaded, 16)
                sp.dma_start(dn_raw[:, 0:EXPERTS, :], down_w.rearrange("e i c -> i e c")).then_inc(w_loaded, 16)
                sp.dma_start(dn_raw[:, SHARED, :], shared_down_w).then_inc(w_loaded, 16)
                for e in range(NE):
                    if e >= 3:
                        sp.wait_ge(gu_split, e - 2)
                    if e < EXPERTS:
                        sp.dma_start(gu_raw[:, e % 3], gate_up_w[e].rearrange("(t p) n -> p t n", p=P)).then_inc(gu_loaded[e % 3], 32)
                    else:
                        sp.dma_start(gu_raw[:, e % 3, :, 0:I], shared_gate_w.rearrange("(t p) n -> p t n", p=P)).then_inc(gu_loaded[e % 3], 16)
                        sp.dma_start(gu_raw[:, e % 3, :, I:GU], shared_up_w.rearrange("(t p) n -> p t n", p=P)).then_inc(gu_loaded[e % 3], 16)

            @block.gpsimd
            def _(pool):
                nc.gpsimd.memset(ident[:], 0.0).then_inc(consts_ready, 1)
                nc.gpsimd.memset(maskq[:], 0.0).then_inc(consts_ready, 1)
                nc.gpsimd.memset(maskk[:], 0.0).then_inc(consts_ready, 1)
                nc.gpsimd.memset(neg_half[:], -0.5).then_inc(consts_ready, 1)
                nc.gpsimd.memset(v_sb[:], 0.0).then_inc(consts_ready, 1)
                pool.wait_ge(consts_ready, 6)
                nc.gpsimd.memset(v_sb[:, :, :, :, HS:HS + 1], 1.0).then_inc(consts_ready, 1)
                nc.gpsimd.affine_select(out=ident[:], in_=ident[:], compare_op=ALU.not_equal, fill=1.0, base=0,
                                        pattern=[[-1, P]], channel_multiplier=1).then_inc(consts_ready, 1)
                nc.gpsimd.affine_select(out=maskq[:], in_=maskq[:], compare_op=ALU.is_ge, fill=MASK, base=0,
                                        pattern=[[-1, P]], channel_multiplier=1).then_inc(consts_ready, 1)
                nc.gpsimd.affine_select(out=maskk[:], in_=maskk[:], compare_op=ALU.is_ge, fill=MASK, base=0,
                                        pattern=[[1, P]], channel_multiplier=-1).then_inc(consts_ready, 1)
                pool.wait_ge(consts_ready, 10)
                nc.gpsimd.tensor_copy(identb[:], ident[:]).then_inc(consts_ready, 1)
                pool.wait_ge(w_loaded, 16 * 8)
                nc.gpsimd.tensor_scalar(dn_raw[:], dn_raw[:], 0.5, None, ALU.mult).then_inc(consts_ready, 1)

            @block.tensor
            def _(pe):
                pe.wait_ge(consts_ready, 12)
                for n, raw in enumerate((wq_raw, wo_raw)):
                    for ct in range(CT):
                        for rt in range(CT):
                            last = nc.tensor.transpose(pt[n][:, ct * C + rt * P:ct * C + (rt + 1) * P],
                                                       raw[:, rt, ct * P:(ct + 1) * P], ident[:])
                last.then_inc(prep_pe, 1)
                for ct in range(CT):
                    last = nc.tensor.matmul(pt[2][0:NL, 0:C], wuk_raw[:, ct, :], wq_raw[:, ct, :],
                                            start=(ct == 0), stop=(ct == CT - 1))
                last.then_inc(prep_pe, 1)
                pe.wait_ge(prep_copied, 1)
                for ct in range(CT):
                    last = nc.tensor.matmul(pt[3][0:NL, 0:C], wuv_raw[:, ct, :], wo_t[:, ct, :],
                                            start=(ct == 0), stop=(ct == CT - 1))
                last.then_inc(prep_pe, 1)
                pe.wait_ge(prep_copied, 3)
                for n, eff in ((4, keff_t), (5, veff)):
                    for ct in range(CT):
                        last = nc.tensor.matmul(pt[n][:, ct * C:(ct + 1) * C], wdkv_raw[:, ct * P:(ct + 1) * P],
                                                eff[:], start=True, stop=True)
                last.then_inc(prep_pe, 1)

            @block.scalar
            def _(act):
                act.wait_ge(prep_pe, 1)
                nc.scalar.copy(wo_t[:], pt[1][:].rearrange("p (t n) -> p t n", t=CT)).then_inc(prep_copied, 1)
                act.wait_ge(prep_pe, 2)
                nc.scalar.copy(keff_t[:], pt[2][0:NL, 0:C]).then_inc(prep_copied, 1)
                act.wait_ge(prep_pe, 3)
                nc.scalar.copy(veff[:], pt[3][0:NL, 0:C]).then_inc(prep_copied, 1)
                for e in range(NE):
                    act.wait_ge(gu_loaded[e % 3], 32 * (e // 3 + 1))
                    nc.scalar.copy(gu_hi[:, e, :, 0:GU], gu_raw[:, e % 3]).then_inc(prep_copied, 1)

            @block.vector
            def _(dve):
                steps = [0]

                def step(ins):
                    steps[0] += 1
                    ins.then_inc(prep_chain, 1)
                    dve.wait_ge(prep_chain, steps[0])

                for w in (gu_hi, gu_lo):
                    step(nc.vector.memset(w[:, 0:EXPERTS, :, GU + 1:GW].bitcast(fp32), 0.0))
                nc.vector.memset(k_stack[SROWS:P], -1.0).then_inc(consts_ready, 1)
                dve.wait_ge(prep_pe, 1)
                for ct in range(CT):
                    step(nc.vector.tensor_copy(
                        full[:, 0, ct, :].rearrange("p (m d h) -> p m h d", m=CT, h=HM),
                        pt[0][:, ct * C:(ct + 1) * C].rearrange("p (h m d) -> p m h d", m=CT, h=HM)))
                dve.wait_ge(prep_pe, 4)
                for ct in range(CT):
                    step(nc.vector.tensor_copy(
                        full[:, 1, ct, :].rearrange("p (m d h) -> p m h d", m=CT, h=HM),
                        pt[4][:, ct * C:(ct + 1) * C].rearrange("p (h m d) -> p m h d", m=CT, h=HM)))
                step(nc.vector.tensor_copy(full[:, 2], pt[5][:].rearrange("p (t n) -> p t n", t=CT)))
                for n, (hi, lo) in enumerate(((wq_hi, wq_lo), (wk_hi, wk_lo), (wv_hi, wv_lo))):
                    step(nc.vector.tensor_copy(hi[:], full[:, n]))
                    step(nc.vector.tensor_tensor(lo[:], full[:, n], hi[:].bitcast(fp32), ALU.subtract))
                dve.wait_ge(consts_ready, 12)
                for hi, lo, raw in [(gu_hi[:, SHARED, :, GU:GW], gu_lo[:, SHARED, :, GU:GW], r_raw[:])] + [
                        (gu_hi[:, e, :, GU:GU + 1], gu_lo[:, e, :, GU:GU + 1], r_raw[:, :, e:e + 1]) for e in range(EXPERTS)]:
                    step(nc.vector.tensor_copy(hi, raw))
                    step(nc.vector.tensor_tensor(lo, raw, hi.bitcast(fp32), ALU.subtract))
                step(nc.vector.tensor_copy(dn_hi[:], dn_raw[:]))
                step(nc.vector.tensor_tensor(dn_lo[:], dn_raw[:], dn_hi[:].bitcast(fp32), ALU.subtract))
                for e in range(NE):
                    dve.wait_ge(prep_copied, 3 + e + 1)
                    nc.vector.tensor_tensor(gu_lo[:, e, :, 0:GU], gu_raw[:, e % 3], gu_hi[:, e, :, 0:GU].bitcast(fp32),
                                            ALU.subtract).then_inc(gu_split, 1)
                dve.wait_ge(gu_split, NE)
                dve.wait_ge(consts_ready, 12)

        st_ps = [ctx1.enter_context(nc.psum_tensor(f"st_ps{n}", [P, 1024], fp32)) for n in range(2)]
        s_ps = [ctx1.enter_context(nc.psum_tensor(f"s_ps{n}", [P, 512], fp32)) for n in range(2)]
        pv_ps = ctx1.enter_context(nc.psum_tensor("pv_ps", [P, 512], fp32))
        w_ps = ctx1.enter_context(nc.psum_tensor("w_ps", [P, 512], fp32))
        w_half = w_ps[:, :].rearrange("p (t n) -> p t n", t=2)

        BODY = 3
        FIRST = 2
        LAST = FIRST + (BATCH - 3 - FIRST) // BODY * BODY - 1
        turns = [0]

        def steps_of(eng, step):
            for b in range(-3, FIRST):
                step(b, b)
            with eng.Fori(0, (LAST - FIRST + 1) // BODY) as turn:
                turns[0] = turn
                for n in range(BODY):
                    step(turn * BODY + (FIRST + n), FIRST + n)
            for b in range(LAST + 1, BATCH + 2):
                step(b, b)

        def loads_of(b, k):
            return (b + 3) // 3 + 1 if isinstance(b, int) else turns[0] + ((k + 3) // 3 + 1)

        def present(b):
            return lambda lag: not isinstance(b, int) or 0 <= b + lag < BATCH

        def wait(eng, semaphore, value):
            if not isinstance(value, int) or value > 0:
                eng.wait_ge(semaphore, value)

        passed = sem("passed")

        def wait_apart(eng, semaphore, value):
            wait(eng, semaphore, value)
            if not isinstance(value, int):
                eng.sem_inc(passed, 1)

        FILLS_AT = [range(0, 3), range(3, 6), range(6, 8), range(8, 10), range(10, 12), (), (), ()]

        with ctx1, ExitStack() as c2:
            block = c2.enter_context(nc.Block())

            @block.sync
            def _(sp):
                def step(b, k):
                    on = present(b)
                    if on(3):
                        wait_apart(sp, xn_ready, b + 1)
                        sp.dma_start(xa[:, k % 3], x_tok[b + 3]).then_inc(x_loaded[k % 3], 16)
                    if on(-2):
                        wait_apart(sp, x1_ready, b - 1)
                        sp.dma_start(xr[:], x_tok[b - 2]).then_inc(xr_loaded, 16)
                    for n, (stack, part, parts, stacked) in enumerate((
                            (q_stack, q_part, Q_PARTS, q_stacked), (k_stack, k_part, K_PARTS, k_stacked))):
                        if not on(2):
                            continue
                        wait_apart(sp, st_done, b * UNITS)
                        for which in range(3):
                            wait_apart(sp, (qk_p0, qk_p1, qk_p2)[which], (b + 2) * 2 + n + 1)
                            for r in range(len(parts)):
                                if parts[r] == which:
                                    sp.dma_start(stack[r * HS:(r + 1) * HS, (k + 2) % 3, :, :],
                                                 part[:, which]).then_inc(stacked, 16)
                    if on(-2):
                        wait_apart(sp, x1_ready, b)
                        sp.dma_start(x1_tok[b - 2], x1_sb[:]).then_inc(x1_stored, 16)
                    if on(1):
                        wait_apart(sp, m_ready, b + 2)
                        for r in range(MROWS):
                            sp.dma_start(q_stack[SROWS + r:SROWS + r + 1, (k + 1) % 3, :, :],
                                         m_part[:, r, :]).then_inc(m_stacked, 16)
                    if on(-2):
                        wait_apart(sp, xn2_ready, b - 1)
                        sp.dma_start(xn2_tok[b - 2], xn2_sb[:]).then_inc(xn2_stored, 16)

                steps_of(sp, step)
                sp.wait_ge(x1_stored, 16 * (BATCH + 1))
                sp.wait_ge(xn2_stored, 16 * (BATCH + 1))

            @block.tensor
            def _(pe):
                def s_fill(b, k, f):
                    g, part = divmod(f, 3)
                    wait(pe, s_max, (b + 1) * FILLS + f - 1)
                    qs, ks = q_stack[0:SROWS, (k + 1) % 3], k_stack[0:SROWS, (k + 1) % 3]
                    bank = s_ps[f % 2]
                    for j in range(2 if part < 2 else 4):
                        h = 4 * g + (2 * part + j if part < 2 else j)
                        qt, width = (1, T) if part < 2 else (0, P)
                        o = bank[:, j * width:(j + 1) * width]
                        nc.tensor.matmul(o, qs[:, h, qt * P:(qt + 1) * P], ks[:, h, 0:width], start=True, stop=False)
                        last = nc.tensor.matmul(o[:, width - P:width], identb[:], maskq[:], start=False, stop=True)
                    last.then_inc(s_done, 1)

                def st_unit(b, k, u):
                    wait(pe, p_ready, b * UNITS + u - 1)
                    qs, ks = q_stack[0:SROWS + MROWS, k % 3], k_stack[0:SROWS + MROWS, k % 3]
                    bank = st_ps[u % 2]
                    for kt in range(TT):
                        for j in range(2):
                            h = 2 * u + j
                            width = T - kt * P
                            o = bank[:, kt * 2 * T + j * width:kt * 2 * T + (j + 1) * width]
                            nc.tensor.matmul(o, ks[:, h, kt * P:(kt + 1) * P], qs[:, h, kt * P:T], start=True, stop=False)
                            last = nc.tensor.matmul(o[:, 0:P], identb[:], maskk[:], start=False, stop=True)
                    last.then_inc(st_done, 1)

                def pv_group(b, k, g):
                    wait(pe, p_ready, b * UNITS + 2 * g + 2)
                    wait(pe, yt_ready, b * GROUPS + g)
                    for kt in range(TT):
                        for j in range(4):
                            width = T - kt * P
                            pos = kt * 2 * T + (j % 2) * width
                            last = nc.tensor.matmul(
                                pv_ps[32 * j:32 * (j + 1), kt * P:T], v_sb[:, k % 3, kt, 4 * g + j, :],
                                prob_t[:, (2 * g + j // 2) % 4, pos:pos + width],
                                start=(kt == 0), stop=(kt == TT - 1), tile_position=(0, 32 * j))
                    last.then_inc(pv_done, 1)

                def project(dst, lhs_of, rhs_of):
                    pairs = [(a, c) for a in ((0, 0), (0, 1), (1, 0)) for c in range(CT)]
                    for n, (a, c) in enumerate(pairs):
                        last = nc.tensor.matmul(dst, lhs_of(a, c), rhs_of(a, c), start=(n == 0), stop=(n == len(pairs) - 1))
                    return last

                xt = (xt_hi, xt_lo)
                w_free = [None]

                def step(b, k):
                    on = present(b)
                    if not isinstance(b, int):
                        w_free[0] = (y_ready, (b - 1) * TT)

                    def take_w(semaphore, value):
                        if w_free[0]:
                            wait(pe, *w_free[0])
                        w_free[0] = (semaphore, value)

                    for u in range(UNITS):
                        if on(0):
                            if u == 0:
                                wait(pe, m_stacked, (b + 1) * MD)
                            st_unit(b, k, u)
                        if on(1):
                            if u == 0:
                                wait(pe, q_stacked, (b + 2) * QD)
                                wait(pe, k_stacked, (b + 2) * QD)
                            for f in FILLS_AT[u]:
                                s_fill(b, k, f)
                        if on(-1) and u == 0:
                            pv_group(b - 1, k - 1, GROUPS - 1)
                        if on(0) and u in (2, 4, 6):
                            pv_group(b, k, u // 2 - 1)
                        if on(2) and u == 0:
                            take_w(xt_lo_ready, b + 3)
                            wait(pe, xn_ready, b + 3)
                            for c in range(CT):
                                for t in range(TT):
                                    last = nc.tensor.transpose(w_half[:, c, t * P:(t + 1) * P],
                                                               xn[:, t, c * P:(c + 1) * P], ident[:])
                            last.then_inc(xt_done, 1)
                        if on(2) and u in (1, 2):
                            n = u - 1
                            w = ((wq_hi, wq_lo), (wk_hi, wk_lo))[n]
                            take_w(qk_rest, (b + 2) * 2 + n + 1)
                            for m in range(CT):
                                last = project(w_half[:, m, :],
                                               lambda a, c: w[a[1]][:, c, m * P:(m + 1) * P], lambda a, c: xt[a[0]][:, c, :])
                            last.then_inc(qk_done, 1)
                        if on(2) and u == 3:
                            take_w(v_ready, b + 3)
                            for t in range(TT):
                                last = project(w_half[:, t, :],
                                               lambda a, c: xt[a[0]][:, c, t * P:(t + 1) * P],
                                               lambda a, c: (wv_hi, wv_lo)[a[1]][:, c, :])
                            last.then_inc(v_done, 1)
                        if on(-1) and u in (4, 6):
                            t = (u - 4) // 2
                            take_w(y_ready, (b - 1) * TT + t + 1)
                            wait(pe, yt_ready, b * GROUPS)
                            for g in range(GROUPS):
                                last = nc.tensor.transpose(w_ps[:, g * P:(g + 1) * P],
                                                           yt_sb[:, (k - 1) % 3, g, t * P:(t + 1) * P], ident[:])
                            last.then_inc(ytr_done, 1)
                        if on(1) and u == 5:
                            take_w(m_ready, b + 2)
                            wait(pe, s_max, (b + 2) * FILLS)
                            for t in range(TT):
                                last = nc.tensor.transpose(w_ps[0:HEADS, t * P:(t + 1) * P], rowmax[:, t, :], ident[:])
                            last.then_inc(mt_done, 1)

                steps_of(pe, step)

            @block.scalar
            def _(act):
                def step(b, k):
                    on = present(b)

                    def copy_group(bb, kk, g):
                        wait(act, pv_done, bb * GROUPS + g + 1)
                        nc.scalar.copy(yt_sb[:, kk % 3, g, :], pv_ps[:, 0:T]).then_inc(yt_ready, 1)

                    def second_part(n):
                        wait(act, qk_rest, (b + 2) * 2 + n + 1)
                        nc.scalar.copy((q_part, k_part)[n][:, 1], (q_rest, k_rest)[n][:]).then_inc(qk_p1, 1)

                    for u in range(UNITS):
                        if on(0):
                            wait(act, st_done, b * UNITS + u + 1)
                            wait(act, pv_done, b * GROUPS + u // 2 - 1)
                            nc.scalar.activation(prob_t[:, u % 4, :], st_ps[u % 2][:, 0:UNIT], ACT.Exp,
                                                 scale=SCALE).then_inc(p_ready, 1)
                        if on(-1) and u == 0:
                            copy_group(b - 1, k - 1, GROUPS - 1)
                        if on(0) and u in (2, 4, 6):
                            copy_group(b, k, u // 2 - 1)
                        if on(2) and u == 0:
                            wait(act, xt_done, b + 3)
                            nc.scalar.copy(xt_hi[:], w_half).then_inc(xt_hi_ready, 1)
                        if on(2) and u in (1, 2):
                            n = u - 1
                            wait(act, qk_done, (b + 2) * 2 + n + 1)
                            wait(act, (q_stacked, k_stacked)[n], (b + 2) * QD)
                            nc.scalar.copy((q_part, k_part)[n][:, 0], w_half).then_inc(qk_p0, 1)
                        if on(2) and u == 2:
                            second_part(0)
                        if on(2) and u == 3:
                            second_part(1)
                            wait(act, v_done, b + 3)
                            wait(act, pv_done, b * GROUPS)
                            for t in range(TT):
                                last = nc.scalar.copy(v_sb[:, (k + 2) % 3, t, :, 0:HS],
                                                      w_half[:, t, :].rearrange("p (h d) -> p h d", h=HEADS))
                            last.then_inc(v_ready, 1)

                steps_of(act, step)

            @block.vector
            def _(dve):
                def step(b, k):
                    on = present(b)

                    def stats(src, st, mv, count, bn_done, done):
                        for t in range(TT):
                            nc.vector.bn_stats(st[:, t, :], src[:, t, :]).then_inc(bn_done, 1)
                        for t in range(TT):
                            wait_apart(dve, bn_done, count * TT + t + 1)
                            nc.vector.bn_aggr(mv[:, t, :], st[:, t, :]).then_inc(done, 1)

                    def normalise(dst, src, mv, rs):
                        for t in range(TT):
                            last = nc.vector.tensor_scalar(dst[:, t, :], src[:, t, :], mv[:, t, 0:1], rs[:, t:t + 1],
                                                           ALU.subtract, ALU.mult)
                        return last

                    for u in range(UNITS):
                        if on(1):
                            for f in FILLS_AT[u]:
                                g, part = divmod(f, 3)
                                wait(dve, s_done, (b + 1) * FILLS + f + 1)
                                if f == 0:
                                    wait(dve, mt_done, b + 1)
                                n, width = (2, T) if part < 2 else (4, P)
                                h = 4 * g + 2 * part if part < 2 else 4 * g
                                nc.vector.tensor_reduce(rowmax[:, 1 if part < 2 else 0, h:h + n],
                                                        s_ps[f % 2][:, :].rearrange("p (h k) -> p h k", h=n),
                                                        AX.X, ALU.max).then_inc(s_max, 1)
                        if on(2) and u == 0:
                            wait(dve, xt_hi_ready, b + 3)
                            nc.vector.tensor_tensor(xt_lo[:], w_half, xt_hi[:].bitcast(fp32), ALU.subtract).then_inc(xt_lo_ready, 1)
                        if on(-2) and u == 0:
                            wait(dve, rstdy, b - 1)
                            normalise(y_sb, y_sb, mvy, rsy).then_inc(lny, 1)
                        if on(2) and u in (1, 2):
                            n = u - 1
                            wait(dve, qk_p0, (b + 2) * 2 + n + 1)
                            wait(dve, qk_p2, (b + 1) * 2 + n + 1)
                            nc.vector.tensor_tensor((q_rest, k_rest)[n][:], w_half, (q_part, k_part)[n][:, 0],
                                                    ALU.subtract).then_inc(qk_rest, 1)
                        if on(-2) and u == 3:
                            wait(dve, x1_ready, b)
                            stats(x1_sb, st2, mv2, b - 2, bn2_done, stats2)
                        if on(-1) and u in (4, 6):
                            t = (u - 4) // 2
                            wait(dve, ytr_done, (b - 1) * TT + t + 1)
                            heads = w_ps[:, :].rearrange("p (h d) -> p h d", d=32)
                            nc.vector.reciprocal(inv[:, t, :], heads[:, :, HS]).then_inc(inv_ready, 1)
                            wait(dve, inv_ready, (b - 1) * TT + t + 1)
                            if t == 0:
                                wait(dve, x1_ready, b)
                            nc.vector.tensor_tensor(y_sb[:, t, :].rearrange("p (h d) -> p h d", d=HS), heads[:, :, 0:HS],
                                                    inv[:, t, :].unsqueeze(2).to_broadcast([P, HEADS, HS]),
                                                    ALU.mult).then_inc(y_ready, 1)
                            if t == 1:
                                wait(dve, y_ready, b * TT)
                                stats(y_sb, sty, mvy, b - 1, bny_done, statsy)
                        if on(1) and u == 5:
                            wait(dve, mt_done, b + 2)
                            wait(dve, m_stacked, (b + 1) * MD)
                            base = (b + 1) * 3
                            nc.vector.tensor_copy(m_part[:, 0, :], w_ps[0:HEADS, 0:T]).then_inc(m_chain, 1)
                            wait(dve, m_chain, base + 1)
                            nc.vector.tensor_tensor(m_rest[:, 0, :], w_ps[0:HEADS, 0:T], m_part[:, 0, :],
                                                    ALU.subtract).then_inc(m_chain, 1)
                            wait(dve, m_chain, base + 2)
                            nc.vector.tensor_copy(m_part[:, 1, :], m_rest[:, 0, :]).then_inc(m_chain, 1)
                            wait(dve, m_chain, base + 3)
                            nc.vector.tensor_tensor(m_part[:, 2, :], m_rest[:, 0, :], m_part[:, 1, :],
                                                    ALU.subtract).then_inc(m_ready, 1)
                        if on(-2) and u == 5:
                            wait(dve, rstd2, b - 1)
                            wait(dve, xn2_stored, 16 * (b - 1))
                            normalise(xn2_sb, x1_sb, mv2, rs2).then_inc(xn2_ready, 1)
                        if on(3) and u == 5:
                            wait(dve, x_loaded[k % 3], loads_of(b, k) * 16)
                            stats(xa[:, k % 3], st1, mv1, b + 3, bn1_done, stats1)
                        if on(3) and u == 7:
                            wait(dve, rstd1, b + 4)
                            wait(dve, xt_done, b + 3)
                            normalise(xn, xa[:, k % 3], mv1, rs1).then_inc(xn_ready, 1)

                steps_of(dve, step)

            @block.gpsimd
            def _(pool):
                def rstd(mv, rs, count, veps, done):
                    nc.gpsimd.tensor_scalar(rs[:], mv[:, :, 1], EPS, None, ALU.add).then_inc(veps, 1)
                    wait_apart(pool, veps, count + 1)
                    nc.gpsimd.tensor_tensor(rs[:], rs[:], neg_half[:], ALU.pow).then_inc(done, 1)

                pool.sem_inc(x1_ready, 1)
                pool.sem_inc(x1_stored, 16)
                pool.sem_inc(xn2_stored, 16)

                def step(b, k):
                    on = present(b)
                    if on(-2):
                        wait_apart(pool, lny, b - 1)
                        wait_apart(pool, xr_loaded, 16 * (b - 1))
                        wait_apart(pool, x1_stored, 16 * (b - 1))
                        wait_apart(pool, xn2_stored, 16 * (b - 1))
                        nc.gpsimd.tensor_tensor(x1_sb[:], y_sb[:], xr[:], ALU.add).then_inc(x1_ready, 1)
                    if on(2):
                        for n, (part, rest, stacked) in enumerate(((q_part, q_rest, q_stacked), (k_part, k_rest, k_stacked))):
                            wait_apart(pool, qk_p1, (b + 2) * 2 + n + 1)
                            nc.gpsimd.tensor_tensor(part[:, 2], rest[:], part[:, 1], ALU.subtract).then_inc(qk_p2, 1)
                    if on(-2):
                        wait_apart(pool, stats2, (b - 1) * TT)
                        rstd(mv2, rs2, b - 2, veps2, rstd2)
                    if on(3):
                        wait_apart(pool, stats1, (b + 4) * TT)
                        rstd(mv1, rs1, b + 3, veps1, rstd1)
                    if on(-1):
                        wait_apart(pool, statsy, b * TT)
                        rstd(mvy, rsy, b - 1, vepsy, rstdy)

                steps_of(pool, step)

        f_shared = sb("f_shared", [P, TILES, C])
        at_f = sb("at_f", [P, TILES, 2])
        block_tokens = sb("block_tokens", [P, BLOCKS], u32)
        block_expert = sb("block_expert", [P, BLOCKS], i32)
        dest_rows = sb("dest_rows", [P, TILES, 2], u32)

        def experts_pass(c, name, n_blocks, shared):
            RING = 4

            def sb3(nm, shape, dt=fp32):
                return c.enter_context(nc.sbuf_tensor(f"{name}_{nm}", shape, dt))

            def sem3(nm):
                return c.enter_context(nc.semaphore(f"{name}_{nm}"))

            tok = sb3("tok", [P, RING, C])
            et_hi = sb3("et_hi", [P, 2, CT, P], f32r)
            et_lo = sb3("et_lo", [P, 2, CT, P], f32r)
            th = sb3("th", [P, 2, I])
            ga = sb3("ga", [P, 2, I])
            hid = sb3("hid", [P, 2, I])
            ht_hi = sb3("ht_hi", [P, 2, P], f32r)
            ht_lo = sb3("ht_lo", [P, 2, P], f32r)
            lg = sb3("lg", [P, RING, 8])
            top8 = sb3("top8", [P, RING, 8])
            top_at = sb3("top_at", [P, RING, 8], u32)
            half_p = sb3("half_p", [P, RING, 2])
            o_sb = sb3("o_sb", [P, 2, C])
            et_ps = c.enter_context(nc.psum_tensor(f"{name}_et_ps", [P, 512], fp32))
            ht_ps = c.enter_context(nc.psum_tensor(f"{name}_ht_ps", [P, 512], fp32))
            gu_ps = [c.enter_context(nc.psum_tensor(f"{name}_gu_ps{n}", [P, 512], fp32)) for n in range(RING)]
            f_ps = [c.enter_context(nc.psum_tensor(f"{name}_f_ps{n}", [P, 512], fp32)) for n in range(2)]
            loaded = [sem3(f"loaded{n}") for n in range(RING)]
            et_done, et_hi_ready, et_lo_ready = sem3("et_done"), sem3("et_hi_ready"), sem3("et_lo_ready")
            gu_done, lg_ready, max_ready, at_ready, top_ready = (
                sem3(n) for n in ("gu_done", "lg_ready", "max_ready", "at_ready", "top_ready"))
            lg1_ready, p_half_ready, p_ready2 = sem3("lg1_ready"), sem3("p_half_ready"), sem3("p_ready2")
            th_ready, ga_ready, h_ready = sem3("th_ready"), sem3("ga_ready"), sem3("h_ready")
            ht_done, ht_hi_ready, ht_lo_ready = sem3("ht_done"), sem3("ht_hi_ready"), sem3("ht_lo_ready")
            dn_done = sem3("dn_done")
            f_ready = sem3("f_ready")
            o_stored = [sem3(f"o_stored{n}") for n in range(2)]

            first, last = 2, n_blocks - 3
            assert (last - first + 1) % RING == 0

            def steps3(eng, step):
                for m in range(-2, first):
                    step(m, m, None)
                with eng.Fori(0, (last - first + 1) // RING) as turn:
                    for n in range(RING):
                        step(turn * RING + (first + n), first + n, turn)
                for m in range(last + 1, n_blocks + 2):
                    step(m, m, None)

            def present3(m):
                return lambda lag: not isinstance(m, int) or 0 <= m + lag < n_blocks

            block = c.enter_context(nc.Block())

            @block.sync
            def _(sp):
                for n in range(2):
                    sp.sem_inc(o_stored[n], 16)

                def step(m, k, turn):
                    on = present3(m)
                    if shared and on(2):
                        wait_apart(sp, et_done, m - 1)
                        sp.dma_start(tok[:, (k + 2) % RING], xn2_tile[m + 2]).then_inc(loaded[(k + 2) % RING], 16)
                    if not shared and on(-2):
                        wait_apart(sp, f_ready, m + 1)
                        sp.dma_start(o_dram[m - 2], o_sb[:, k % 2]).then_inc(o_stored[k % 2], 16)

                steps3(sp, step)
                if not shared:
                    for n in range(2):
                        sp.wait_ge(o_stored[n], 16 * (n_blocks // 2 + 1))

            @block.gpsimd
            def _(pool):
                if not shared:
                    for n in range(n_blocks):
                        if n >= RING:
                            pool.wait_ge(et_done, n - RING + 1)
                        nc.gpsimd.indirect_dma_start(
                            out=tok[:, n % RING], out_offset=None, in_=xn2_rows,
                            in_offset=bass.IndirectOffsetOnAxis(ap=block_tokens[:, n:n + 1], axis=0),
                        ).then_inc(loaded[n % RING], 16)

            @block.tensor
            def _(pe):
                pe.sem_inc(f_ready, 2)

                def step(m, k, turn):
                    on = present3(m)
                    if on(2):
                        wait(pe, loaded[(k + 2) % RING], 16 * ((k + 2) // RING + 1 + (turn if turn is not None else 0)))
                        wait(pe, et_lo_ready, m + 2)
                        for ct in range(CT):
                            last = nc.tensor.transpose(et_ps[:, ct * P:(ct + 1) * P],
                                                       tok[:, (k + 2) % RING, ct * P:(ct + 1) * P], ident[:])
                        last.then_inc(et_done, 1)
                    if on(-2):
                        if shared:
                            w_hi, w_lo = dn_hi[:, SHARED, :], dn_lo[:, SHARED, :]
                        else:
                            e = pe.value_load(block_expert[0:1, (bass.ds(m - 2, 1) if turn is not None else slice(m - 2, m - 1))],
                                              min_val=0, max_val=EXPERTS - 1)
                            w_hi, w_lo = (w[:, bass.ds(e, 1), :].rearrange("p a c -> p (a c)") for w in (dn_hi, dn_lo))
                        wait(pe, ht_lo_ready, m - 1)
                        wait(pe, f_ready, m - 1)
                        for j, (part, w) in enumerate(((ht_hi, w_hi), (ht_hi, w_lo), (ht_lo, w_hi))):
                            last = nc.tensor.matmul(f_ps[k % 2][:, 0:C], part[:, k % 2, :], w, start=(j == 0), stop=(j == 2))
                        last.then_inc(dn_done, 1)
                    if on(-1):
                        wait(pe, h_ready, m)
                        if not on(-2):
                            wait(pe, ht_lo_ready, m - 1)
                        nc.tensor.transpose(ht_ps[:, 0:P], hid[:, (k - 1) % 2, :], ident[:]).then_inc(ht_done, 1)
                    if on(1):
                        if not shared:
                            e = pe.value_load(block_expert[0:1, (bass.ds(m + 1, 1) if turn is not None else slice(m + 1, m + 2))],
                                              min_val=0, max_val=EXPERTS - 1)
                        wait(pe, et_lo_ready, m + 2)
                        j = 0
                        for part, w in ((et_hi, gu_hi), (et_hi, gu_lo), (et_lo, gu_hi)):
                            for ct in range(CT):
                                rhs = w[:, SHARED, ct, :] if shared else \
                                    w[:, bass.ds(e, 1), ct, :].rearrange("p a n -> p (a n)")
                                last = nc.tensor.matmul(gu_ps[(k + 1) % RING][:, 0:GW], part[:, (k + 1) % 2, ct, :], rhs,
                                                        start=(j == 0), stop=(j == 3 * CT - 1))
                                j += 1
                        last.then_inc(gu_done, 1)

                steps3(pe, step)

            @block.scalar
            def _(act):
                def step(m, k, turn):
                    on = present3(m)
                    if on(2):
                        wait(act, et_done, m + 3)
                        wait(act, gu_done, m + 1)
                        nc.scalar.copy(et_hi[:, k % 2], et_ps[:, 0:C].rearrange("p (c n) -> p c n", c=CT)).then_inc(et_hi_ready, 1)
                    if on(-2):
                        wait(act, dn_done, m - 1)
                        if shared:
                            dst = f_shared[:, bass.ds(m - 2, 1), :].rearrange("p a c -> p (a c)") if turn is not None \
                                else f_shared[:, m - 2, :]
                        else:
                            wait(act, o_stored[k % 2], 16 * (k // 2 + (turn * (RING // 2) if turn is not None else 0)))
                            dst = o_sb[:, k % 2]
                        nc.scalar.copy(dst, f_ps[k % 2][:, 0:C]).then_inc(f_ready, 1)
                    if on(-1):
                        wait(act, ht_done, m)
                        nc.scalar.copy(ht_hi[:, (k - 1) % 2], ht_ps[:, 0:P]).then_inc(ht_hi_ready, 1)
                    if on(0):
                        if shared:
                            wait(act, gu_done, m + 1)
                        else:
                            wait(act, p_ready2, m + 1)
                        wait(act, ga_ready, m - 1)
                        nc.scalar.activation(th[:, k % 2], gu_ps[k % RING][:, 0:I], ACT.Tanh,
                                             scale=0.5 if shared else half_p[:, k % RING, 0:1]).then_inc(th_ready, 1)
                    if on(1):
                        wait(act, gu_done, m + 2)
                        if shared:
                            nc.scalar.copy(lg[:, (k + 1) % RING], gu_ps[(k + 1) % RING][:, GU:GU + 8]).then_inc(lg_ready, 1)
                        else:
                            nc.scalar.activation(lg[:, (k + 1) % RING, 0:1], gu_ps[(k + 1) % RING][:, GU:GU + 1],
                                                 ACT.Exp, scale=-1.0).then_inc(lg_ready, 1)

                steps3(act, step)

            @block.vector
            def _(dve):
                def step(m, k, turn):
                    on = present3(m)
                    if on(2):
                        wait(dve, et_hi_ready, m + 3)
                        nc.vector.tensor_tensor(et_lo[:, k % 2], et_ps[:, 0:C].rearrange("p (c n) -> p c n", c=CT),
                                                et_hi[:, k % 2].bitcast(fp32), ALU.subtract).then_inc(et_lo_ready, 1)
                    if on(-1):
                        wait(dve, ht_hi_ready, m)
                        nc.vector.tensor_tensor(ht_lo[:, (k - 1) % 2], ht_ps[:, 0:P], ht_hi[:, (k - 1) % 2].bitcast(fp32),
                                                ALU.subtract).then_inc(ht_lo_ready, 1)
                    if on(0):
                        wait(dve, th_ready, m + 1)
                        nc.vector.scalar_tensor_tensor(out=ga[:, k % 2], in0=th[:, k % 2], scalar=1.0,
                                                       in1=gu_ps[k % RING][:, 0:I], op0=ALU.add, op1=ALU.mult).then_inc(ga_ready, 1)
                        wait(dve, ht_done, m - 1)
                        wait(dve, ga_ready, m + 1)
                        if shared:
                            nc.vector.tensor_tensor(hid[:, k % 2], ga[:, k % 2], gu_ps[k % RING][:, I:GU], ALU.mult).then_inc(h_ready, 1)
                        else:
                            nc.vector.scalar_tensor_tensor(out=hid[:, k % 2], in0=ga[:, k % 2], scalar=half_p[:, k % RING, 1:2],
                                                           in1=gu_ps[k % RING][:, I:GU], op0=ALU.mult, op1=ALU.mult).then_inc(h_ready, 1)
                    if on(1):
                        r = (k + 1) % RING
                        if shared:
                            wait_apart(dve, lg_ready, m + 2)
                            nc.vector.max(top8[:, r], lg[:, r]).then_inc(max_ready, 1)
                            wait_apart(dve, max_ready, m + 2)
                            nc.vector.max_index(top_at[:, r], top8[:, r], lg[:, r]).then_inc(at_ready, 1)
                            wait(dve, at_ready, m + 2)
                            dst = at_f[:, bass.ds(m + 1, 1), :].rearrange("p a c -> p (a c)") if turn is not None else at_f[:, m + 1, :]
                            nc.vector.tensor_copy(dst, top_at[:, r, 0:2]).then_inc(top_ready, 1)
                        else:
                            wait(dve, lg_ready, m + 2)
                            nc.vector.tensor_scalar(lg[:, r, 1:2], lg[:, r, 0:1], 2.0, 2.0, ALU.mult, ALU.add).then_inc(lg1_ready, 1)
                            wait(dve, lg1_ready, m + 2)
                            nc.vector.reciprocal(half_p[:, r, 0:1], lg[:, r, 1:2]).then_inc(p_half_ready, 1)
                            wait(dve, p_half_ready, m + 2)
                            nc.vector.tensor_scalar(half_p[:, r, 1:2], half_p[:, r, 0:1], half_p[:, r, 0:1], 4.0,
                                                    ALU.mult, ALU.mult).then_inc(p_ready2, 1)

                steps3(dve, step)

        with ExitStack() as c3:
            experts_pass(c3, "sh", TILES, True)

        with ExitStack() as c5:
            def sb5(nm, shape, dt=fp32):
                return c5.enter_context(nc.sbuf_tensor(nm, shape, dt))

            cols8 = sb5("cols8", [P, EXPERTS])
            colsb = sb5("colsb", [P, BLOCKS], f16)
            colsf = sb5("colsf", [P, BLOCKS])
            colsp = sb5("colsp", [P, P], f16)
            tokid = sb5("tokid", [P, TILES])
            before = sb5("before", [P, P], bf16)
            ones = sb5("ones", [P, P], bf16)
            keep = sb5("keep", [P, EXPERTS, TILES])
            hot = sb5("hot", [P, 2, TILES, EXPERTS])
            hots = sb5("hots", [P, TILES, EXPERTS], bf16)
            total = sb5("total", [P, EXPERTS, TILES])
            upto = sb5("upto", [P, EXPERTS, TILES])
            cnt = sb5("cnt", [P, EXPERTS])
            cnt_i = sb5("cnt_i", [P, EXPERTS], i32)
            nblk = sb5("nblk", [P, EXPERTS])
            ends = sb5("ends", [P, EXPERTS])
            starts = sb5("starts", [P, EXPERTS])
            place = sb5("place", [P, TILES, EXPERTS])
            dest = sb5("dest", [P, 2, TILES])
            dest_i = sb5("dest_i", [P, 2, TILES], i32)
            part_i = sb5("part_i", [P, 2, 2, TILES], i32)
            part_f = sb5("part_f", [P, 2, 2, TILES])
            over = sb5("over", [P, BLOCKS, EXPERTS])
            bexp = sb5("bexp", [P, BLOCKS])
            RB = 4
            in_block = sb5("in_block", [P, RB, P], f16)
            of_block = sb5("of_block", [P, RB, BLOCKS], f16)
            rank_ps = c5.enter_context(nc.psum_tensor("rank_ps", [P, 512], fp32))
            total_ps = c5.enter_context(nc.psum_tensor("total_ps", [P, 512], fp32))
            ids_ps = c5.enter_context(nc.psum_tensor("ids_ps", [P, 512], fp32))
            iotas, hots_ready, ranks_done, hot_made, ids_done, r_chain = (
                c5.enter_context(nc.semaphore(n)) for n in ("iotas", "hots_ready", "ranks_done", "hot_made", "ids_done", "r_chain"))
            block = c5.enter_context(nc.Block())

            @block.gpsimd
            def _(pool):
                imprecise = dict(allow_small_or_imprecise_dtypes=True)
                nc.gpsimd.iota(cols8[:], pattern=[[1, EXPERTS]], base=0, channel_multiplier=0, **imprecise).then_inc(iotas, 1)
                nc.gpsimd.iota(colsf[:], pattern=[[1, BLOCKS]], base=0, channel_multiplier=0, **imprecise).then_inc(iotas, 1)
                nc.gpsimd.iota(colsb[:], pattern=[[1, BLOCKS]], base=0, channel_multiplier=0, **imprecise).then_inc(iotas, 1)
                nc.gpsimd.iota(colsp[:], pattern=[[1, P]], base=0, channel_multiplier=0, **imprecise).then_inc(iotas, 1)
                nc.gpsimd.iota(tokid[:], pattern=[[P, TILES]], base=-TOKENS // 2, channel_multiplier=1, **imprecise).then_inc(iotas, 1)
                nc.gpsimd.memset(ones[:], 1.0).then_inc(iotas, 1)
                nc.gpsimd.memset(before[:], 1.0).then_inc(iotas, 1)
                nc.gpsimd.memset(keep[:], 1.0).then_inc(iotas, 1)
                pool.wait_ge(iotas, 8)
                nc.gpsimd.memset(keep[:, :, 0:1], 0.0).then_inc(iotas, 1)
                nc.gpsimd.affine_select(out=before[:], in_=before[:], compare_op=ALU.is_gt, fill=0.0, base=0,
                                        pattern=[[1, P]], channel_multiplier=-1).then_inc(iotas, 1)

            @block.tensor
            def _(pe):
                pe.wait_ge(iotas, 10)
                pe.wait_ge(hots_ready, 1)
                flat = hots[:, :, :].rearrange("p t e -> p (t e)")
                nc.tensor.matmul(rank_ps[:, 0:TILES * EXPERTS], before[:], flat, start=True, stop=True).then_inc(ranks_done, 1)
                nc.tensor.matmul(total_ps[:, 0:TILES * EXPERTS], ones[:], flat, start=True, stop=True).then_inc(ranks_done, 1)
                for n in range(2 * TILES):
                    pe.wait_ge(hot_made, n + 1)
                    nc.tensor.matmul(ids_ps[:, 0:BLOCKS], in_block[:, n % RB, :], of_block[:, n % RB, :],
                                     start=(n == 0), stop=(n == 2 * TILES - 1)).then_inc(ids_done, 1)

            @block.vector
            def _(dve):
                steps = [0]

                def step(ins):
                    steps[0] += 1
                    ins.then_inc(r_chain, 1)
                    dve.wait_ge(r_chain, steps[0])

                te = [P, TILES, EXPERTS]
                dve.wait_ge(iotas, 10)
                for k in range(2):
                    step(nc.vector.tensor_tensor(hot[:, k], cols8[:].unsqueeze(1).to_broadcast(te),
                                                 at_f[:, :, k:k + 1].to_broadcast(te), ALU.is_equal))
                nc.vector.tensor_tensor(hots[:], hot[:, 0], hot[:, 1], ALU.add).then_inc(hots_ready, 1)
                dve.wait_ge(ranks_done, 2)
                step(nc.vector.tensor_copy(total[:], total_ps[:, 0:TILES * EXPERTS].rearrange("p (t e) -> p e t", e=EXPERTS)))
                step(nc.vector.tensor_tensor_scan(
                    out=upto[:].rearrange("p e t -> p (e t)"), data0=keep[:].rearrange("p e t -> p (e t)"),
                    data1=total[:].rearrange("p e t -> p (e t)"), initial=0.0, op0=ALU.mult, op1=ALU.add))
                step(nc.vector.tensor_scalar(cnt[:], upto[:, :, TILES - 1], float(P - 1), None, ALU.add))
                step(nc.vector.tensor_copy(cnt_i[:], cnt[:]))
                step(nc.vector.tensor_scalar(cnt_i[:], cnt_i[:], LOG_P, None, ALU.logical_shift_right))
                step(nc.vector.tensor_copy(nblk[:], cnt_i[:]))
                step(nc.vector.tensor_tensor_scan(out=ends[:], data0=keep[:, 0, 1:1 + EXPERTS], data1=nblk[:],
                                                  initial=0.0, op0=ALU.mult, op1=ALU.add))
                step(nc.vector.tensor_tensor(starts[:], ends[:], nblk[:], ALU.subtract))
                step(nc.vector.tensor_tensor(upto[:], upto[:], total[:], ALU.subtract))
                step(nc.vector.scalar_tensor_tensor(out=upto[:], in0=starts[:].unsqueeze(2).to_broadcast([P, EXPERTS, TILES]),
                                                    scalar=float(P), in1=upto[:], op0=ALU.mult, op1=ALU.add))
                step(nc.vector.tensor_tensor(place[:], rank_ps[:, 0:TILES * EXPERTS].rearrange("p (t e) -> p t e", e=EXPERTS),
                                             upto[:].rearrange("p e t -> p t e"), ALU.add))
                for k in range(2):
                    step(nc.vector.tensor_tensor(hot[:, k], hot[:, k], place[:], ALU.mult))
                step(nc.vector.tensor_reduce(dest[:], hot[:], AX.X, ALU.add))
                step(nc.vector.tensor_copy(dest_i[:], dest[:]))
                step(nc.vector.tensor_scalar(part_i[:, 0], dest_i[:], P - 1, None, ALU.bitwise_and))
                step(nc.vector.tensor_scalar(part_i[:, 1], dest_i[:], LOG_P, None, ALU.logical_shift_right))
                step(nc.vector.tensor_copy(part_f[:], part_i[:]))
                for n in range(2 * TILES):
                    t, k = n // 2, n % 2
                    if n >= RB:
                        dve.wait_ge(ids_done, n - RB + 1)
                    nc.vector.tensor_scalar(in_block[:, n % RB, :], colsp[:], part_f[:, 0, k, t:t + 1], None, ALU.is_equal)
                    nc.vector.tensor_scalar(of_block[:, n % RB, :], colsb[:], part_f[:, 1, k, t:t + 1], tokid[:, t:t + 1],
                                            ALU.is_equal, ALU.mult).then_inc(hot_made, 1)
                step(nc.vector.tensor_tensor(over[:], colsf[:].unsqueeze(2).to_broadcast([P, BLOCKS, EXPERTS]),
                                             ends[:].unsqueeze(1).to_broadcast([P, BLOCKS, EXPERTS]), ALU.is_ge))
                step(nc.vector.tensor_reduce(bexp[:], over[:], AX.X, ALU.add))
                step(nc.vector.tensor_scalar(bexp[:], bexp[:], float(EXPERTS - 1), None, ALU.min))
                step(nc.vector.tensor_copy(block_expert[:], bexp[:]))
                step(nc.vector.tensor_copy(dest_rows[:].rearrange("p t k -> p k t"), dest_i[:]))
                dve.wait_ge(ids_done, 2 * TILES)
                step(nc.vector.tensor_scalar(bexp[:], ids_ps[:, 0:BLOCKS], float(TOKENS // 2), None, ALU.add))
                step(nc.vector.tensor_copy(block_tokens[:], bexp[:]))

        with ExitStack() as c3:
            experts_pass(c3, "ex", BLOCKS, False)

        with ExitStack() as c4:
            def sb4(nm, shape, dt=fp32):
                return c4.enter_context(nc.sbuf_tensor(nm, shape, dt))

            def sem4(nm):
                return c4.enter_context(nc.semaphore(nm))

            Q = 4
            g_sb = sb4("g_sb", [P, 2, Q, 2, C])
            x1_in = sb4("x1_in", [P, 2, Q, C])
            f_sb = sb4("f_sb", [P, 2, Q, C])
            stf = sb4("stf", [P, Q, 6])
            mvf = sb4("mvf", [P, 2, Q, 2])
            rsf = sb4("rsf", [P, 2, Q])
            halves = sb4("halves", [P, Q])
            fin = sb4("fin", [P, 2, Q, C])
            g_loaded = [sem4(f"g_loaded{n}") for n in range(2)]
            x1_loaded = [sem4(f"x1_loaded{n}") for n in range(2)]
            two_added, all_added, bnf_done, statsf, vepsf, rstdf, lnf, fin_ready, out_stored = (
                sem4(n) for n in ("two_added", "all_added", "bnf_done", "statsf", "vepsf", "rstdf", "lnf", "fin_ready", "out_stored"))
            groups = TILES // Q
            block = c4.enter_context(nc.Block())

            @block.sync
            def _(sp):
                for g in range(groups + 2):
                    if g < groups:
                        if g >= 2:
                            sp.wait_ge(fin_ready, g - 1)
                        sp.dma_start(x1_in[:, g % 2], x1_tile[g * Q:(g + 1) * Q].rearrange("t p c -> p t c")).then_inc(x1_loaded[g % 2], 16)
                    if g >= 2:
                        sp.wait_ge(fin_ready, g - 1)
                        sp.dma_start(out_tile[(g - 2) * Q:(g - 1) * Q].rearrange("t p c -> p t c"), fin[:, g % 2]).then_inc(out_stored, 16)
                        sp.wait_ge(out_stored, 16 * (g - 1))

            @block.gpsimd
            def _(pool):
                nc.gpsimd.memset(halves[:], -0.5).then_inc(vepsf, 1)
                pool.wait_ge(vepsf, 1)

                def rstd(g):
                    pool.wait_ge(statsf, Q * (g + 1))
                    nc.gpsimd.tensor_scalar(rsf[:, g % 2], mvf[:, g % 2, :, 1], EPS, None, ALU.add).then_inc(vepsf, 1)
                    pool.wait_ge(vepsf, g + 2)
                    nc.gpsimd.tensor_tensor(rsf[:, g % 2], rsf[:, g % 2], halves[:], ALU.pow).then_inc(rstdf, 1)

                for g in range(groups):
                    for q in range(Q):
                        for k in range(2):
                            if g >= 2 and q == 0 and k == 0:
                                pool.wait_ge(two_added, g - 1)
                            nc.gpsimd.indirect_dma_start(
                                out=g_sb[:, g % 2, q, k], out_offset=None, in_=o_rows,
                                in_offset=bass.IndirectOffsetOnAxis(ap=dest_rows[:, g * Q + q, k:k + 1], axis=0),
                            ).then_inc(g_loaded[g % 2], 16)
                    if g >= 1:
                        rstd(g - 1)
                rstd(groups - 1)

            @block.vector
            def _(dve):
                def finish(g):
                    dve.wait_ge(rstdf, g + 1)
                    for q in range(Q):
                        last = nc.vector.tensor_scalar(f_sb[:, g % 2, q], f_sb[:, g % 2, q], mvf[:, g % 2, q, 0:1],
                                                       rsf[:, g % 2, q:q + 1], ALU.subtract, ALU.mult)
                    last.then_inc(lnf, 1)
                    dve.wait_ge(lnf, g + 1)
                    dve.wait_ge(x1_loaded[g % 2], 16 * (g // 2 + 1))
                    if g >= 2:
                        dve.wait_ge(out_stored, 16 * (g - 1))
                    nc.vector.tensor_tensor(fin[:, g % 2], f_sb[:, g % 2], x1_in[:, g % 2], ALU.add).then_inc(fin_ready, 1)

                for g in range(groups):
                    if g >= 2:
                        dve.wait_ge(fin_ready, g - 1)
                    dve.wait_ge(g_loaded[g % 2], 16 * 2 * Q * (g // 2 + 1))
                    nc.vector.tensor_tensor(f_sb[:, g % 2], g_sb[:, g % 2, :, 0], g_sb[:, g % 2, :, 1], ALU.add).then_inc(two_added, 1)
                    dve.wait_ge(two_added, g + 1)
                    nc.vector.tensor_tensor(f_sb[:, g % 2], f_sb[:, g % 2], f_shared[:, g * Q:(g + 1) * Q], ALU.add).then_inc(all_added, 1)
                    dve.wait_ge(all_added, g + 1)
                    for q in range(Q):
                        nc.vector.bn_stats(stf[:, q], f_sb[:, g % 2, q]).then_inc(bnf_done, 1)
                    for q in range(Q):
                        dve.wait_ge(bnf_done, g * Q + q + 1)
                        nc.vector.bn_aggr(mvf[:, g % 2, q], stf[:, q]).then_inc(statsf, 1)
                    if g >= 1:
                        finish(g - 1)
                finish(groups - 1)


_INS = ["L0_attn_x", "L0_attn_Wq_w", "L0_attn_Wdkv_w", "L0_attn_Wuk_w", "L0_attn_Wuv_w", "L0_attn_Wo_w",
        "L0_ffn_router_w", "L0_ffn_gate_up_w", "L0_ffn_down_w", "L0_ffn_shared_gate_w", "L0_ffn_shared_up_w",
        "L0_ffn_shared_down_w"]


def kernel(**inputs):
    import numpy as _np
    import concourse.bacc as _bacc
    from concourse import mybir as _mybir
    from concourse.bass_utils import run_bass_kernel_spmd as _run

    nc = _bacc.Bacc("TRN2", target_bir_lowering=False, num_devices=1)
    arrays, args = {}, []
    for name in _INS:
        a = _np.ascontiguousarray(inputs[name])
        arrays[f"in_{name}_dram"] = a
        args.append(nc.dram_tensor(f"in_{name}_dram", a.shape, _mybir.dt.from_np(a.dtype), kind="ExternalInput").ap())
    shape = inputs["L0_attn_x"].shape
    args.append(nc.dram_tensor("out_dram", shape, _mybir.dt.float32, kind="ExternalOutput").ap())
    sandwich_block_kernel(nc, *args)
    r = _run(nc, [arrays], core_ids=[0])
    return r.results[0]["out_dram"]
```

```python
import concourse.bass as bass
from concourse import mybir
from contextlib import ExitStack


def sandwich_block_kernel(
    nc: bass.Bass,
    x: bass.AP,
    w_q: bass.AP,
    w_dkv: bass.AP,
    w_uk: bass.AP,
    w_uv: bass.AP,
    w_o: bass.AP,
    router_w: bass.AP,
    gate_up_w: bass.AP,
    down_w: bass.AP,
    shared_gate_w: bass.AP,
    shared_up_w: bass.AP,
    shared_down_w: bass.AP,
    out: bass.AP,
):
    fp32 = mybir.dt.float32
    f32r = mybir.dt.float32r
    bf16 = mybir.dt.bfloat16
    ALU = mybir.AluOpType
    ACT = mybir.ActivationFunctionType
    AX = mybir.AxisListType
    f16 = mybir.dt.float16
    u32 = mybir.dt.uint32
    i32 = mybir.dt.int32

    P = 128
    BATCH, T, C = x.shape
    NL = w_dkv.shape[0]
    HEADS = 16
    HS = C // HEADS
    TT = T // P
    CT = C // P
    HM = HEADS // CT
    EXPERTS, _, GU = gate_up_w.shape
    I = GU // 2
    TILES = BATCH * TT
    EPS = 1e-5
    MASK = -1e30
    SCALE = float(HS) ** -0.5
    SHARED = EXPERTS
    NE = EXPERTS + 1
    GW = GU + EXPERTS
    TOKENS = BATCH * T
    LOG_P = P.bit_length() - 1
    BLOCKS = 2 * TOKENS // P + EXPERTS - 1
    RING = 4
    TURN = 3 * RING

    Q_PARTS = [0, 0, 1, 1, 0, 2]
    K_PARTS = [0, 1, 0, 1, 2, 0]
    SROWS = HS * len(Q_PARTS)
    MROWS = 2
    UNIT = 2 * T + 2 * P
    UNITS = HEADS // 2
    GROUPS = HEADS // 4
    FILLS = 3 * GROUPS

    x_tok = x.rearrange("b (t p) c -> b p t c", p=P)
    x1_dram = nc.dram_tensor("x1_scratch", (BATCH, T, C), fp32, kind="Internal").ap()
    xn2_dram = nc.dram_tensor("xn2_scratch", (BATCH, T, C), fp32, kind="Internal").ap()
    x1_tok = x1_dram.rearrange("b (t p) c -> b p t c", p=P)
    xn2_tok = xn2_dram.rearrange("b (t p) c -> b p t c", p=P)
    x1_tile = x1_dram.rearrange("b (t p) c -> (b t) p c", p=P)
    xn2_tile = xn2_dram.rearrange("b (t p) c -> (b t) p c", p=P)
    xn2_rows = xn2_dram.rearrange("b t c -> (b t) c")
    o_rows = nc.dram_tensor("o_scratch", (2 * TOKENS + BLOCKS * P, C), fp32, kind="Internal").ap()
    o_choice = [o_rows[k * TOKENS:(k + 1) * TOKENS, :].rearrange("(t p) c -> t p c", p=P) for k in range(2)]
    out_tile = out.rearrange("b (t p) c -> (b t) p c", p=P)

    ctx = ExitStack()
    with ctx:
        def sb(name, shape, dt=fp32):
            return ctx.enter_context(nc.sbuf_tensor(name, shape, dt))

        def ps(name, shape):
            return ctx.enter_context(nc.psum_tensor(name, shape, fp32))

        def sem(name):
            return ctx.enter_context(nc.semaphore(name))

        ident = sb("ident", [P, P])
        identb = sb("identb", [P, P], bf16)
        maskq = sb("maskq", [P, P], bf16)
        maskk = sb("maskk", [P, P], bf16)
        neg_half = sb("neg_half", [P, TT])
        gu_hi = sb("gu_hi", [P, NE, CT, GW], f32r)
        gu_lo = sb("gu_lo", [P, NE, CT, GW], f32r)
        dn_hi = sb("dn_hi", [P, NE, C], f32r)
        dn_lo = sb("dn_lo", [P, NE, C], f32r)

        ctx1 = ExitStack()

        def sb1(name, shape, dt=fp32):
            return ctx1.enter_context(nc.sbuf_tensor(name, shape, dt))

        wq_hi, wq_lo, wk_hi, wk_lo, wv_hi, wv_lo = (
            sb1(n, [P, CT, C], f32r) for n in ("wq_hi", "wq_lo", "wk_hi", "wk_lo", "wv_hi", "wv_lo"))
        gu_raw = sb1("gu_raw", [P, NE, CT, GU])
        r_raw = sb1("r_raw", [P, CT, EXPERTS])
        xa = sb1("xa", [P, 3, TT, C])
        xr = sb1("xr", [P, TT, C])
        xn = sb1("xn", [P, TT, C])
        st1 = sb1("st1", [P, TT, 6])
        mv1 = sb1("mv1", [P, TT, 2])
        rs1 = sb1("rs1", [P, TT])
        xt_hi = sb1("xt_hi", [P, CT, T], f32r)
        xt_lo = sb1("xt_lo", [P, CT, T], f32r)
        q_part = sb1("q_part", [P, 3, CT, T], bf16)
        k_part = sb1("k_part", [P, 3, CT, T], bf16)
        q_rest = sb1("q_rest", [P, CT, T])
        k_rest = sb1("k_rest", [P, CT, T])
        q_stack = sb1("q_stack", [P, 3, HEADS, T], bf16)
        k_stack = sb1("k_stack", [P, 3, HEADS, T], bf16)
        v_sb = sb1("v_sb", [P, 3, TT, HEADS, 32])
        rowmax = sb1("rowmax", [P, TT, HEADS])
        m_part = sb1("m_part", [HEADS, MROWS, T], bf16)
        prob_t = sb1("prob_t", [P, 4, UNIT])
        yt_sb = sb1("yt_sb", [P, 3, GROUPS, T])
        inv = sb1("inv", [P, TT, HEADS])
        y_sb = sb1("y_sb", [P, TT, C])
        sty = sb1("sty", [P, TT, 6])
        mvy = sb1("mvy", [P, TT, 2])
        rsy = sb1("rsy", [P, TT])
        x1_sb = sb1("x1_sb", [P, TT, C])
        st2 = sb1("st2", [P, TT, 6])
        mv2 = sb1("mv2", [P, TT, 2])
        rs2 = sb1("rs2", [P, TT])
        xn2_sb = sb1("xn2_sb", [P, TT, C])

        dn_raw = yt_sb[:, :, :, :].rearrange("p a b c -> p (a b c)")[:, 0:NE * C].rearrange("p (e c) -> p e c", e=NE)

        consts_ready = sem("consts_ready")
        neg_half_ready = sem("neg_half_ready")
        w_loaded = sem("w_loaded")
        prep_pe = sem("prep_pe")
        prep_copied = sem("prep_copied")
        ex_loaded = sem("ex_loaded")
        ex_upper = sem("ex_upper")
        ex_split = sem("ex_split")
        prep_chain = sem("prep_chain")
        x_loaded = [sem(f"x_loaded{n}") for n in range(3)]
        xr_loaded = sem("xr_loaded")
        bn1_done = sem("bn1_done")
        stats1 = sem("stats1")
        veps1 = sem("veps1")
        rstd1 = sem("rstd1")
        xn_ready = sem("xn_ready")
        xt_done = sem("xt_done")
        xt_hi_ready = sem("xt_hi_ready")
        xt_lo_ready = sem("xt_lo_ready")
        qk_done = sem("qk_done")
        qk_p0 = sem("qk_p0")
        qk_rest = sem("qk_rest")
        qk_p1 = sem("qk_p1")
        qk_p2 = sem("qk_p2")
        v_done = sem("v_done")
        v_ready = sem("v_ready")
        q_stacked = sem("q_stacked")
        k_stacked = sem("k_stacked")
        m_stacked = sem("m_stacked")
        s_done = sem("s_done")
        s_max = sem("s_max")
        mt_done = sem("mt_done")
        m_chain = sem("m_chain")
        m_ready = sem("m_ready")
        st_done = sem("st_done")
        p_ready = sem("p_ready")
        pv_done = sem("pv_done")
        yt_ready = sem("yt_ready")
        ytr_done = sem("ytr_done")
        inv_ready = sem("inv_ready")
        y_ready = sem("y_ready")
        bny_done = sem("bny_done")
        statsy = sem("statsy")
        vepsy = sem("vepsy")
        rstdy = sem("rstdy")
        lny = sem("lny")
        x1_ready = sem("x1_ready")
        bn2_done = sem("bn2_done")
        stats2 = sem("stats2")
        veps2 = sem("veps2")
        rstd2 = sem("rstd2")
        x1_stored = sem("x1_stored")
        xn2_stored = sem("xn2_stored")
        xn2_ready = sem("xn2_ready")

        third_stacked = sem("third_stacked")
        QD = 16 * (len(Q_PARTS) - 1)
        MD = 16 * MROWS

        with ExitStack() as c0:
            def sb0(name, shape, dt=fp32):
                return c0.enter_context(nc.sbuf_tensor(name, shape, dt))

            raws = prob_t[:, :, :].rearrange("p a b -> p (a b)")
            at = [0]

            def raw_view(rows, *dims):
                n = dims[0] * dims[-1] if len(dims) == 2 else dims[0]
                at[0] += n
                v = raws[0:rows, at[0] - n:at[0]]
                return v.rearrange("p (t n) -> p t n", t=dims[0]) if len(dims) == 2 else v

            wq_raw = raw_view(P, CT, C)
            wo_raw = raw_view(P, CT, C)
            wuk_raw = raw_view(P, CT, NL)
            wuv_raw = raw_view(P, CT, NL)
            wo_t = raw_view(P, CT, C)
            wdkv_raw = raw_view(NL, C)
            keff_t = raw_view(NL, C)
            veff = raw_view(NL, C)
            pt = [c0.enter_context(nc.psum_tensor(f"pt{n}", [P, 512], fp32)) for n in range(6)]
            block = c0.enter_context(nc.Block())

            @block.sync
            def _(sp):
                for dst, src in ((wq_raw, w_q), (wo_raw, w_o), (wuk_raw, w_uk), (wuv_raw, w_uv)):
                    sp.dma_start(dst[:], src.rearrange("(t p) n -> p t n", p=P)).then_inc(w_loaded, 16)
                sp.dma_start(wdkv_raw[:], w_dkv).then_inc(w_loaded, 16)
                sp.dma_start(xa[:, 0], x_tok[0]).then_inc(x_loaded[0], 16)
                for dst, src in ((r_raw[:], router_w), (gu_raw[:, SHARED, :, 0:I], shared_gate_w),
                                 (gu_raw[:, SHARED, :, I:GU], shared_up_w)):
                    sp.dma_start(dst, src.rearrange("(t p) n -> p t n", p=P)).then_inc(ex_loaded, 16)
                for ct in range(CT):
                    sp.dma_start(gu_raw[:, 0:EXPERTS, ct, :],
                                 gate_up_w[:, ct * P:(ct + 1) * P, :].rearrange("e p n -> p e n")).then_inc(ex_loaded, 16)
                sp.dma_start(dn_raw[:, 0:EXPERTS, :], down_w.rearrange("e i c -> i e c")).then_inc(ex_loaded, 16)
                sp.dma_start(dn_raw[:, SHARED, :], shared_down_w).then_inc(ex_loaded, 16)

            @block.gpsimd
            def _(pool):
                nc.gpsimd.memset(ident[:], 0.0).then_inc(consts_ready, 1)
                nc.gpsimd.memset(neg_half[:], -0.5).then_inc(neg_half_ready, 1)
                pool.wait_ge(consts_ready, 1)
                nc.gpsimd.affine_select(out=ident[:], in_=ident[:], compare_op=ALU.not_equal, fill=1.0, base=0,
                                        pattern=[[-1, P]], channel_multiplier=1).then_inc(consts_ready, 1)
                nc.gpsimd.memset(maskq[:], 0.0).then_inc(consts_ready, 1)
                nc.gpsimd.memset(maskk[:], 0.0).then_inc(consts_ready, 1)
                nc.gpsimd.memset(v_sb[:], 0.0).then_inc(consts_ready, 1)
                for w in (gu_hi, gu_lo):
                    nc.gpsimd.memset(w[:, 0:EXPERTS, :, GU + 1:GW].bitcast(fp32), 0.0).then_inc(consts_ready, 1)
                pool.wait_ge(consts_ready, 7)
                nc.gpsimd.memset(v_sb[:, :, :, :, HS:HS + 1], 1.0).then_inc(consts_ready, 1)
                nc.gpsimd.affine_select(out=maskq[:], in_=maskq[:], compare_op=ALU.is_ge, fill=MASK, base=0,
                                        pattern=[[-1, P]], channel_multiplier=1).then_inc(consts_ready, 1)
                nc.gpsimd.affine_select(out=maskk[:], in_=maskk[:], compare_op=ALU.is_ge, fill=MASK, base=0,
                                        pattern=[[1, P]], channel_multiplier=-1).then_inc(consts_ready, 1)
                nc.gpsimd.tensor_copy(identb[:], ident[:]).then_inc(consts_ready, 1)
                pool.wait_ge(consts_ready, 11)
                for n in (1, 2):
                    nc.gpsimd.memset(k_stack[SROWS:P, n], -1.0).then_inc(consts_ready, 1)
                    if n == 1:
                        pool.wait_ge(stats1, TT)
                        pool.wait_ge(neg_half_ready, 1)
                        pool.wait_ge(consts_ready, 12)
                        nc.gpsimd.tensor_scalar(rs1[:], mv1[:, :, 1], EPS, None, ALU.add).then_inc(veps1, 1)
                        pool.wait_ge(veps1, 1)
                        nc.gpsimd.tensor_tensor(rs1[:], rs1[:], neg_half[:], ALU.pow).then_inc(rstd1, 1)
                        pool.wait_ge(rstd1, 1)

            @block.tensor
            def _(pe):
                pe.wait_ge(consts_ready, 2)
                pe.wait_ge(w_loaded, 16 * 5)
                for n, raw in enumerate((wq_raw, wo_raw)):
                    for ct in range(CT):
                        for rt in range(CT):
                            last = nc.tensor.transpose(pt[n][:, ct * C + rt * P:ct * C + (rt + 1) * P],
                                                       raw[:, rt, ct * P:(ct + 1) * P], ident[:])
                last.then_inc(prep_pe, 1)
                for ct in range(CT):
                    last = nc.tensor.matmul(pt[2][0:NL, 0:C], wuk_raw[:, ct, :], wq_raw[:, ct, :],
                                            start=(ct == 0), stop=(ct == CT - 1))
                last.then_inc(prep_pe, 1)
                pe.wait_ge(prep_copied, 1)
                for ct in range(CT):
                    last = nc.tensor.matmul(pt[3][0:NL, 0:C], wuv_raw[:, ct, :], wo_t[:, ct, :],
                                            start=(ct == 0), stop=(ct == CT - 1))
                last.then_inc(prep_pe, 1)
                pe.wait_ge(prep_copied, 3)
                for n, eff in ((4, keff_t), (5, veff)):
                    for ct in range(CT):
                        last = nc.tensor.matmul(pt[n][:, ct * C:(ct + 1) * C], wdkv_raw[:, ct * P:(ct + 1) * P],
                                                eff[:], start=True, stop=True)
                last.then_inc(prep_pe, 1)

            @block.scalar
            def _(act):
                act.wait_ge(prep_pe, 1)
                nc.scalar.copy(wo_t[:], pt[1][:].rearrange("p (t n) -> p t n", t=CT)).then_inc(prep_copied, 1)
                act.wait_ge(prep_pe, 2)
                nc.scalar.copy(keff_t[:], pt[2][0:NL, 0:C]).then_inc(prep_copied, 1)
                act.wait_ge(prep_pe, 3)
                nc.scalar.copy(veff[:], pt[3][0:NL, 0:C]).then_inc(prep_copied, 1)
                for n, (bank, hi) in enumerate(((0, wq_hi), (4, wk_hi))):
                    if n == 1:
                        act.wait_ge(prep_pe, 4)
                    for ct in range(CT):
                        nc.scalar.copy(hi[:, ct, :].rearrange("p (m d h) -> p m h d", m=CT, h=HM),
                                       pt[bank][:, ct * C:(ct + 1) * C].rearrange("p (h m d) -> p m h d", m=CT, h=HM)
                                       ).then_inc(prep_copied, 1)
                nc.scalar.copy(wv_hi[:], pt[5][:].rearrange("p (t n) -> p t n", t=CT)).then_inc(prep_copied, 1)

            @block.vector
            def _(dve):
                nc.vector.memset(k_stack[SROWS:P, 0], -1.0).then_inc(prep_chain, 1)
                dve.wait_ge(x_loaded[0], 16)
                for t in range(TT):
                    nc.vector.bn_stats(st1[:, t, :], xa[:, 0, t, :]).then_inc(bn1_done, 1)
                for t in range(TT):
                    dve.wait_ge(bn1_done, t + 1)
                    nc.vector.bn_aggr(mv1[:, t, :], st1[:, t, :]).then_inc(stats1, 1)
                for n, (bank, hi, lo) in enumerate(((0, wq_hi, wq_lo), (4, wk_hi, wk_lo))):
                    for ct in range(CT):
                        dve.wait_ge(prep_copied, 3 + (n + 1) * CT)
                        order = "p (m d h) -> p m h d"
                        nc.vector.tensor_tensor(lo[:, ct, :].rearrange(order, m=CT, h=HM),
                                                pt[bank][:, ct * C:(ct + 1) * C].rearrange("p (h m d) -> p m h d", m=CT, h=HM),
                                                hi[:, ct, :].bitcast(fp32).rearrange(order, m=CT, h=HM),
                                                ALU.subtract).then_inc(prep_chain, 1)
                dve.wait_ge(prep_copied, 3 + 2 * CT + 1)
                nc.vector.tensor_tensor(wv_lo[:], pt[5][:].rearrange("p (t n) -> p t n", t=CT), wv_hi[:].bitcast(fp32),
                                        ALU.subtract).then_inc(prep_chain, 1)
                dve.wait_ge(rstd1, 1)
                for t in range(TT):
                    last = nc.vector.tensor_scalar(xn[:, t, :], xa[:, 0, t, :], mv1[:, t, 0:1], rs1[:, t:t + 1],
                                                   ALU.subtract, ALU.mult)
                last.then_inc(xn_ready, 1)
                dve.wait_ge(prep_chain, 2 * CT + 2)
                dve.wait_ge(consts_ready, 13)

        st_ps = [ctx1.enter_context(nc.psum_tensor(f"st_ps{n}", [P, 1024], fp32)) for n in range(2)]
        s_ps = [ctx1.enter_context(nc.psum_tensor(f"s_ps{n}", [P, 512], fp32)) for n in range(2)]
        pv_ps = ctx1.enter_context(nc.psum_tensor("pv_ps", [P, 512], fp32))
        w_ps = ctx1.enter_context(nc.psum_tensor("w_ps", [P, 512], fp32))
        w_half = w_ps[:, :].rearrange("p (t n) -> p t n", t=2)

        BODY = 3
        FIRST = 2
        LAST = FIRST + (BATCH - 3 - FIRST) // BODY * BODY - 1
        turns = [0]

        def steps_of(eng, step):
            for b in range(-3, FIRST):
                step(b, b)
            with eng.Fori(0, (LAST - FIRST + 1) // BODY) as turn:
                turns[0] = turn
                for n in range(BODY):
                    step(turn * BODY + (FIRST + n), FIRST + n)
            for b in range(LAST + 1, BATCH + 2):
                step(b, b)

        def loads_of(b, k):
            return (b + 3) // 3 + 1 if isinstance(b, int) else turns[0] + ((k + 3) // 3 + 1)

        def present(b):
            return lambda lag: not isinstance(b, int) or 0 <= b + lag < BATCH

        def wait(eng, semaphore, value):
            if not isinstance(value, int) or value > 0:
                eng.wait_ge(semaphore, value)

        passed = sem("passed")

        def wait_apart(eng, semaphore, value):
            wait(eng, semaphore, value)
            if not isinstance(value, int):
                eng.sem_inc(passed, 1)

        FILLS_AT = [(1, (4, 5), ()), (1, (6, 7), ()), (1, (8, 9), ()), (1, (10, 11), ()),
                    (1, (), ()), (1, (), ()), (2, (), (0, 1)), (2, (2, 3), ())]

        DN_PIECES = 3
        PIECES = [(dn_hi[:, e:e + 3], dn_lo[:, e:e + 3], dn_raw[:, e:e + 3], 0.5) for e in range(0, NE, 3)] + [
            (gu_hi[:, e, :, 0:GU], gu_lo[:, e, :, 0:GU], gu_raw[:, e], 1.0) for e in range(NE)]

        PIECES_AT = {(-2, 4): range(0, 3), (-2, 5): range(3, 6), (-1, 4): range(6, 8), (-1, 5): range(8, 12)}

        def pieces_at(b, u):
            return PIECES_AT.get((b, u), ()) if isinstance(b, int) else ()

        with ctx1, ExitStack() as c2:
            block = c2.enter_context(nc.Block())

            def stack_part(eng, k, n, which):
                stack, part, parts, stacked = ((q_stack, q_part, Q_PARTS, q_stacked), (k_stack, k_part, K_PARTS, k_stacked))[n]
                if which == 2:
                    stacked = third_stacked
                for r in range(len(parts)):
                    if parts[r] == which:
                        eng.dma_start(stack[r * HS:(r + 1) * HS, k % 3, :, :], part[:, which]).then_inc(stacked, 16)

            @block.sync
            def _(sp):
                def step(b, k):
                    on = present(b)
                    if on(3) and k > -3:
                        wait_apart(sp, xn_ready, b + 1)
                        sp.dma_start(xa[:, k % 3], x_tok[b + 3]).then_inc(x_loaded[k % 3], 16)
                    if on(-2):
                        wait_apart(sp, x1_ready, b - 1)
                        sp.dma_start(xr[:], x_tok[b - 2]).then_inc(xr_loaded, 16)
                    if on(2):
                        wait_apart(sp, st_done, b * UNITS)
                        for which, part_ready in enumerate((qk_p0, qk_p1)):
                            for n in range(2):
                                wait_apart(sp, part_ready, (b + 2) * 2 + n + 1)
                                stack_part(sp, k + 2, n, which)
                    if on(-2):
                        wait_apart(sp, x1_ready, b)
                        sp.dma_start(x1_tok[b - 2], x1_sb[:]).then_inc(x1_stored, 16)
                    if on(1):
                        wait_apart(sp, m_ready, b + 2)
                        for r in range(MROWS):
                            sp.dma_start(q_stack[SROWS + r:SROWS + r + 1, (k + 1) % 3, :, :],
                                         m_part[:, r, :]).then_inc(m_stacked, 16)
                    if on(-2):
                        wait_apart(sp, xn2_ready, b - 1)
                        sp.dma_start(xn2_tok[b - 2], xn2_sb[:]).then_inc(xn2_stored, 16)

                steps_of(sp, step)
                sp.wait_ge(x1_stored, 16 * (BATCH + 1))
                sp.wait_ge(xn2_stored, 16 * (BATCH + 1))

            @block.tensor
            def _(pe):
                def s_fill(b, k, f):
                    if f == 0:
                        wait(pe, q_stacked, (b + 1) * QD)
                        wait(pe, k_stacked, (b + 1) * QD)
                        wait(pe, third_stacked, (b + 1) * 32)
                    g, part = divmod(f, 3)
                    wait(pe, s_max, b * FILLS + f - 1)
                    qs, ks = q_stack[0:SROWS, k % 3], k_stack[0:SROWS, k % 3]
                    bank = s_ps[f % 2]
                    for j in range(2 if part < 2 else 4):
                        h = 4 * g + (2 * part + j if part < 2 else j)
                        qt, width = (1, T) if part < 2 else (0, P)
                        o = bank[:, j * width:(j + 1) * width]
                        nc.tensor.matmul(o, qs[:, h, qt * P:(qt + 1) * P], ks[:, h, 0:width], start=True, stop=False)
                        last = nc.tensor.matmul(o[:, width - P:width], identb[:], maskq[:], start=False, stop=True)
                    last.then_inc(s_done, 1)

                def st_unit(b, k, u):
                    wait(pe, p_ready, b * UNITS + u - 1)
                    qs, ks = q_stack[0:SROWS + MROWS, k % 3], k_stack[0:SROWS + MROWS, k % 3]
                    bank = st_ps[u % 2]
                    for kt in range(TT):
                        for j in range(2):
                            h = 2 * u + j
                            width = T - kt * P
                            o = bank[:, kt * 2 * T + j * width:kt * 2 * T + (j + 1) * width]
                            nc.tensor.matmul(o, ks[:, h, kt * P:(kt + 1) * P], qs[:, h, kt * P:T], start=True, stop=False)
                            last = nc.tensor.matmul(o[:, 0:P], identb[:], maskk[:], start=False, stop=True)
                    last.then_inc(st_done, 1)

                def pv_group(b, k, g, kt):
                    if kt == 0:
                        wait(pe, p_ready, b * UNITS + 2 * g + 2)
                        wait(pe, yt_ready, b * GROUPS + g)
                    for j in range(4):
                        width = T - kt * P
                        pos = kt * 2 * T + (j % 2) * width
                        last = nc.tensor.matmul(
                            pv_ps[32 * j:32 * (j + 1), kt * P:T], v_sb[:, k % 3, kt, 4 * g + j, :],
                            prob_t[:, (2 * g + j // 2) % 4, pos:pos + width],
                            start=(kt == 0), stop=(kt == TT - 1), tile_position=(0, 32 * j))
                    if kt == TT - 1:
                        last.then_inc(pv_done, 1)

                def project(dst, lhs_of, rhs_of):
                    pairs = [(a, c) for a in ((0, 0), (0, 1), (1, 0)) for c in range(CT)]
                    for n, (a, c) in enumerate(pairs):
                        last = nc.tensor.matmul(dst, lhs_of(a, c), rhs_of(a, c), start=(n == 0), stop=(n == len(pairs) - 1))
                    return last

                xt = (xt_hi, xt_lo)
                w_free = [None]

                def step(b, k):
                    on = present(b)
                    if not isinstance(b, int):
                        w_free[0] = (y_ready, (b - 1) * TT)

                    def take_w(semaphore, value):
                        if w_free[0]:
                            wait(pe, *w_free[0])
                        w_free[0] = (semaphore, value)

                    for u in range(UNITS):
                        if on(0):
                            if u == 0:
                                wait(pe, m_stacked, (b + 1) * MD)
                            st_unit(b, k, u)
                        ahead, early, late = FILLS_AT[u]
                        if on(ahead):
                            for f in early:
                                s_fill(b + ahead, k + ahead, f)
                        if on(1) and u == 4:
                            take_w(m_ready, b + 2)
                            wait(pe, s_max, (b + 2) * FILLS)
                            for t in range(TT):
                                last = nc.tensor.transpose(w_ps[0:HEADS, t * P:(t + 1) * P], rowmax[:, t, :], ident[:])
                            last.then_inc(mt_done, 1)
                        if on(-1) and u < 2:
                            pv_group(b - 1, k - 1, GROUPS - 1, u)
                        if on(0) and u >= 2:
                            pv_group(b, k, u // 2 - 1, u % 2)
                        if on(2) and u == 0:
                            take_w(xt_lo_ready, b + 3)
                            wait(pe, xn_ready, b + 3)
                            for c in range(CT):
                                for t in range(TT):
                                    last = nc.tensor.transpose(w_half[:, c, t * P:(t + 1) * P],
                                                               xn[:, t, c * P:(c + 1) * P], ident[:])
                            last.then_inc(xt_done, 1)
                        if on(2) and u in (1, 2):
                            n = u - 1
                            w = ((wq_hi, wq_lo), (wk_hi, wk_lo))[n]
                            take_w(qk_rest, (b + 2) * 2 + n + 1)
                            for m in range(CT):
                                last = project(w_half[:, m, :],
                                               lambda a, c: w[a[1]][:, c, m * P:(m + 1) * P], lambda a, c: xt[a[0]][:, c, :])
                            last.then_inc(qk_done, 1)
                        if on(2) and u == 3:
                            take_w(v_ready, b + 3)
                            for t in range(TT):
                                last = project(w_half[:, t, :],
                                               lambda a, c: xt[a[0]][:, c, t * P:(t + 1) * P],
                                               lambda a, c: (wv_hi, wv_lo)[a[1]][:, c, :])
                            last.then_inc(v_done, 1)
                        if on(-1) and u in (5, 6):
                            t = u - 5
                            take_w(y_ready, (b - 1) * TT + t + 1)
                            wait(pe, yt_ready, b * GROUPS)
                            for g in range(GROUPS):
                                last = nc.tensor.transpose(w_ps[:, g * P:(g + 1) * P],
                                                           yt_sb[:, (k - 1) % 3, g, t * P:(t + 1) * P], ident[:])
                            last.then_inc(ytr_done, 1)
                        if on(ahead):
                            for f in late:
                                s_fill(b + ahead, k + ahead, f)

                steps_of(pe, step)

            @block.scalar
            def _(act):
                def step(b, k):
                    on = present(b)

                    def copy_group(bb, kk, g):
                        wait(act, pv_done, bb * GROUPS + g + 1)
                        nc.scalar.copy(yt_sb[:, kk % 3, g, :], pv_ps[:, 0:T]).then_inc(yt_ready, 1)

                    def second_part(n):
                        wait(act, qk_rest, (b + 2) * 2 + n + 1)
                        nc.scalar.copy((q_part, k_part)[n][:, 1], (q_rest, k_rest)[n][:]).then_inc(qk_p1, 1)

                    for u in range(UNITS):
                        for n in pieces_at(b, u):
                            if n == len(PIECES) - 1:
                                act.wait_ge(ex_split, DN_PIECES)
                            act.wait_ge(ex_loaded, 16 * 7)
                            hi, _, raw, scale = PIECES[n]
                            nc.scalar.activation(hi, raw, ACT.Copy, scale=scale).then_inc(ex_upper, 1)
                        if on(0):
                            wait(act, st_done, b * UNITS + u + 1)
                            wait(act, pv_done, b * GROUPS + u // 2 - 1)
                            nc.scalar.activation(prob_t[:, u % 4, :], st_ps[u % 2][:, 0:UNIT], ACT.Exp,
                                                 scale=SCALE).then_inc(p_ready, 1)
                        if on(-1) and u == 1:
                            copy_group(b - 1, k - 1, GROUPS - 1)
                        if on(0) and u in (3, 5, 7):
                            copy_group(b, k, u // 2 - 1)
                        if on(2) and u == 0:
                            wait(act, xt_done, b + 3)
                            nc.scalar.copy(xt_hi[:], w_half).then_inc(xt_hi_ready, 1)
                        if on(2) and u in (1, 2):
                            n = u - 1
                            wait(act, qk_done, (b + 2) * 2 + n + 1)
                            wait(act, (q_stacked, k_stacked)[n], (b + 2) * QD)
                            wait(act, third_stacked, (b + 2) * 32)
                            nc.scalar.copy((q_part, k_part)[n][:, 0], w_half).then_inc(qk_p0, 1)
                        if on(2) and u == 2:
                            second_part(0)
                        if on(2) and u == 3:
                            second_part(1)
                            wait(act, v_done, b + 3)
                            wait(act, pv_done, b * GROUPS)
                            for t in range(TT):
                                last = nc.scalar.copy(v_sb[:, (k + 2) % 3, t, :, 0:HS],
                                                      w_half[:, t, :].rearrange("p (h d) -> p h d", h=HEADS))
                            last.then_inc(v_ready, 1)

                steps_of(act, step)

            @block.vector
            def _(dve):
                def step(b, k):
                    on = present(b)

                    def stats(src, st, mv, count, bn_done, done):
                        for t in range(TT):
                            nc.vector.bn_stats(st[:, t, :], src[:, t, :]).then_inc(bn_done, 1)
                        for t in range(TT):
                            wait_apart(dve, bn_done, count * TT + t + 1)
                            nc.vector.bn_aggr(mv[:, t, :], st[:, t, :]).then_inc(done, 1)

                    def normalise(dst, src, mv, rs):
                        for t in range(TT):
                            last = nc.vector.tensor_scalar(dst[:, t, :], src[:, t, :], mv[:, t, 0:1], rs[:, t:t + 1],
                                                           ALU.subtract, ALU.mult)
                        return last

                    def maximum(bb, f):
                        g, part = divmod(f, 3)
                        wait(dve, s_done, bb * FILLS + f + 1)
                        if f == 0:
                            wait(dve, mt_done, bb)
                        n, width = (2, T) if part < 2 else (4, P)
                        h = 4 * g + 2 * part if part < 2 else 4 * g
                        nc.vector.tensor_reduce(rowmax[:, 1 if part < 2 else 0, h:h + n],
                                                s_ps[f % 2][:, :].rearrange("p (h k) -> p h k", h=n),
                                                AX.X, ALU.max).then_inc(s_max, 1)

                    for u in range(UNITS):
                        ahead, early, late = FILLS_AT[u]
                        if on(ahead):
                            for f in early:
                                maximum(b + ahead, f)
                        if on(2) and u == 0:
                            wait(dve, xt_hi_ready, b + 3)
                            nc.vector.tensor_tensor(xt_lo[:], w_half, xt_hi[:].bitcast(fp32), ALU.subtract).then_inc(xt_lo_ready, 1)
                        if on(2) and u in (1, 2):
                            n = u - 1
                            wait(dve, qk_p0, (b + 2) * 2 + n + 1)
                            wait(dve, qk_p2, (b + 1) * 2 + n + 1)
                            nc.vector.tensor_tensor((q_rest, k_rest)[n][:], w_half, (q_part, k_part)[n][:, 0],
                                                    ALU.subtract).then_inc(qk_rest, 1)
                        if on(-2) and u == 1:
                            wait(dve, rstdy, b - 1)
                            normalise(y_sb, y_sb, mvy, rsy).then_inc(lny, 1)
                        if on(-2) and u == 3:
                            wait(dve, x1_ready, b)
                            stats(x1_sb, st2, mv2, b - 2, bn2_done, stats2)
                        if on(-1) and u in (5, 6):
                            t = u - 5
                            wait(dve, ytr_done, (b - 1) * TT + t + 1)
                            heads = w_ps[:, :].rearrange("p (h d) -> p h d", d=32)
                            nc.vector.reciprocal(inv[:, t, :], heads[:, :, HS]).then_inc(inv_ready, 1)
                            wait(dve, inv_ready, (b - 1) * TT + t + 1)
                            if t == 0:
                                wait(dve, x1_ready, b)
                            nc.vector.tensor_tensor(y_sb[:, t, :].rearrange("p (h d) -> p h d", d=HS), heads[:, :, 0:HS],
                                                    inv[:, t, :].unsqueeze(2).to_broadcast([P, HEADS, HS]),
                                                    ALU.mult).then_inc(y_ready, 1)
                        if on(ahead):
                            for f in late:
                                maximum(b + ahead, f)
                        if on(3) and k > -3 and u == 4:
                            wait(dve, x_loaded[k % 3], loads_of(b, k) * 16)
                            stats(xa[:, k % 3], st1, mv1, b + 3, bn1_done, stats1)
                        if on(1) and u == 4:
                            wait(dve, mt_done, b + 2)
                            wait(dve, m_stacked, (b + 1) * MD)
                            nc.vector.tensor_copy(m_part[:, 0, :], w_ps[0:HEADS, 0:T]).then_inc(m_chain, 1)
                            wait(dve, m_chain, b + 2)
                            nc.vector.tensor_tensor(m_part[:, 1, :], w_ps[0:HEADS, 0:T], m_part[:, 0, :],
                                                    ALU.subtract).then_inc(m_ready, 1)
                        for n in pieces_at(b, u):
                            dve.wait_ge(ex_upper, n + 1)
                            hi, lo, raw, scale = PIECES[n]
                            nc.vector.scalar_tensor_tensor(out=lo, in0=raw, scalar=scale, in1=hi.bitcast(fp32),
                                                           op0=ALU.mult, op1=ALU.subtract).then_inc(ex_split, 1)
                        if pieces_at(b, u) and n == len(PIECES) - 1:
                            for j, (which, raw) in enumerate(((slice(SHARED, NE), r_raw[:].unsqueeze(1)),
                                                              (slice(0, EXPERTS), r_raw[:].rearrange("p c e -> p e c").unsqueeze(3)))):
                                cols = slice(GU, GW) if j == 0 else slice(GU, GU + 1)
                                hi, lo = gu_hi[:, which, :, cols], gu_lo[:, which, :, cols]
                                nc.vector.tensor_copy(hi, raw).then_inc(ex_upper, 1)
                                dve.wait_ge(ex_upper, n + 2 + j)
                                nc.vector.tensor_tensor(lo, raw, hi.bitcast(fp32), ALU.subtract).then_inc(ex_split, 1)
                        if on(-2) and u == 5:
                            wait(dve, rstd2, b - 1)
                            wait(dve, xn2_stored, 16 * (b - 1))
                            normalise(xn2_sb, x1_sb, mv2, rs2).then_inc(xn2_ready, 1)
                        if on(3) and k > -3 and u == 7:
                            wait(dve, rstd1, b + 4)
                            wait(dve, xt_done, b + 3)
                            normalise(xn, xa[:, k % 3], mv1, rs1).then_inc(xn_ready, 1)
                        if on(-1) and u == 7:
                            wait(dve, y_ready, b * TT)
                            stats(y_sb, sty, mvy, b - 1, bny_done, statsy)

                steps_of(dve, step)

            @block.gpsimd
            def _(pool):
                def rstd(mv, rs, count, veps, done):
                    nc.gpsimd.tensor_scalar(rs[:], mv[:, :, 1], EPS, None, ALU.add).then_inc(veps, 1)
                    wait_apart(pool, veps, count + 1)
                    nc.gpsimd.tensor_tensor(rs[:], rs[:], neg_half[:], ALU.pow).then_inc(done, 1)

                pool.sem_inc(x1_ready, 1)
                pool.sem_inc(x1_stored, 16)
                pool.sem_inc(xn2_stored, 16)

                def step(b, k):
                    on = present(b)
                    if on(-2):
                        wait_apart(pool, lny, b - 1)
                        wait_apart(pool, xr_loaded, 16 * (b - 1))
                        wait_apart(pool, x1_stored, 16 * (b - 1))
                        wait_apart(pool, xn2_stored, 16 * (b - 1))
                        nc.gpsimd.tensor_tensor(x1_sb[:], y_sb[:], xr[:], ALU.add).then_inc(x1_ready, 1)
                    if on(2):
                        for n, (part, rest, stacked) in enumerate(((q_part, q_rest, q_stacked), (k_part, k_rest, k_stacked))):
                            wait_apart(pool, qk_p1, (b + 2) * 2 + n + 1)
                            nc.gpsimd.tensor_tensor(part[:, 2], rest[:], part[:, 1], ALU.subtract).then_inc(qk_p2, 1)
                            if n == 0:
                                wait_apart(pool, st_done, b * UNITS)
                            wait_apart(pool, qk_p2, (b + 2) * 2 + n + 1)
                            stack_part(pool, k + 2, n, 2)
                    if on(-2):
                        wait_apart(pool, stats2, (b - 1) * TT)
                        rstd(mv2, rs2, b - 2, veps2, rstd2)
                    if on(3) and k > -3:
                        wait_apart(pool, stats1, (b + 4) * TT)
                        rstd(mv1, rs1, b + 3, veps1, rstd1)
                    if on(-1):
                        wait_apart(pool, statsy, b * TT)
                        rstd(mvy, rsy, b - 1, vepsy, rstdy)

                steps_of(pool, step)

        f_shared = sb("f_shared", [P, TILES, C])
        at_f = sb("at_f", [P, TILES, 2])
        block_tokens = sb("block_tokens", [P, BLOCKS], u32)
        block_expert = sb("block_expert", [P, BLOCKS + 2 * RING], i32)
        x1_all = sb("x1_all", [P, TILES, C])
        x1_loaded = sem("x1_loaded")
        block_rows = sb("block_rows", [P, BLOCKS], u32)

        def experts_pass(c, name, n_blocks, shared):
            def sb3(nm, shape, dt=fp32):
                return c.enter_context(nc.sbuf_tensor(f"{name}_{nm}", shape, dt))

            def sem3(nm):
                return c.enter_context(nc.semaphore(f"{name}_{nm}"))

            tok = sb3("tok", [P, RING, C])
            et_hi = sb3("et_hi", [P, 2, CT, P], f32r)
            et_lo = sb3("et_lo", [P, 2, CT, P], f32r)
            th = sb3("th", [P, 2, I])
            ga = sb3("ga", [P, 2, I])
            hid = sb3("hid", [P, 2, I])
            ht_hi = sb3("ht_hi", [P, 2, P], f32r)
            ht_lo = sb3("ht_lo", [P, 2, P], f32r)
            lg = sb3("lg", [P, RING, 8])
            top8 = sb3("top8", [P, RING, 8])
            top_at = sb3("top_at", [P, RING, 8], u32)
            half_p = sb3("half_p", [P, RING, 2])
            o_sb = sb3("o_sb", [P, RING, C])
            et_ps = c.enter_context(nc.psum_tensor(f"{name}_et_ps", [P, 512], fp32))
            ht_ps = c.enter_context(nc.psum_tensor(f"{name}_ht_ps", [P, 512], fp32))
            GB = RING if shared else 3
            gu_ps = [c.enter_context(nc.psum_tensor(f"{name}_gu_ps{n}", [P, 512], fp32)) for n in range(GB)]
            f_ps = [c.enter_context(nc.psum_tensor(f"{name}_f_ps{n}", [P, 512], fp32)) for n in range(2)]
            if not shared:
                s_th, s_ga, s_hid = (sb3(n, [P, I]) for n in ("s_th", "s_ga", "s_hid"))
                s_ht_hi, s_ht_lo = (sb3(n, [P, P], f32r) for n in ("s_ht_hi", "s_ht_lo"))
                s_ht_ps = c.enter_context(nc.psum_tensor(f"{name}_s_ht_ps", [P, 512], fp32))
                s_f_ps = s_ht_ps
            s_th_ready, s_ga_ready, s_h_ready, s_ht_done, s_hi_ready, s_lo_ready, s_dn_done, s_f_ready = (
                sem3(n) for n in ("s_th_ready", "s_ga_ready", "s_h_ready", "s_ht_done", "s_hi_ready", "s_lo_ready",
                                  "s_dn_done", "s_f_ready"))
            gu_kept = sem3("gu_kept")
            loaded = [sem3(f"loaded{n}") for n in range(RING)]
            et_done, et_hi_ready, et_lo_ready = sem3("et_done"), sem3("et_hi_ready"), sem3("et_lo_ready")
            gu_done, lg_ready, max_ready, at_ready, top_ready = (
                sem3(n) for n in ("gu_done", "lg_ready", "max_ready", "at_ready", "top_ready"))
            lg1_ready, p_half_ready, p_ready2 = sem3("lg1_ready"), sem3("p_half_ready"), sem3("p_ready2")
            th_ready, ga_ready, h_ready = sem3("th_ready"), sem3("ga_ready"), sem3("h_ready")
            ht_done, ht_hi_ready, ht_lo_ready = sem3("ht_done"), sem3("ht_hi_ready"), sem3("ht_lo_ready")
            dn_done = sem3("dn_done")
            f_ready = sem3("f_ready")
            o_stored = [sem3(f"o_stored{n}") for n in range(RING)]
            o_free = sem3("o_free")

            first = 3
            last = first + (n_blocks if shared else 2 * TILES) // TURN * TURN - TURN - 1

            def shared_tile(m, k, turn, at):
                if shared or (m if turn is None else k) < 0:
                    return None
                if (at == 2) != (k % 2 == 1):
                    return None
                n = k // 2 - (1 if at == 3 else 0)
                if turn is None:
                    return (n, f_shared[:, n, :]) if 0 <= n < TILES else None
                n = turn * (TURN // 2) + n
                return n, f_shared[:, bass.ds(n, 1), :].rearrange("p a c -> p (a c)")

            def steps3(eng, step):
                for m in range(-2, first):
                    step(m, m, None)
                with eng.Fori(0, (last - first + 1) // TURN) as turn:
                    for n in range(TURN):
                        step(turn * TURN + (first + n), first + n, turn)
                for m in range(last + 1, n_blocks + 3):
                    step(m, m, None)

            def present3(m):
                return lambda lag: not isinstance(m, int) or 0 <= m + lag < n_blocks

            block = c.enter_context(nc.Block())

            @block.sync
            def _(sp):
                def step(m, k, turn):
                    on = present3(m)
                    if shared and on(2):
                        wait_apart(sp, et_done, m - 1)
                        sp.dma_start(tok[:, (k + 2) % RING], xn2_tile[m + 2]).then_inc(loaded[(k + 2) % RING], 16)

                if shared:
                    steps3(sp, step)
                    for t in range(0, TILES, TILES // 4):
                        sp.dma_start(x1_all[:, t:t + TILES // 4], x1_tile[t:t + TILES // 4].rearrange("t p c -> p t c")
                                     ).then_inc(x1_loaded, 16)

            @block.gpsimd
            def _(pool):
                if not shared:
                    LAG = 8
                    pool.sem_inc(o_free, RING)
                    for n in range(n_blocks + LAG + 2):
                        if n < n_blocks:
                            if n >= RING:
                                pool.wait_ge(et_done, n - RING + 1)
                            nc.gpsimd.indirect_dma_start(
                                out=tok[:, n % RING], out_offset=None, in_=xn2_rows,
                                in_offset=bass.IndirectOffsetOnAxis(ap=block_tokens[:, n:n + 1], axis=0),
                            ).then_inc(loaded[n % RING], 16)
                        o = n - LAG
                        if 0 <= o < n_blocks:
                            pool.wait_ge(f_ready, o + 3)
                            nc.gpsimd.indirect_dma_start(
                                out=o_rows, out_offset=bass.IndirectOffsetOnAxis(ap=block_rows[:, o:o + 1], axis=0),
                                in_=o_sb[:, o % RING], in_offset=None,
                            ).then_inc(o_stored[o % RING], 16)
                        if o >= 2:
                            pool.wait_ge(o_stored[(o - 2) % RING], 16 * ((o - 2) // RING + 1))
                            pool.sem_inc(o_free, 1)

            @block.tensor
            def _(pe):
                pe.sem_inc(f_ready, 2)
                pe.sem_inc(s_f_ready, 1)
                experts = None if shared else [[pe.alloc_register(f"expert{a}{n}") for n in range(RING)] for a in range(2)]

                def expert_of(a, b, n):
                    if n < 0:
                        return pe.value_load(block_expert[0:1, b:b + 1], min_val=0, max_val=EXPERTS - 1)
                    return pe.snap(experts[a][n % RING], min_val=0, max_val=EXPERTS - 1)

                def step(m, k, turn):
                    on = present3(m)
                    if not shared and k >= first and (k - first) % RING == 0:
                        four = (lambda at: slice(at, at + RING)) if turn is None else (lambda at: bass.ds(at, RING))
                        pe.load(experts[0], block_expert[0:1, four(m + 1)])
                        pe.load(experts[1], block_expert[0:1, four(m - 3)])
                    if on(2):
                        wait(pe, loaded[(k + 2) % RING], 16 * ((k + 2) // RING + 1 + (turn * (TURN // RING) if turn is not None else 0)))
                        wait(pe, et_lo_ready, m + 2)
                        for ct in range(CT):
                            last = nc.tensor.transpose(et_ps[:, ct * P:(ct + 1) * P],
                                                       tok[:, (k + 2) % RING, ct * P:(ct + 1) * P], ident[:])
                        last.then_inc(et_done, 1)
                    if on(-3) and not shared:
                        e = expert_of(1, m - 3, k - first)
                        w_hi, w_lo = (w[:, bass.ds(e, 1), :].rearrange("p a c -> p (a c)") for w in (dn_hi, dn_lo))
                        wait(pe, ht_lo_ready, m - 2)
                        wait(pe, f_ready, m - 2)
                        for j, (part, w) in enumerate(((ht_hi, w_hi), (ht_hi, w_lo), (ht_lo, w_hi))):
                            last = nc.tensor.matmul(f_ps[(k - 3) % 2][:, 0:C], part[:, (k - 3) % 2, :], w, start=(j == 0), stop=(j == 2))
                        last.then_inc(dn_done, 1)
                    if on(-2) and not shared:
                        wait(pe, h_ready, m - 1)
                        nc.tensor.transpose(ht_ps[:, 0:P], hid[:, (k - 2) % 2, :], ident[:]).then_inc(ht_done, 1)
                    if on(1):
                        if not shared:
                            e = expert_of(0, m + 1, k - first)
                        wait(pe, et_lo_ready, m + 2)
                        if shared:
                            wait(pe, gu_kept, m - 1)
                        j = 0
                        for part, w in ((et_hi, gu_hi), (et_hi, gu_lo), (et_lo, gu_hi)):
                            for ct in range(CT):
                                rhs = w[:, SHARED, ct, :] if shared else \
                                    w[:, bass.ds(e, 1), ct, :].rearrange("p a n -> p (a n)")
                                last = nc.tensor.matmul(gu_ps[(k + 1) % GB][:, 0:GW], part[:, (k + 1) % 2, ct, :], rhs,
                                                        start=(j == 0), stop=(j == 3 * CT - 1))
                                j += 1
                        last.then_inc(gu_done, 1)
                    tile = shared_tile(m, k, turn, 3)
                    if tile:
                        wait(pe, s_lo_ready, tile[0] + 1)
                        for j, (part, w) in enumerate(((s_ht_hi, dn_hi), (s_ht_hi, dn_lo), (s_ht_lo, dn_hi))):
                            last = nc.tensor.matmul(s_f_ps[:, 0:C], part[:], w[:, SHARED, :], start=(j == 0), stop=(j == 2))
                        last.then_inc(s_dn_done, 1)
                    tile = shared_tile(m, k, turn, 2)
                    if tile:
                        wait(pe, s_h_ready, tile[0] + 1)
                        wait(pe, s_f_ready, tile[0] + 1)
                        nc.tensor.transpose(s_ht_ps[:, 0:P], s_hid[:], ident[:]).then_inc(s_ht_done, 1)

                steps3(pe, step)

            @block.scalar
            def _(act):
                def step(m, k, turn):
                    on = present3(m)
                    if on(2):
                        wait(act, et_done, m + 3)
                        wait(act, gu_done, m + 1)
                        nc.scalar.copy(et_hi[:, k % 2], et_ps[:, 0:C].rearrange("p (c n) -> p c n", c=CT)).then_inc(et_hi_ready, 1)
                    if on(-3) and not shared:
                        wait(act, dn_done, m - 2)
                        wait(act, o_free, m - 2)
                        nc.scalar.copy(o_sb[:, (k - 3) % RING], f_ps[(k - 3) % 2][:, 0:C]).then_inc(f_ready, 1)
                    if on(-2) and not shared:
                        wait(act, ht_done, m - 1)
                        nc.scalar.copy(ht_hi[:, (k - 2) % 2], ht_ps[:, 0:P]).then_inc(ht_hi_ready, 1)
                    if on(0) and not shared:
                        wait(act, p_ready2, m + 1)
                        wait(act, ga_ready, m - 1)
                        nc.scalar.activation(th[:, k % 2], gu_ps[k % GB][:, 0:I], ACT.Tanh,
                                             scale=half_p[:, k % RING, 0:1]).then_inc(th_ready, 1)
                    if on(1):
                        wait(act, gu_done, m + 2)
                        if shared:
                            nc.scalar.copy(lg[:, (k + 1) % RING], gu_ps[(k + 1) % GB][:, GU:GU + 8]).then_inc(lg_ready, 1)
                            dst = f_shared[:, bass.ds(m + 1, 1), :].rearrange("p a c -> p (a c)") if turn is not None \
                                else f_shared[:, m + 1, :]
                            nc.scalar.copy(dst, gu_ps[(k + 1) % GB][:, 0:GU]).then_inc(gu_kept, 1)
                        else:
                            nc.scalar.activation(lg[:, (k + 1) % RING, 0:1], gu_ps[(k + 1) % GB][:, GU:GU + 1],
                                                 ACT.Exp, scale=-1.0).then_inc(lg_ready, 1)
                    tile = shared_tile(m, k, turn, 3)
                    if tile:
                        wait_apart(act, s_dn_done, tile[0] + 1)
                        nc.scalar.copy(tile[1], s_f_ps[:, 0:C]).then_inc(s_f_ready, 1)
                    tile = shared_tile(m, k, turn, 1)
                    if tile:
                        wait(act, s_ga_ready, tile[0])
                        nc.scalar.activation(s_th[:], tile[1][:, 0:I], ACT.Tanh, scale=0.5).then_inc(s_th_ready, 1)
                    tile = shared_tile(m, k, turn, 2)
                    if tile:
                        wait(act, s_dn_done, tile[0])
                        wait(act, s_ht_done, tile[0] + 1)
                        nc.scalar.copy(s_ht_hi[:], s_ht_ps[:, 0:P]).then_inc(s_hi_ready, 1)

                steps3(act, step)

            @block.vector
            def _(dve):
                def step(m, k, turn):
                    on = present3(m)
                    if shared and on(0):
                        wait_apart(dve, lg_ready, m + 1)
                        nc.vector.max(top8[:, k % RING], lg[:, k % RING]).then_inc(max_ready, 1)
                    if shared and on(-2):
                        wait(dve, at_ready, m - 1)
                        dst = at_f[:, bass.ds(m - 2, 1), :].rearrange("p a c -> p (a c)") if turn is not None else at_f[:, m - 2, :]
                        nc.vector.tensor_copy(dst, top_at[:, (k - 2) % RING, 0:2]).then_inc(top_ready, 1)
                    if shared and on(-1):
                        r = (k - 1) % RING
                        wait_apart(dve, max_ready, m)
                        nc.vector.max_index(top_at[:, r], top8[:, r], lg[:, r]).then_inc(at_ready, 1)
                    if on(2):
                        wait(dve, et_hi_ready, m + 3)
                        nc.vector.tensor_tensor(et_lo[:, k % 2], et_ps[:, 0:C].rearrange("p (c n) -> p c n", c=CT),
                                                et_hi[:, k % 2].bitcast(fp32), ALU.subtract).then_inc(et_lo_ready, 1)
                    if on(-2) and not shared:
                        wait(dve, ht_hi_ready, m - 1)
                        nc.vector.tensor_tensor(ht_lo[:, (k - 2) % 2], ht_ps[:, 0:P], ht_hi[:, (k - 2) % 2].bitcast(fp32),
                                                ALU.subtract).then_inc(ht_lo_ready, 1)
                    if on(-1) and not shared:
                        h, bank = (k - 1) % 2, gu_ps[(k - 1) % GB]
                        wait(dve, th_ready, m)
                        nc.vector.scalar_tensor_tensor(out=ga[:, h], in0=th[:, h], scalar=1.0, in1=bank[:, 0:I],
                                                       op0=ALU.add, op1=ALU.mult).then_inc(ga_ready, 1)
                        wait(dve, ht_done, m - 2)
                        wait(dve, ga_ready, m)
                        nc.vector.scalar_tensor_tensor(out=hid[:, h], in0=ga[:, h], scalar=half_p[:, (k - 1) % RING, 1:2],
                                                       in1=bank[:, I:GU], op0=ALU.mult, op1=ALU.mult).then_inc(h_ready, 1)
                    r = (k + 1) % RING
                    weigh = on(1) and not shared
                    hidden, lower = shared_tile(m, k, turn, 1), shared_tile(m, k, turn, 2)
                    if weigh:
                        wait(dve, lg_ready, m + 2)
                        nc.vector.tensor_scalar(lg[:, r, 1:2], lg[:, r, 0:1], 2.0, 2.0, ALU.mult, ALU.add).then_inc(lg1_ready, 1)
                    if hidden:
                        wait(dve, s_h_ready, hidden[0])
                        wait(dve, s_th_ready, hidden[0] + 1)
                        nc.vector.scalar_tensor_tensor(out=s_ga[:], in0=s_th[:], scalar=1.0, in1=hidden[1][:, 0:I],
                                                       op0=ALU.add, op1=ALU.mult).then_inc(s_ga_ready, 1)
                    if lower:
                        wait(dve, s_hi_ready, lower[0] + 1)
                        nc.vector.tensor_tensor(s_ht_lo[:], s_ht_ps[:, 0:P], s_ht_hi[:].bitcast(fp32),
                                                ALU.subtract).then_inc(s_lo_ready, 1)
                    if weigh:
                        wait(dve, lg1_ready, m + 2)
                        nc.vector.reciprocal(half_p[:, r, 0:1], lg[:, r, 1:2]).then_inc(p_half_ready, 1)
                    if hidden:
                        wait(dve, s_ht_done, hidden[0])
                        wait(dve, s_ga_ready, hidden[0] + 1)
                        nc.vector.tensor_tensor(s_hid[:], s_ga[:], hidden[1][:, I:GU], ALU.mult).then_inc(s_h_ready, 1)
                    if weigh:
                        wait(dve, p_half_ready, m + 2)
                        nc.vector.tensor_scalar(half_p[:, r, 1:2], half_p[:, r, 0:1], half_p[:, r, 0:1], 4.0,
                                                ALU.mult, ALU.mult).then_inc(p_ready2, 1)

                steps3(dve, step)

        with ExitStack() as c3:
            experts_pass(c3, "sh", TILES, True)

        with ExitStack() as c5:
            def sb5(nm, shape, dt=fp32):
                return c5.enter_context(nc.sbuf_tensor(nm, shape, dt))

            cols8 = sb5("cols8", [P, EXPERTS])
            colsb = sb5("colsb", [P, BLOCKS], f16)
            colsf = sb5("colsf", [P, BLOCKS])
            colsp = sb5("colsp", [P, P], f16)
            tokid = sb5("tokid", [P, TILES])
            spare = sb5("spare", [P, BLOCKS])
            second = sb5("second", [P, BLOCKS])
            tok_f = sb5("tok_f", [P, BLOCKS])
            rows_f = sb5("rows_f", [P, BLOCKS])
            upper = sb5("upper", [P, BLOCKS])
            before = sb5("before", [P, P], bf16)
            ones = sb5("ones", [P, P], bf16)
            keep = sb5("keep", [P, EXPERTS, TILES])
            hot = sb5("hot", [P, 2, TILES, EXPERTS])
            hots = sb5("hots", [P, TILES, EXPERTS], bf16)
            total = sb5("total", [P, EXPERTS, TILES])
            upto = sb5("upto", [P, EXPERTS, TILES])
            cnt = sb5("cnt", [P, EXPERTS])
            cnt_i = sb5("cnt_i", [P, EXPERTS], i32)
            nblk = sb5("nblk", [P, EXPERTS])
            ends = sb5("ends", [P, EXPERTS])
            starts = sb5("starts", [P, EXPERTS])
            place = sb5("place", [P, TILES, EXPERTS])
            dest = sb5("dest", [P, 2, TILES])
            dest_i = sb5("dest_i", [P, 2, TILES], i32)
            part_i = sb5("part_i", [P, 2, 2, TILES], i32)
            part_f = sb5("part_f", [P, 2, 2, TILES])
            over = sb5("over", [P, BLOCKS, EXPERTS])
            bexp = sb5("bexp", [P, BLOCKS])
            RB = 8
            in_block = sb5("in_block", [P, RB, P], f16)
            of_block = sb5("of_block", [P, RB, BLOCKS], f16)
            id_block = sb5("id_block", [P, RB, BLOCKS], f16)
            rank_ps = c5.enter_context(nc.psum_tensor("rank_ps", [P, 512], fp32))
            total_ps = c5.enter_context(nc.psum_tensor("total_ps", [P, 512], fp32))
            ids_ps = [c5.enter_context(nc.psum_tensor(f"ids_ps{k}", [P, 512], fp32)) for k in range(2)]
            iotas, hots_ready, ranks_done, hot_made, hot_numbered, ids_done, r_chain = (
                c5.enter_context(nc.semaphore(n))
                for n in ("iotas", "hots_ready", "ranks_done", "hot_made", "hot_numbered", "ids_done", "r_chain"))
            block = c5.enter_context(nc.Block())

            @block.gpsimd
            def _(pool):
                imprecise = dict(allow_small_or_imprecise_dtypes=True)
                nc.gpsimd.iota(cols8[:], pattern=[[1, EXPERTS]], base=0, channel_multiplier=0, **imprecise).then_inc(iotas, 1)
                nc.gpsimd.iota(colsf[:], pattern=[[1, BLOCKS]], base=0, channel_multiplier=0, **imprecise).then_inc(iotas, 1)
                nc.gpsimd.iota(colsb[:], pattern=[[1, BLOCKS]], base=0, channel_multiplier=0, **imprecise).then_inc(iotas, 1)
                nc.gpsimd.iota(colsp[:], pattern=[[1, P]], base=0, channel_multiplier=0, **imprecise).then_inc(iotas, 1)
                half = TILES // 2
                nc.gpsimd.iota(tokid[:, 0:half], pattern=[[P, half]], base=-TOKENS // 2, channel_multiplier=1, **imprecise).then_inc(iotas, 1)
                nc.gpsimd.iota(tokid[:, half:TILES], pattern=[[P, half]], base=1, channel_multiplier=1, **imprecise).then_inc(iotas, 1)
                nc.gpsimd.iota(spare[:], pattern=[[P, BLOCKS]], base=2 * TOKENS, channel_multiplier=1, **imprecise).then_inc(iotas, 1)
                nc.gpsimd.memset(ones[:], 1.0).then_inc(iotas, 1)
                nc.gpsimd.memset(before[:], 1.0).then_inc(iotas, 1)
                nc.gpsimd.memset(keep[:], 1.0).then_inc(iotas, 1)
                pool.wait_ge(iotas, 10)
                nc.gpsimd.memset(keep[:, :, 0:1], 0.0).then_inc(iotas, 1)
                nc.gpsimd.affine_select(out=before[:], in_=before[:], compare_op=ALU.is_gt, fill=0.0, base=0,
                                        pattern=[[1, P]], channel_multiplier=-1).then_inc(iotas, 1)

            @block.tensor
            def _(pe):
                pe.wait_ge(iotas, 12)
                pe.wait_ge(hots_ready, 1)
                flat = hots[:, :, :].rearrange("p t e -> p (t e)")
                nc.tensor.matmul(rank_ps[:, 0:TILES * EXPERTS], before[:], flat, start=True, stop=True).then_inc(ranks_done, 1)
                nc.tensor.matmul(total_ps[:, 0:TILES * EXPERTS], ones[:], flat, start=True, stop=True).then_inc(ranks_done, 1)
                for n in range(2 * TILES):
                    pe.wait_ge(hot_numbered, n + 1)
                    nc.tensor.matmul(ids_ps[n % 2][:, 0:BLOCKS], in_block[:, n % RB, :], id_block[:, n % RB, :],
                                     start=(n < 2), stop=(n >= 2 * TILES - 2)).then_inc(ids_done, 1)

            @block.scalar
            def _(act):
                act.wait_ge(iotas, 12)
                for n in range(2 * TILES):
                    act.wait_ge(hot_made, n + 1)
                    nc.scalar.activation(id_block[:, n % RB, :], of_block[:, n % RB, :], ACT.Copy,
                                         scale=tokid[:, n // 2:n // 2 + 1]).then_inc(hot_numbered, 1)

            @block.vector
            def _(dve):
                steps = [0]

                def step(ins):
                    steps[0] += 1
                    ins.then_inc(r_chain, 1)
                    dve.wait_ge(r_chain, steps[0])

                te = [P, TILES, EXPERTS]
                dve.wait_ge(iotas, 12)
                for k in range(2):
                    step(nc.vector.tensor_tensor(hot[:, k], cols8[:].unsqueeze(1).to_broadcast(te),
                                                 at_f[:, :, k:k + 1].to_broadcast(te), ALU.is_equal))
                nc.vector.tensor_tensor(hots[:], hot[:, 0], hot[:, 1], ALU.add).then_inc(hots_ready, 1)
                dve.wait_ge(ranks_done, 2)
                step(nc.vector.tensor_copy(total[:], total_ps[:, 0:TILES * EXPERTS].rearrange("p (t e) -> p e t", e=EXPERTS)))
                step(nc.vector.tensor_tensor_scan(
                    out=upto[:].rearrange("p e t -> p (e t)"), data0=keep[:].rearrange("p e t -> p (e t)"),
                    data1=total[:].rearrange("p e t -> p (e t)"), initial=0.0, op0=ALU.mult, op1=ALU.add))
                step(nc.vector.tensor_scalar(cnt[:], upto[:, :, TILES - 1], float(P - 1), None, ALU.add))
                step(nc.vector.tensor_copy(cnt_i[:], cnt[:]))
                step(nc.vector.tensor_scalar(cnt_i[:], cnt_i[:], LOG_P, None, ALU.logical_shift_right))
                step(nc.vector.tensor_copy(nblk[:], cnt_i[:]))
                step(nc.vector.tensor_tensor_scan(out=ends[:], data0=keep[:, 0, 1:1 + EXPERTS], data1=nblk[:],
                                                  initial=0.0, op0=ALU.mult, op1=ALU.add))
                step(nc.vector.tensor_tensor(starts[:], ends[:], nblk[:], ALU.subtract))
                step(nc.vector.tensor_tensor(upto[:], upto[:], total[:], ALU.subtract))
                step(nc.vector.scalar_tensor_tensor(out=upto[:], in0=starts[:].unsqueeze(2).to_broadcast([P, EXPERTS, TILES]),
                                                    scalar=float(P), in1=upto[:], op0=ALU.mult, op1=ALU.add))
                step(nc.vector.tensor_tensor(place[:], rank_ps[:, 0:TILES * EXPERTS].rearrange("p (t e) -> p t e", e=EXPERTS),
                                             upto[:].rearrange("p e t -> p t e"), ALU.add))
                for k in range(2):
                    step(nc.vector.tensor_tensor(hot[:, k], hot[:, k], place[:], ALU.mult))
                step(nc.vector.tensor_reduce(dest[:], hot[:], AX.X, ALU.add))
                step(nc.vector.tensor_copy(dest_i[:], dest[:]))
                step(nc.vector.tensor_scalar(part_i[:, 0], dest_i[:], P - 1, None, ALU.bitwise_and))
                step(nc.vector.tensor_scalar(part_i[:, 1], dest_i[:], LOG_P, None, ALU.logical_shift_right))
                step(nc.vector.tensor_copy(part_f[:], part_i[:]))
                for n in range(2 * TILES):
                    t, k = n // 2, n % 2
                    if n >= RB:
                        dve.wait_ge(ids_done, n - RB + 1)
                    nc.vector.tensor_scalar(in_block[:, n % RB, :], colsp[:], part_f[:, 0, k, t:t + 1], None, ALU.is_equal)
                    nc.vector.tensor_scalar(of_block[:, n % RB, :], colsb[:], part_f[:, 1, k, t:t + 1], None,
                                            ALU.is_equal).then_inc(hot_made, 1)
                step(nc.vector.tensor_tensor(over[:], colsf[:].unsqueeze(2).to_broadcast([P, BLOCKS, EXPERTS]),
                                             ends[:].unsqueeze(1).to_broadcast([P, BLOCKS, EXPERTS]), ALU.is_ge))
                step(nc.vector.tensor_reduce(bexp[:], over[:], AX.X, ALU.add))
                step(nc.vector.tensor_scalar(bexp[:], bexp[:], float(EXPERTS - 1), None, ALU.min))
                step(nc.vector.memset(block_expert[:], 0))
                step(nc.vector.tensor_copy(block_expert[:, 0:BLOCKS], bexp[:]))
                dve.wait_ge(ids_done, 2 * TILES)
                step(nc.vector.tensor_copy(second[:], ids_ps[1][:, 0:BLOCKS]))
                step(nc.vector.tensor_tensor(bexp[:], ids_ps[0][:, 0:BLOCKS], second[:], ALU.add))
                step(nc.vector.tensor_scalar(upper[:], bexp[:], 0.0, None, ALU.is_gt))
                step(nc.vector.tensor_tensor(tok_f[:], bexp[:], upper[:], ALU.subtract))
                step(nc.vector.tensor_scalar(tok_f[:], tok_f[:], float(TOKENS // 2), None, ALU.add))
                step(nc.vector.tensor_copy(block_tokens[:], tok_f[:]))
                step(nc.vector.tensor_scalar(second[:], second[:], 0.0, float(TOKENS), ALU.not_equal, ALU.mult))
                step(nc.vector.tensor_tensor(rows_f[:], tok_f[:], second[:], ALU.add))
                step(nc.vector.tensor_tensor(spare[:], spare[:], rows_f[:], ALU.subtract))
                step(nc.vector.tensor_scalar(upper[:], bexp[:], 0.0, None, ALU.is_equal))
                step(nc.vector.tensor_tensor(spare[:], spare[:], upper[:], ALU.mult))
                step(nc.vector.tensor_tensor(rows_f[:], rows_f[:], spare[:], ALU.add))
                step(nc.vector.tensor_copy(block_rows[:], rows_f[:]))

        with ExitStack() as c3:
            experts_pass(c3, "ex", BLOCKS, False)

        with ExitStack() as c4:
            def sb4(nm, shape, dt=fp32):
                return c4.enter_context(nc.sbuf_tensor(nm, shape, dt))

            def sem4(nm):
                return c4.enter_context(nc.semaphore(nm))

            Q = 4
            g_sb = sb4("g_sb", [P, 3, 2, Q, C])
            f_sb = sb4("f_sb", [P, 3, Q, C])
            stf = sb4("stf", [P, Q, 6])
            mvf = sb4("mvf", [P, 2, Q, 2])
            rsf = sb4("rsf", [P, 2, Q])
            halves = sb4("halves", [P, Q])
            fin = sb4("fin", [P, 2, Q, C])
            neg_mean = sb4("neg_mean", [P, 2, Q])
            o_loaded = [sem4(f"o_loaded{n}") for n in range(3)]
            out_stored = [sem4(f"out_stored{n}") for n in range(2)]
            two_summed, all_added, bnf_done, statsf, vepsf, rstdf, meanf, lnf, fin_ready = (
                sem4(n) for n in ("two_summed", "all_added", "bnf_done", "statsf", "vepsf", "rstdf", "meanf", "lnf", "fin_ready"))
            sum_ps = [c4.enter_context(nc.psum_tensor(f"sum_ps{n}", [P, Q * C], fp32)) for n in range(2)]
            groups = TILES // Q
            block = c4.enter_context(nc.Block())

            @block.sync
            def _(sp):
                for g in range(groups):
                    tiles = slice(g * Q, (g + 1) * Q)
                    if g >= 3:
                        sp.wait_ge(two_summed, g - 2)
                    for k in range(2):
                        sp.dma_start(g_sb[:, g % 3, k], o_choice[k][tiles].rearrange("t p c -> p t c")).then_inc(o_loaded[g % 3], 16)

            @block.gpsimd
            def _(pool):
                nc.gpsimd.memset(halves[:], -0.5).then_inc(vepsf, 1)
                pool.wait_ge(vepsf, 1)
                for g in range(groups + 1):
                    if g < groups:
                        pool.wait_ge(statsf, Q * (g + 1))
                        nc.gpsimd.tensor_scalar(rsf[:, g % 2], mvf[:, g % 2, :, 1], EPS, None, ALU.add).then_inc(vepsf, 1)
                        pool.wait_ge(vepsf, g + 2)
                        nc.gpsimd.tensor_tensor(rsf[:, g % 2], rsf[:, g % 2], halves[:], ALU.pow).then_inc(rstdf, 1)
                    if g >= 1:
                        h = g - 1
                        pool.wait_ge(lnf, h + 1)
                        if h == 0:
                            pool.wait_ge(x1_loaded, 16 * 4)
                        if h >= 2:
                            pool.wait_ge(out_stored[h % 2], 16 * (h // 2))
                        nc.gpsimd.tensor_tensor(fin[:, h % 2], f_sb[:, h % 3], x1_all[:, h * Q:(h + 1) * Q],
                                                ALU.add).then_inc(fin_ready, 1)

            @block.tensor
            def _(pe):
                for g in range(groups):
                    pe.wait_ge(o_loaded[g % 3], 32 * (g // 3 + 1))
                    if g >= 2:
                        pe.wait_ge(all_added, g - 1)
                    for q in range(Q):
                        for k in range(2):
                            last = nc.tensor.matmul(sum_ps[g % 2][:, q * C:(q + 1) * C], ident[:], g_sb[:, g % 3, k, q],
                                                    start=(k == 0), stop=(k == 1))
                    last.then_inc(two_summed, 1)

            @block.scalar
            def _(act):
                def store(g):
                    act.wait_ge(fin_ready, g + 1)
                    act.dma_start(out_tile[g * Q:(g + 1) * Q].rearrange("t p c -> p t c"),
                                  fin[:, g % 2]).then_inc(out_stored[g % 2], 16)

                for g in range(groups):
                    act.wait_ge(meanf, g + 1)
                    for q in range(Q):
                        last = nc.scalar.activation(f_sb[:, g % 3, q], f_sb[:, g % 3, q], ACT.Identity,
                                                    bias=neg_mean[:, g % 2, q:q + 1], scale=rsf[:, g % 2, q:q + 1])
                    last.then_inc(lnf, 1)
                    if g >= 1:
                        store(g - 1)
                store(groups - 1)
                for n in range(2):
                    act.wait_ge(out_stored[n], 16 * (groups // 2))

            @block.vector
            def _(dve):
                def means(g):
                    dve.wait_ge(rstdf, g + 1)
                    nc.vector.scalar_tensor_tensor(out=neg_mean[:, g % 2], in0=mvf[:, g % 2, :, 0], scalar=-1.0,
                                                   in1=rsf[:, g % 2], op0=ALU.mult, op1=ALU.mult).then_inc(meanf, 1)

                for g in range(groups + 1):
                    if g < groups:
                        if g >= 3:
                            dve.wait_ge(fin_ready, g - 2)
                        dve.wait_ge(two_summed, g + 1)
                        nc.vector.tensor_tensor(f_sb[:, g % 3], sum_ps[g % 2][:, :].rearrange("p (q c) -> p q c", q=Q),
                                                f_shared[:, g * Q:(g + 1) * Q], ALU.add).then_inc(all_added, 1)
                        if g >= 1:
                            means(g - 1)
                        dve.wait_ge(all_added, g + 1)
                        for q in range(Q):
                            nc.vector.bn_stats(stf[:, q], f_sb[:, g % 3, q]).then_inc(bnf_done, 1)
                        for q in range(Q):
                            dve.wait_ge(bnf_done, g * Q + q + 1)
                            nc.vector.bn_aggr(mvf[:, g % 2, q], stf[:, q]).then_inc(statsf, 1)
                    else:
                        means(g - 1)


_INS = ["L0_attn_x", "L0_attn_Wq_w", "L0_attn_Wdkv_w", "L0_attn_Wuk_w", "L0_attn_Wuv_w", "L0_attn_Wo_w",
        "L0_ffn_router_w", "L0_ffn_gate_up_w", "L0_ffn_down_w", "L0_ffn_shared_gate_w", "L0_ffn_shared_up_w",
        "L0_ffn_shared_down_w"]


def kernel(**inputs):
    import numpy as _np
    import concourse.bacc as _bacc
    from concourse import mybir as _mybir
    from concourse.bass_utils import run_bass_kernel_spmd as _run

    nc = _bacc.Bacc("TRN2", target_bir_lowering=False, num_devices=1)
    arrays, args = {}, []
    for name in _INS:
        a = _np.ascontiguousarray(inputs[name])
        arrays[f"in_{name}_dram"] = a
        args.append(nc.dram_tensor(f"in_{name}_dram", a.shape, _mybir.dt.from_np(a.dtype), kind="ExternalInput").ap())
    shape = inputs["L0_attn_x"].shape
    args.append(nc.dram_tensor("out_dram", shape, _mybir.dt.float32, kind="ExternalOutput").ap())
    sandwich_block_kernel(nc, *args)
    r = _run(nc, [arrays], core_ids=[0])
    return r.results[0]["out_dram"]
```
